# Optimizing a Trainium2 kernel written in Bass

```python
import numpy as np
import jax
import jax.numpy as jnp

def _softmax(x, axis=-1):
    return jax.nn.softmax(x, axis=axis)

def _gelu(x):
    return jax.nn.gelu(x, approximate=True)

def _silu(x):
    return jax.nn.silu(x)

def _sigmoid(x):
    return jax.nn.sigmoid(x)

def _layernorm(x, axis=-1, eps=1e-05):
    m = jnp.mean(x, axis=axis, keepdims=True)
    v = jnp.var(x, axis=axis, keepdims=True)
    return (x - m) / jnp.sqrt(v + eps)

def _scatter_add(tgt, idx, src, axis=0):
    return tgt.at[idx].add(src)

def _segment_sum(src, seg, n):
    return jax.ops.segment_sum(src, seg, n)
kernel_name = 'mk_adaln_d1_jaxref_r8_401119'

def setup_inputs(seed: int=0):
    np.random.seed(seed)
    _w = jnp.asarray

    def _L0_attn_setup():
        import jax, jax.numpy as jnp
        import numpy as np
        B, SQ, H = (2, 256, 256)
        NH = 16
        HN = H // NH
        key = jax.random.key(seed)
        ks = jax.random.split(key, 6)
        query = jax.random.normal(ks[0], (B, SQ, H), dtype=jnp.float32)
        k_in = jax.random.normal(ks[1], (B, SQ, H), dtype=jnp.float32)
        v_in = jax.random.normal(ks[2], (B, SQ, H), dtype=jnp.float32)
        Wqkv = jax.random.normal(ks[3], (3 * H, H), dtype=jnp.float32) * (1.0 / np.sqrt(H))
        Wproj = jax.random.normal(ks[4], (H, H), dtype=jnp.float32) * (1.0 / np.sqrt(H))
        bproj = jnp.zeros((H,), dtype=jnp.float32)
        return {'query': query, 'key': k_in, 'value': v_in, 'Wqkv': Wqkv, 'Wproj': Wproj, 'bproj': bproj}
    _L0_attn_in = _L0_attn_setup()

    def _L0_ffn_setup():
        import jax, jax.numpy as jnp
        import numpy as np
        TOP_K = 2
        key = jax.random.key(seed)
        ks = jax.random.split(key, 4)
        G, S, F, E, H = (4, 256, 256, 8, 256)
        return {'x': jax.random.normal(ks[0], (G, S, F), dtype=jnp.float32), 'router_logits': jax.random.normal(ks[1], (F, E), dtype=jnp.float32) * 0.02, 'gating_einsum': jax.random.normal(ks[2], (E, 2, H, F), dtype=jnp.float32) * 0.02, 'linear': jax.random.normal(ks[3], (E, H, F), dtype=jnp.float32) * 0.02, 'per_expert_scale': jnp.ones((E,), dtype=jnp.float32), 'router_scale': jnp.ones((F,), dtype=jnp.float32)}
    _L0_ffn_in = _L0_ffn_setup()
    _L0_c = _w((lambda *s: np.random.randn(*s).astype(np.float32) * 0.05)(4, 256))
    _L0_wmod = _w((lambda *s: np.random.randn(*s).astype(np.float32) * 0.05)(256, 6 * 256) * 256 ** (-0.5))
    _d = {'L0_attn_query': _L0_attn_in['query'], 'L0_attn_key': _L0_attn_in['key'], 'L0_attn_value': _L0_attn_in['value'], 'L0_attn_Wqkv': _L0_attn_in['Wqkv'], 'L0_attn_Wproj': _L0_attn_in['Wproj'], 'L0_attn_bproj': _L0_attn_in['bproj'], 'L0_ffn_router_logits': _L0_ffn_in['router_logits'], 'L0_ffn_gating_einsum': _L0_ffn_in['gating_einsum'], 'L0_ffn_linear': _L0_ffn_in['linear'], 'L0_ffn_per_expert_scale': _L0_ffn_in['per_expert_scale'], 'L0_ffn_router_scale': _L0_ffn_in['router_scale'], 'L0_c': _L0_c, 'L0_wmod': _L0_wmod}
    _x0 = _d['L0_attn_query']
    _d['L0_attn_query'] = jax.random.normal(jax.random.fold_in(jax.random.key(seed), 1), (4, 512, 256), dtype=_x0.dtype)
    del _x0
    return _d

def reference(L0_attn_query, L0_attn_key, L0_attn_value, L0_attn_Wqkv, L0_attn_Wproj, L0_attn_bproj, L0_ffn_router_logits, L0_ffn_gating_einsum, L0_ffn_linear, L0_ffn_per_expert_scale, L0_ffn_router_scale, L0_c, L0_wmod):

    def _L0_attn_ref(query, key, value, Wqkv, Wproj, bproj):
        import jax, jax.numpy as jnp
        import numpy as np
        B, SQ, H = (2, 256, 256)
        NH = 16
        HN = H // NH
        b, sq, h = query.shape
        nh, hn = (NH, HN)
        norm = 1.0 / jnp.sqrt(jnp.asarray(hn, query.dtype))
        x = jnp.transpose(query, (1, 0, 2)).reshape(sq * b, h)
        mixed = x @ Wqkv.T
        mixed = mixed.reshape(sq, b, nh, 3, hn)
        q = mixed[..., 0, :]
        k = mixed[..., 1, :]
        v = mixed[..., 2, :]
        q = q.reshape(sq, b * nh, hn).transpose(1, 0, 2)
        k = k.reshape(sq, b * nh, hn).transpose(1, 0, 2)
        v = v.reshape(sq, b * nh, hn).transpose(1, 0, 2)
        attn = jnp.einsum('gqd,gkd->gqk', q, k) * norm
        attn = jax.nn.softmax(attn, axis=-1)
        ctx = jnp.einsum('gqk,gkd->gqd', attn, v)
        ctx = ctx.reshape(nh, b, sq, hn)
        ctx = jnp.transpose(ctx, (2, 1, 0, 3)).reshape(sq * b, h)
        out = ctx @ Wproj.T + bproj
        out = out.reshape(sq, b, h)
        return jnp.transpose(out, (1, 0, 2))

    def _L0_ffn_ref(x, router_logits, gating_einsum, linear, per_expert_scale, router_scale):
        import jax, jax.numpy as jnp
        import numpy as np
        TOP_K = 2
        G, S, F = x.shape
        E = router_logits.shape[-1]
        H = linear.shape[1]
        k = TOP_K
        dtype = x.dtype
        var = jnp.mean(jnp.square(x.astype(jnp.float32)), axis=-1, keepdims=True)
        router_input = x * jax.lax.rsqrt(var + 1e-06).astype(dtype)
        root_size = jax.lax.rsqrt(jnp.array(F, dtype=dtype))
        router_input = router_input * root_size * router_scale.astype(dtype)
        logits = jnp.einsum('gsd,de->gse', router_input, router_logits.astype(dtype))
        logits32 = logits.astype(jnp.float32)
        probs = jax.nn.softmax(logits32, axis=-1)
        _, choices = jax.lax.approx_max_k(logits32, k=k)
        indicator = jax.nn.one_hot(choices, E, dtype=probs.dtype).sum(axis=-2)
        renorm = jnp.sum(indicator * probs, axis=-1, keepdims=True)
        renorm = jnp.where(renorm > 0.0, renorm, 1.0)
        weights = probs / renorm
        x_flat = x.reshape((-1, F))
        batch_size = G * S
        choices_flat = choices.ravel()
        xs_order = choices_flat.argsort()
        xs_reverse_argsort = xs_order.argsort()
        xs_indices = jnp.repeat(jnp.arange(batch_size), k)[xs_order]
        sorted_xs = x_flat[xs_indices, :]
        choices_oh = jax.nn.one_hot(choices, num_classes=E, dtype=jnp.int32)
        tokens_per_expert = jnp.sum(choices_oh, axis=(0, 1, 2))
        combine_weights = (choices_oh.astype(jnp.float32) * jnp.expand_dims(weights, axis=2)).sum(axis=-1).astype(weights.dtype)
        w_gate = jnp.transpose(gating_einsum, (0, 3, 1, 2)).reshape(E, F, 2 * H)
        gate_out = jax.lax.ragged_dot(sorted_xs, w_gate.astype(dtype), group_sizes=tokens_per_expert)
        gate_out = gate_out.reshape(gate_out.shape[0], 2, H)
        activation = jax.nn.gelu(gate_out[:, 0, :]) * gate_out[:, 1, :]
        expert_outputs = jax.lax.ragged_dot(activation, linear.astype(dtype), group_sizes=tokens_per_expert)
        expert_indices = jnp.repeat(jnp.arange(E), tokens_per_expert, total_repeat_length=expert_outputs.shape[0])
        expert_outputs = expert_outputs * per_expert_scale.astype(expert_outputs.dtype)[expert_indices, None]
        out = expert_outputs[xs_reverse_argsort].reshape((G, S, k, -1))
        out = jnp.einsum('blkd,blk->bld', out, combine_weights, preferred_element_type=out.dtype)
        return out
    x = L0_attn_query
    mod = (_silu(L0_c) @ L0_wmod).reshape(L0_c.shape[0], 6, 1, -1)
    sa, ca, ga, sb, cb, gb = (mod[:, 0], mod[:, 1], mod[:, 2], mod[:, 3], mod[:, 4], mod[:, 5])
    ga = (2 * (ga >= 0) - 1) * jnp.maximum(jnp.abs(ga), 0.25)
    gb = (2 * (gb >= 0) - 1) * jnp.maximum(jnp.abs(gb), 0.25)
    h = _layernorm(x, axis=-1) * (1 + ca) + sa
    x = x + ga * _L0_attn_ref(h, L0_attn_key, L0_attn_value, L0_attn_Wqkv, L0_attn_Wproj, L0_attn_bproj)
    h = _layernorm(x, axis=-1) * (1 + cb) + sb
    x = x + gb * _L0_ffn_ref(h, L0_ffn_router_logits, L0_ffn_gating_einsum, L0_ffn_linear, L0_ffn_per_expert_scale, L0_ffn_router_scale)
    return x

_drawn_inputs = setup_inputs


def setup_inputs(seed=0):
    import zlib

    import numpy as np

    out = dict(_drawn_inputs(seed))
    spreads = {'L0_attn_bproj': (0.0, 0.326),
     'L0_ffn_per_expert_scale': (1.0, 0.6),
     'L0_ffn_router_scale': (1.0, 0.6)}
    factors = {'L0_ffn_router_logits': 8.0, 'L0_ffn_gating_einsum': 8.0, 'L0_ffn_linear': 8.0}
    for name, (base, spread) in spreads.items():
        noise = np.random.default_rng([zlib.crc32(name.encode()), seed]).standard_normal(out[name].shape)
        drawn = base * np.exp(spread * noise) if base else spread * noise
        out[name] = jnp.asarray(drawn.astype(out[name].dtype))
    for name, factor in factors.items():
        out[name] = (out[name] * factor).astype(out[name].dtype)
    return out
```

```python
from contextlib import ExitStack

import concourse.bass as bass
from concourse import mybir

F32 = mybir.dt.float32
BF16 = mybir.dt.bfloat16
U32 = mybir.dt.uint32
I32 = mybir.dt.int32
ACT = mybir.ActivationFunctionType
ALU = mybir.AluOpType
AX = mybir.AxisListType.X

P = 128
B, SQ, H = 4, 512, 256
NH, HN = 16, 16
TB = SQ // P
NT = B * TB
KC = H // P
NQ = B * NH // 4
PR = 6 * HN
MR = 3
E = 8
CAP = (B * SQ * 2 + E * (P - 1)) // P
SEG = B * SQ + P
FULL = B * SQ * 2 // P
DUMMY = E * SEG
ROWS = DUMMY + (CAP - FULL) * P
ONE = 1
BIG = 32768.0
EPS_LN, EPS_RMS = 1e-5, 1e-6
SA, CA, GA, SB, CB, GB = range(6)


def adaln_block(nc, query, w_qkv, w_proj, b_proj, router_w, gating, linear,
                expert_scale, router_scale, cond, w_mod, out):
    ctx = ExitStack()
    with ctx:
        def sb(name, shape, dt=F32):
            return ctx.enter_context(nc.sbuf_tensor(name, shape, dt))

        def sem(name):
            return ctx.enter_context(nc.semaphore(name))

        def dram(name, shape, dt=F32):
            return nc.dram_tensor(name, shape, dt, kind="Internal").ap()

        qk_d = dram("qk_d", [2, NQ, 3, 64, SQ], BF16)
        ctx_d = dram("ctx_d", [NQ, P, SQ])
        mod_d = dram("mod_d", [B, 6 * H])
        slots_d = dram("slots_d", [ROWS, H])
        made_d = dram("made_d", [CAP * P, H])

        ident = sb("ident", [P, P])
        minus_half = sb("minus_half", [P, 16])
        identb = sb("identb", [P, P], BF16)
        x_sb = sb("x_sb", [P, NT, H])
        w_T = sb("w_T", [P, KC, 3 * H])
        wp_T = sb("wp_T", [P, KC, H])
        lin = sb("lin", [P, E, KC, H])
        lin_flat = lin[:, :, :, :].rearrange("p e k n -> p (e k n)")
        wmod = lin_flat[:, 0:12 * H].rearrange("p (k n) -> p k n", k=KC)
        wp_raw = lin_flat[:, 12 * H:14 * H].rearrange("p (k n) -> p k n", k=KC)
        gate_T = sb("gate_T", [P, E, KC, 2 * H])
        cT = sb("cT", [P, KC, B])
        sig = sb("sig", [P, KC, B])
        area = sb("area", [P, 8 * H])
        mod_r = area[0:B, 0:6 * H]
        sgn = sb("sgn", [B, 2, H])
        modT = sb("modT", [P, 4, B])
        mod_b = sb("mod_b", [P, 4, B, H])
        mod_flat = mod_b[:, :, :, :].rearrange("p r b n -> p (r b n)")
        bp_b = sb("bp_b", [P, H])
        st = sb("st", [P, TB, 6])
        mv = sb("mv", [P, TB, 2])
        rstd = sb("rstd", [P, TB])
        nbias = sb("nbias", [P, TB])
        xn = mod_flat[:, 0:8 * H].rearrange("p (n t h) -> p n t h", n=2, t=TB)
        hT = mod_flat[:, 8 * H:16 * H].rearrange("p (n k x) -> p n k x", n=2, k=KC)
        space = sb("space", [P, 12 * H])
        w_raw = space[:, 0:6 * H].rearrange("p (s n) -> p s n", s=6)
        pieces = space[:, :].bitcast(BF16).rearrange("p (m c x) -> p m c x", m=4, c=3)
        wp_g = space[:, 0:8 * H].rearrange("p (b k n) -> p b k n", b=B, k=KC)
        rest = sb("rest", [P, 2, SQ])
        v_all = sb("v_all", [P, NQ, TB, P])
        v_st = area[:, 0:4 * H].rearrange("p (n x) -> p n x", n=2)
        qst = sb("qst", [P, 4, 4 * SQ], BF16)
        kst = sb("kst", [P, 4, 4 * SQ], BF16)
        negm = sb("negm", [P, 2, 16])
        mrest = sb("mrest", [P, 2, 16])
        mpc = sb("mpc", [P, 2, P], BF16)
        m_T = sb("m_T", [48, 2, P], BF16)
        probs = sb("probs", [P, 2, 4 * SQ])
        gate_raw = probs[:, :, :].rearrange("p n x -> p (n x)").rearrange("p (e c f) -> p e c f", e=4, c=4)
        h2 = qst[:, :, :].rearrange("p n x -> p (n x)").bitcast(F32).rearrange("p (n h) -> p n h", n=NT)
        ctx_o = area[:, 4 * H:8 * H].rearrange("p (n x) -> p n x", n=2)
        v_flat = v_all[:, :, :, :].rearrange("p q t c -> p (q t c)")
        ctx_n = v_flat[:, 0:KC * B * SQ].rearrange("p (k b x) -> p k b x", k=KC, b=B)
        sums = v_flat[:, KC * B * SQ:2 * KC * B * SQ].rearrange("p (k b x) -> p k b x", k=KC, b=B)

        late = kst[:, :, :].rearrange("p n x -> p (n x)").bitcast(F32)
        h2T = late[:, 0:4 * H].rearrange("p (n k x) -> p n k x", n=4, k=KC)
        squares = late[:, 4 * H:5 * H]
        xs = late[:, 5 * H:7 * H].rearrange("p (n h) -> p n h", n=2)
        xsT = late[:, 7 * H:9 * H].rearrange("p (n k x) -> p n k x", n=2, k=KC)
        gelu = late[:, 9 * H:11 * H].rearrange("p (n h) -> p n h", n=2)
        acts = late[:, 11 * H:13 * H].rearrange("p (n h) -> p n h", n=2)
        actsT = late[:, 13 * H:14 * H].rearrange("p (k x) -> p k x", k=KC)
        made = late[:, 14 * H:16 * H].rearrange("p (n h) -> p n h", n=2)
        back = probs[:, :, :].rearrange("p n x -> p (n x)").rearrange("p (n c h) -> p n c h", n=8, c=2)
        taken = [0]

        def small(*shape, dt=F32):
            n = 1
            for d in shape:
                n *= d
            v = area[:, taken[0]:taken[0] + n]
            taken[0] += n
            assert taken[0] <= 8 * H
            v = v if dt == F32 else v.bitcast(dt)
            if len(shape) == 2:
                v = v.rearrange("p (a b) -> p a b", a=shape[0])
            if len(shape) == 3:
                v = v.rearrange("p (a b c) -> p a b c", a=shape[0], b=shape[1])
            return v

        st2, mv2 = small(TB, 6), small(TB, 2)
        rstd2, nbias2 = small(TB), small(TB)
        ssq, rrms = small(NT), small(NT)
        logit, prob, chosen = small(TB, E), small(TB, E), small(TB, E)
        top, total, guard = small(TB), small(TB), small(TB)
        above, equal = small(TB, E, E), small(TB, E, E)
        count, totals, upto, place = small(TB, E), small(E, TB), small(E, TB), small(TB, E)
        mark, hit = small(TB, E), small(TB, E)
        start = small(E)
        hits = small(2, NT, E)
        slot_b = small(2, NT, dt=U32)
        slot_f, slot_w = small(2, NT), small(2, NT)
        slot_i = small(2, NT, dt=U32)
        earlier = sb("earlier", [P, E * E])
        after_0 = sb("after_0", [P, E * TB])
        minus_geq = sb("minus_geq", [P, P])
        ones = sb("ones", [P, P])
        seg_0 = sb("seg_0", [P, E])
        zeros = sb("zeros", [P, H])
        tab = sb("tab", [1, 2, 40 * E])
        m_rows = sb("m_rows", [P, E * 16])
        work = v_flat[0:1, 0:3 * 40 * E].rearrange("o (a b) -> o a b", a=3)
        ends, firsts, filled, shift = (sb(n, [P, E]) for n in ("ends", "firsts", "filled", "shift"))
        tab_f = sb("tab_f", [1, 2 * 40])
        row_shift = sb("row_shift", [P, NT])
        tab_i = sb("tab_i", [1, 2 * 40], I32)
        run_i = sb("run_i", [1, E], I32)
        r_w = sb("r_w", [P, KC, E])
        r_scale = sb("r_scale", [P, KC])
        e_scale = sb("e_scale", [P, E])

        ps = ctx.enter_context(nc.psum_tensor("ps", [P, 8, 512], F32))

        x_loaded = [sem(f"x_loaded{b}") for b in range(B)]
        w_loaded = sem("w_loaded")
        wp_loaded = sem("wp_loaded")
        mod_loaded = sem("mod_loaded")
        bp_loaded = sem("bp_loaded")
        pool_step = sem("pool_step")
        ident_ready = sem("ident_ready")
        v_init = sem("v_init")
        sig_exp = sem("sig_exp")
        silu_ready = sem("silu_ready")
        dve_chain = sem("dve_chain")
        wT_done = sem("wT_done")
        wT_evac = sem("wT_evac")
        modrow_done = sem("modrow_done")
        modrow_ready = sem("modrow_ready")
        modT_done = sem("modT_done")
        modT_ready = sem("modT_ready")
        mod_stored = sem("mod_stored")
        modb_loaded = sem("modb_loaded")
        var_ready = sem("var_ready")
        var_eps = sem("var_eps")
        rstd_ready = sem("rstd_ready")
        xn_ready = sem("xn_ready")
        xT_done = sem("xT_done")
        hT_ready = sem("hT_ready")
        qk_done = sem("qk_done")
        hi_ready = sem("hi_ready")
        rest_ready = sem("rest_ready")
        mid_ready = sem("mid_ready")
        lo_ready = sem("lo_ready")
        qk_stored = [sem(f"qk_stored{n}") for n in range(4)]
        v_done = sem("v_done")
        v_evac = sem("v_evac")
        stack_loaded = [sem(f"stack_loaded{n}") for n in range(4)]
        mrow_loaded = [sem(f"mrow_loaded{n}") for n in range(4)]
        s_ready = sem("s_ready")
        s_reduced = sem("s_reduced")
        split1, split2, split3, m_split = (sem(n) for n in ("split1", "split2", "split3", "m_split"))
        m_turned = sem("m_turned")
        m_evac = sem("m_evac")
        st_ready = sem("st_ready")
        exp_done = sem("exp_done")
        v_staged = sem("v_staged")
        pv_done = sem("pv_done")
        ctx_evac = sem("ctx_evac")
        ctx_stored = [sem(f"ctx_stored{n}") for n in range(2)]
        ctx_loaded = [sem(f"ctx_loaded{n}") for n in range(B)]
        ctx_ready = sem("ctx_ready")
        proj_done = sem("proj_done")
        x1_ready = sem("x1_ready")
        xb_ready = sem("xb_ready")
        out_stored = sem("out_stored")
        gate_loaded = sem("gate_loaded")
        gate_turned = sem("gate_turned")
        gate_evac = sem("gate_evac")
        lin_loaded = sem("lin_loaded")
        router_loaded = sem("router_loaded")
        rw_ready = sem("rw_ready")
        const_ready = sem("const_ready")
        wpg_ready = sem("wpg_ready")
        var2_ready, var2_eps, rstd2_ready, nbias2_ready = (sem(n) for n in ("var2_ready", "var2_eps", "rstd2_ready", "nbias2_ready"))
        normed2 = sem("normed2")
        h2_ready = sem("h2_ready")
        ssq_ready, ssq_eps, rrms_ready = (sem(n) for n in ("ssq_ready", "ssq_eps", "rrms_ready"))
        h2_turned, h2T_ready, logit_done, logit_read = (sem(n) for n in ("h2_turned", "h2T_ready", "logit_done", "logit_read"))
        d_ready, e_ready = sem("d_ready"), sem("e_ready")
        chosen_ready, counted, slot_ready = sem("chosen_ready"), sem("counted"), sem("slot_ready")
        sent = sem("sent")
        pad_stored = sem("pad_stored")
        tab_ready = sem("tab_ready")
        xs_loaded = [sem(f"xs_loaded{n}") for n in range(2)]
        xs_turned, xsT_ready, gate_done, gelu_ready, acts_ready, acts_turned, actsT_ready, down_done, made_ready = (
            sem(n) for n in ("xs_turned", "xsT_ready", "gate_done", "gelu_ready", "acts_ready", "acts_turned",
                             "actsT_ready", "down_done", "made_ready"))
        made_stored = [sem(f"made_stored{n}") for n in range(2)]
        back_loaded = [sem(f"back_loaded{n}") for n in range(8)]
        out_ready = sem("out_ready")
        squared = sem("squared")
        rows_ready = sem("rows_ready")

        block = ctx.enter_context(nc.Block())

        S_BANK, ST_BANK, PV_BANK, M_BANK = 0, 2, 6, 7
        m_ps = ps[:, M_BANK, 0:P // 2].bitcast(BF16)

        STACK = [(0, 3), (3 * HN, 2), (5 * HN, 1)]

        @block.sync
        def _(sp):
            x_v = query.rearrange("b (t p) h -> b p t h", p=P)
            sp.dma_start(x_sb[:, 0:TB, :], x_v[0]).then_inc(x_loaded[0], 16)
            for k in range(KC):
                sp.dma_start(cT[:, k, :], cond[:, k * P:(k + 1) * P].rearrange("b p -> p b"),
                             allow_slow_non_contiguous=True).then_inc(mod_loaded, 16)
            sp.dma_start(wmod[:, :, :], w_mod.rearrange("(k p) n -> p k n", p=P)).then_inc(mod_loaded, 16)
            for side in range(2):
                for quad in range(4):
                    rows = w_qkv.rearrange("(q h s d) i -> q s d h i", q=4, h=4, s=3)[quad, side]
                    sp.dma_start(w_raw[64 * (quad % 2):64 * (quad % 2) + 64, 2 * side + quad // 2, :],
                                 rows).then_inc(w_loaded, 16)
            for half in range(2):
                rows = w_qkv.rearrange("(n h s d) i -> n s h d i", n=2, h=8, s=3)[half, 2]
                sp.dma_start(w_raw[:, 4 + half, :], rows).then_inc(w_loaded, 16)
            for b in range(1, B):
                sp.dma_start(x_sb[:, b * TB:(b + 1) * TB, :], x_v[b]).then_inc(x_loaded[b], 16)
            sp.dma_start(wp_raw[:, :, :], w_proj.rearrange("(k p) n -> p k n", p=P)).then_inc(wp_loaded, 16)
            sp.dma_start(bp_b[:, :], b_proj.partition_broadcast(P)).then_inc(bp_loaded, 16)
            gate_v = gating.rearrange("e s (c p) f -> p e (s c) f", p=P)
            for e in range(4):
                sp.dma_start(gate_raw[:, e], gate_v[:, e]).then_inc(gate_loaded, 16)
            for k in range(KC):
                sp.dma_start(r_w[:, k, :], router_w[k * P:(k + 1) * P, :]).then_inc(router_loaded, 16)
                sp.dma_start(r_scale[:, k:k + 1], router_scale[k * P:(k + 1) * P].rearrange("(p o) -> p o", o=1)).then_inc(router_loaded, 16)
            sp.dma_start(e_scale[:, :], expert_scale.partition_broadcast(P)).then_inc(router_loaded, 16)
            sp.wait_ge(modrow_ready, 1)
            sp.dma_start(mod_d, mod_r[:, :]).then_inc(mod_stored, 16)
            sp.wait_ge(mod_stored, 16)

            for b in range(B):
                for m in range(4):
                    n = 4 * b + m
                    side, half = m // 2, m % 2
                    sp.wait_ge(lo_ready, n + 1)
                    for q in range(2):
                        sp.dma_start(qk_d[side, 4 * b + 2 * half + q].rearrange("p r x -> r p x"),
                                     pieces[64 * q:64 * q + 64, m, :, :]).then_inc(qk_stored[m], 16)
                if b == 2:
                    sp.wait_ge(gate_turned, 4)
                    for e in range(4):
                        sp.dma_start(gate_raw[:, e], gate_v[:, 4 + e]).then_inc(gate_loaded, 16)

            def load_stack(i, par):
                for side, stack in ((0, qst), (1, kst)):
                    rows = qk_d[side, i] if isinstance(i, int) else \
                        qk_d[side, bass.ds(i, 1)].rearrange("o p r x -> (o p) r x")
                    rows = rows.rearrange("p (d h) x -> p d (h x)", d=HN)
                    for piece, (r0, n) in enumerate(STACK):
                        src = rows[0:n] if side == 0 else rows[piece:piece + 1].to_broadcast([n, HN, 4 * SQ])
                        sp.dma_start(stack[r0:r0 + n * HN, par, :], src).then_inc(stack_loaded[par], 16)

            def load_mrow(par4, par2):
                sp.dma_start(qst[PR:PR + MR, par4, :], m_T[:, par2, :]).then_inc(mrow_loaded[par4], 16)

            for m in range(4):
                sp.wait_ge(qk_stored[m], 32)
            for i in range(4):
                load_stack(i, i)
            sp.wait_ge(v_done, 2 * B)
            for n, row in enumerate((GA, SB, CB, GB)):
                sp.dma_start(mod_b[:, n, :, :],
                             mod_d[:, row * H:(row + 1) * H].partition_broadcast(P)).then_inc(modb_loaded, 16)
            sp.wait_ge(wT_done, 4)
            sp.dma_start(lin[:, :, :, :], linear.rearrange("e (k p) f -> p e k f", p=P)).then_inc(lin_loaded, 16)
            sp.wait_ge(const_ready, 1)
            for n in range(CAP - FULL):
                sp.dma_start(slots_d[DUMMY + n * P:DUMMY + (n + 1) * P, :], zeros[:, :]).then_inc(pad_stored, 16)
            sp.wait_ge(m_evac, 1)
            load_mrow(0, 0)
            for m in range(4):
                sp.wait_ge(qk_stored[m], 32 * B)

            def quad(it, u, more):
                i = 4 * it + u
                if more or u < 3:
                    sp.wait_ge(m_evac, i + 2)
                    load_mrow((u + 1) % 4, (u + 1) % 2)
                if more:
                    sp.wait_ge(st_ready, 8 * i + 8)
                    load_stack(i + 4, u)
                sp.wait_ge(ctx_evac, ONE + i + 1)
                dst = ctx_d[i] if isinstance(i, int) else ctx_d[bass.ds(i, 1)]
                sp.dma_start(dst, ctx_o[:, u % 2, :]).then_inc(ctx_stored[u % 2], 16)

            with sp.Fori(0, 3) as it:
                for u in range(4):
                    quad(it, u, True)
            for u in range(4):
                quad(3, u, False)

            for n in range(2):
                sp.wait_ge(ctx_stored[n], ONE + 16 * NQ // 2)
            for b in range(B):
                for kc in range(KC):
                    src = ctx_d[8 * kc:8 * kc + 8, 32 * b:32 * b + HN, :]
                    sp.dma_start(ctx_n[:, kc, b, :], src).then_inc(ctx_loaded[b], 16)
                    src = ctx_d[8 * kc:8 * kc + 8, 32 * b + HN:32 * b + HN + 1, :].to_broadcast([8, HN, SQ])
                    sp.dma_start(sums[:, kc, b, :], src).then_inc(ctx_loaded[b], 16)

            sp.wait_ge(tab_ready, 1)
            for e in range(E):
                row = sp.value_load(run_i[0:1, e:e + 1], min_val=e * SEG, max_val=e * SEG + B * SQ)
                sp.dma_start(slots_d[bass.ds(row, P), :], zeros[:, :]).then_inc(pad_stored, 16)
            sp.wait_ge(pad_stored, 16 * (E + CAP - FULL))
            sp.wait_ge(sent, 16 * 2 * NT)

            def load_slots(t, u):
                row = sp.value_load(tab_i[0:1, bass.ds(t, 1)], min_val=0, max_val=ROWS - P)
                sp.dma_start(xs[:, u, :], slots_d[bass.ds(row, P), :]).then_inc(xs_loaded[u], 16)

            def store_made(t, u):
                sp.wait_ge(made_ready, t + 1)
                sp.dma_start(made_d[bass.ds(t * P, P), :], made[:, u, :]).then_inc(made_stored[u], 16)

            load_slots(0, 0)
            load_slots(1, 1)

            def tile(t, u, more):
                if more:
                    sp.wait_ge(xs_turned, t + 1)
                    load_slots(t + 2, u)
                store_made(t, u)

            with sp.Fori(0, (CAP - 3) // 2) as it:
                for u in range(2):
                    tile(2 * it + u, u, True)
            for t in range(CAP - 3, CAP):
                tile(t, t % 2, t + 2 < CAP)

            out_v = out.rearrange("b (t p) h -> (b t) p h", p=P)
            for n in range(NT):
                sp.wait_ge(out_ready, n + 1)
                sp.dma_start(out_v[n], x_sb[:, n, :]).then_inc(out_stored, 16)
            sp.wait_ge(out_stored, 16 * NT)

        @block.gpsimd
        def _(pool):
            pool.memset(minus_half[:, :], -0.5)
            pool.memset(ident[:, :], 0.0).then_inc(pool_step, 1)
            pool.wait_ge(pool_step, 1)
            pool.affine_select(out=ident[:, :], in_=ident[:, :], compare_op=ALU.not_equal, fill=1.0,
                               base=0, pattern=[[-1, P]], channel_multiplier=1).then_inc(ident_ready, 1)
            pool.wait_ge(ident_ready, 1)
            pool.tensor_copy(identb[:, :], ident[:, :]).then_inc(ident_ready, 1)

            def inverse_deviation(b):
                pool.wait_ge(var_ready, b + 1)
                pool.tensor_scalar(rstd[:, :], mv[:, :, 1], EPS_LN, None, ALU.add).then_inc(var_eps, 1)
                pool.wait_ge(var_eps, b + 1)
                pool.tensor_tensor(rstd[:, :], rstd[:, :], minus_half[:, 0:TB], ALU.pow).then_inc(rstd_ready, 1)

            inverse_deviation(0)
            inverse_deviation(1)
            pool.memset(v_all[:, :, :, :], 1.0).then_inc(v_init, 1)
            pool.wait_ge(v_init, 1)
            pool.memset(kst[PR:PR + MR, :, :], 1.0).then_inc(v_init, 1)
            pool.wait_ge(v_init, 2)
            pool.memset(zeros[:, :], 0.0)
            pool.memset(mpc[:, :, :], 0.0)
            for e in range(E):
                pool.memset(seg_0[:, e:e + 1], float(e * SEG))
            pool.memset(ones[:, :], 1.0)
            pool.memset(minus_geq[:, :], -1.0)
            pool.memset(after_0[:, :], 1.0)
            pool.memset(earlier[:, :], 1.0).then_inc(const_ready, 1)
            pool.wait_ge(const_ready, 1)
            pool.affine_select(out=minus_geq[:, :], in_=minus_geq[:, :], compare_op=ALU.is_ge, fill=0.0,
                               base=0, pattern=[[-1, P]], channel_multiplier=1)
            pool.affine_select(out=after_0[:, :], in_=after_0[:, :], compare_op=ALU.is_gt, fill=0.0,
                               base=0, pattern=[[0, E], [1, TB]], channel_multiplier=0)
            pool.affine_select(out=earlier[:, :], in_=earlier[:, :], compare_op=ALU.is_gt, fill=0.0,
                               base=0, pattern=[[1, E], [-1, E]], channel_multiplier=0).then_inc(const_ready, 1)
            pool.wait_ge(const_ready, 2)
            pool.iota(m_rows[:, :], pattern=[[0, E], [P, 16]], base=0, channel_multiplier=0,
                      allow_small_or_imprecise_dtypes=True).then_inc(const_ready, 1)
            pool.wait_ge(const_ready, 3)
            pool.iota(tab[:, 0, :], pattern=[[1, 40], [0, E]], base=0, channel_multiplier=0,
                      allow_small_or_imprecise_dtypes=True)
            pool.iota(tab[:, 1, :], pattern=[[0, 40], [1, E]], base=0, channel_multiplier=0,
                      allow_small_or_imprecise_dtypes=True).then_inc(const_ready, 1)
            pool.wait_ge(router_loaded, 80)
            for k in range(KC):
                last = pool.tensor_scalar(r_w[:, k, :], r_w[:, k, :], r_scale[:, k:k + 1], H ** -0.5, ALU.mult, ALU.mult)
            last.then_inc(rw_ready, 1)
            pool.wait_ge(rw_ready, 1)
            for n in range(4 * B):
                if n in (4, 8):
                    inverse_deviation(1 + n // 4)
                pool.wait_ge(rest_ready, n + 1)
                pool.tensor_scalar(pieces[:, n % 4, 1, :], rest[:, n % 2, :], 1.0, None, ALU.mult)\
                    .then_inc(mid_ready, 1)

            def stage_v(i, par2):
                pool.wait_ge(v_init, 2)
                pool.tensor_copy(v_st[:, par2, :], v_all[:, bass.ds(i, 1), :, :].rearrange("p o t c -> p (o t c)"))\
                    .then_inc(v_staged, 1)

            def split_max(j, par2):
                pc = mpc[:, par2, 0:48].rearrange("p (s n) -> p s n", s=MR)
                pool.tensor_tensor(pc[:, 0, :], negm[:, par2, :], ones[:, 0:16], ALU.mult).then_inc(split1, 1)
                pool.wait_ge(split1, j + 1)
                pool.tensor_tensor(mrest[:, par2, :], negm[:, par2, :], pc[:, 0, :], ALU.subtract).then_inc(split2, 1)
                pool.wait_ge(split2, j + 1)
                pool.tensor_tensor(pc[:, 1, :], mrest[:, par2, :], ones[:, 0:16], ALU.mult).then_inc(split3, 1)
                pool.wait_ge(split3, j + 1)
                pool.tensor_tensor(pc[:, 2, :], mrest[:, par2, :], pc[:, 1, :], ALU.subtract).then_inc(m_split, 1)

            pool.wait_ge(v_evac, 2 * B)
            stage_v(0, 0)
            for j in range(2):
                pool.wait_ge(s_reduced, 16 * (j + 1))
                split_max(j, j)

            def quad(it, u, more):
                i = 4 * it + u
                if more or u < 3:
                    if not more:
                        pool.wait_ge(pv_done, 4 * i)
                    stage_v(i + 1, (u + 1) % 2)
                if more or u < 2:
                    pool.wait_ge(s_reduced, 16 * (i + 3))
                    pool.wait_ge(m_turned, i + 1)
                    split_max(i + 2, u % 2)

            with pool.Fori(0, 3) as it:
                for u in range(4):
                    quad(it, u, True)
            pool.wait_ge(modb_loaded, 64)
            pool.wait_ge(bp_loaded, 16)
            pool.wait_ge(xn_ready, B)
            for u in range(4):
                quad(3, u, False)
                pool.tensor_tensor(rest[:, 0, 0:H], mod_b[:, 0, u, :], bp_b[:, :], ALU.mult).then_inc(pool_step, 1)
                pool.wait_ge(pool_step, 2 + u)
                for t in range(TB):
                    last = pool.tensor_tensor(x_sb[:, u * TB + t, :], x_sb[:, u * TB + t, :], rest[:, 0, 0:H], ALU.add)
                last.then_inc(xb_ready, 1)
                pool.wait_ge(xb_ready, u + 1)
                for k in range(KC):
                    last = pool.tensor_tensor(wp_g[:, u, k, :], wp_T[:, k, :], mod_b[:, 0, u, :], ALU.mult)
                last.then_inc(wpg_ready, 1)
                pool.wait_ge(wpg_ready, u + 1)

            def power(out_, in_, scale, eps, added, ready, b):
                pool.tensor_scalar(out_, in_, scale, eps, ALU.mult, ALU.add).then_inc(added, 1)
                pool.wait_ge(added, b + 1)
                pool.tensor_tensor(out_, out_, minus_half[:, 0:TB], ALU.pow).then_inc(ready, 1)

            for b in range(B):
                pool.wait_ge(var2_ready, b + 1)
                power(rstd2, mv2[:, :, 1], 1.0, EPS_LN, var2_eps, rstd2_ready, b)
                pool.wait_ge(ssq_ready, b + 1)
                power(rrms[:, b * TB:(b + 1) * TB], ssq[:, b * TB:(b + 1) * TB], 1.0 / H, EPS_RMS, ssq_eps, rrms_ready, b)
                pool.wait_ge(slot_ready, b + 1)
                for n in range(b * TB, (b + 1) * TB):
                    for c in range(2):
                        pool.indirect_dma_start(out=slots_d, out_offset=bass.IndirectOffsetOnAxis(ap=slot_i[:, c, n:n + 1], axis=0),
                                                in_=h2[:, n, :], in_offset=None).then_inc(sent, 16)
            pool.wait_ge(rows_ready, 1)
            for n in range(2):
                pool.wait_ge(made_stored[n], ONE + 16 * (CAP // 2 + (CAP % 2 if n == 0 else 0)))
            for n in range(NT):
                if n >= 8:
                    pool.wait_ge(out_ready, n - 7)
                for c in range(2):
                    pool.indirect_dma_start(out=back[:, n % 8, c, :], out_offset=None, in_=made_d,
                                            in_offset=bass.IndirectOffsetOnAxis(ap=slot_b[:, c, n:n + 1], axis=0))\
                        .then_inc(back_loaded[n % 8], 16)

        @block.scalar
        def _(act):
            act.sem_inc(ctx_evac, ONE)
            for n in range(2):
                act.sem_inc(ctx_stored[n], ONE)
                act.sem_inc(made_stored[n], ONE)
            act.wait_ge(mod_loaded, 48)
            act.activation(sig[:, :, :], cT[:, :, :], ACT.Exp, scale=-1.0).then_inc(sig_exp, 1)
            for s in range(4):
                act.wait_ge(wT_done, s + 1)
                dst = w_T[:, :, s * H:(s + 1) * H] if s < 3 else wp_T[:, :, :]
                act.activation(dst, ps[:, s, :].rearrange("p (k n) -> p k n", k=KC), ACT.Copy).then_inc(wT_evac, 1)

            act.wait_ge(modT_ready, 1)
            act.wait_ge(v_init, 2)

            def evac_hT(b):
                act.wait_ge(xT_done, b + 1)
                if b >= 2:
                    act.wait_ge(v_done, 2 * (b - 1))
                for k in range(KC):
                    last = act.activation(hT[:, b % 2, k, :], ps[:, k, :], ACT.Identity,
                                          bias=modT[:, SA * KC + k, b:b + 1], scale=modT[:, CA * KC + k, b:b + 1])
                last.then_inc(hT_ready, 1)

            evac_hT(0)
            for b in range(B):
                for m in range(4):
                    n = 4 * b + m
                    act.wait_ge(qk_done, n + 1)
                    if b >= 1:
                        act.wait_ge(qk_stored[m], 32 * b)
                    act.activation(pieces[:, m, 0, :], ps[:, 2 + m, :], ACT.Copy,
                                   scale=HN ** -0.5 if m < 2 else 1.0).then_inc(hi_ready, 1)
                if b + 1 < B:
                    evac_hT(b + 1)
                for hf in range(2):
                    act.wait_ge(v_done, 2 * b + hf + 1)
                    for tt in range(2):
                        dst = v_all[:, 4 * b:4 * b + 4, 2 * hf + tt, :].rearrange("p q (h c) -> p q h c", h=4)
                        last = act.activation(dst[:, :, :, 0:HN],
                                              ps[:, 6 + hf, tt * H:(tt + 1) * H].rearrange("p (q h d) -> p q h d", q=4, h=4),
                                              ACT.Copy)
                    last.then_inc(v_evac, 1)
                if b % 2:
                    for e in range(2 * (b - 1), 2 * (b + 1)):
                        act.wait_ge(gate_turned, e + 1)
                        act.activation(gate_T[:, e, :, :], ps[:, 2 + 2 * (e % 2):4 + 2 * (e % 2), :], ACT.Copy)\
                            .then_inc(gate_evac, 1)

            def exps(n, pair, slot):
                act.wait_ge(st_ready, n + 1)
                act.activation(probs[:, slot, pair * 2 * SQ:(pair + 1) * 2 * SQ],
                               ps[:, ST_BANK + 2 * pair:ST_BANK + 2 * pair + 2, :], ACT.Exp).then_inc(exp_done, 1)

            def evac_m(j, par2):
                act.wait_ge(m_turned, j + 1)
                act.activation(m_T[:, par2, :], m_ps[0:48, :], ACT.Copy).then_inc(m_evac, 1)

            def evac_ctx(i, par2):
                act.wait_ge(pv_done, 4 * i + 4)
                act.activation(ctx_o[:, par2, :], ps[:, PV_BANK, :], ACT.Copy).then_inc(ctx_evac, 1)

            evac_m(0, 0)
            exps(0, 0, 0)
            exps(1, 1, 0)

            def quad(it, u, more):
                i = 4 * it + u
                for k in range(4):
                    if k < 3 or more or u < 3:
                        for pair in range(2):
                            exps(8 * i + 2 * (k + 1) + pair, pair, (k + 1) % 2)
                    if k == 2 and (more or u < 3):
                        evac_m(i + 1, (u + 1) % 2)
                act.wait_ge(ctx_stored[u % 2], ONE + 16 * (2 * it + u // 2))
                evac_ctx(i, u % 2)

            with act.Fori(0, 3) as it:
                for u in range(4):
                    quad(it, u, True)
            for u in range(4):
                quad(3, u, False)

            def x1_out(b):
                for n in range(b * TB, (b + 1) * TB):
                    act.wait_ge(proj_done, n + 1)
                    act.activation(x_sb[:, n, :], ps[:, n % 2, 0:H], ACT.Copy).then_inc(x1_ready, 1)

            x1_out(0)
            for b in range(B):
                act.wait_ge(nbias2_ready, b + 1)
                for t in range(TB):
                    last = act.activation(h2[:, b * TB + t, :], x_sb[:, b * TB + t, :], ACT.Identity,
                                          bias=nbias2[:, t:t + 1], scale=rstd2[:, t:t + 1])
                last.then_inc(normed2, 1)
                if b + 1 < B:
                    x1_out(b + 1)
                act.wait_ge(h2_ready, b + 1)
                for t in range(TB):
                    n = b * TB + t
                    if n:
                        act.wait_ge(squared, n)
                    act.activation(squares, h2[:, n, :], ACT.Square, accum_out=ssq[:, n:n + 1]).then_inc(squared, 1)
                act.wait_ge(squared, TB * (b + 1))
                act.activation(guard[:, 0:1], ssq[:, b * TB:b * TB + 1], ACT.Copy).then_inc(ssq_ready, 1)
                for t in range(TB):
                    n = b * TB + t
                    act.wait_ge(h2_turned, n + 1)
                    if n >= 4:
                        act.wait_ge(logit_done, n - 3)
                    act.activation(h2T[:, n % 4, :, :], ps[:, 2 + n % 2, 0:H].rearrange("p (k x) -> p k x", k=KC),
                                   ACT.Copy).then_inc(h2T_ready, 1)
                act.wait_ge(d_ready, b + 1)
                act.activation(prob[:, :, :], logit[:, :, :], ACT.Exp).then_inc(e_ready, 1)

            def take_xsT(t, u):
                act.wait_ge(xs_turned, t + 1)
                act.activation(xsT[:, u, :, :], ps[:, 0, 0:H].rearrange("p (k x) -> p k x", k=KC), ACT.Copy).then_inc(xsT_ready, 1)

            def do_gelu(t, u):
                act.wait_ge(gate_done, t + 1)
                act.activation(gelu[:, u, :], ps[:, 2 + u, 0:H], ACT.Gelu_apprx_tanh).then_inc(gelu_ready, 1)

            def take_made(t, u, before):
                act.wait_ge(down_done, t + 1)
                act.wait_ge(made_stored[u], ONE + 16 * before)
                act.activation(made[:, u, :], ps[:, 4, 0:H], ACT.Copy).then_inc(made_ready, 1)

            take_xsT(0, 0)
            do_gelu(0, 0)
            with act.Fori(0, CAP // 2) as it:
                for u in range(2):
                    t = 2 * it + u
                    take_xsT(t + 1, 1 - u)
                    do_gelu(t + 1, 1 - u)
                    take_made(t, u, it)
            take_made(CAP - 1, 0, CAP // 2)

        @block.vector
        def _(dve):
            chain = [0]

            def link(ins):
                chain[0] += 1
                ins.then_inc(dve_chain, 1)
                dve.wait_ge(dve_chain, chain[0])

            dve.wait_ge(sig_exp, 1)
            link(dve.tensor_scalar(sig[:, :, :], sig[:, :, :], 1.0, None, ALU.add))
            link(dve.reciprocal(sig[:, :, :], sig[:, :, :]))
            dve.tensor_tensor(sig[:, :, :], cT[:, :, :], sig[:, :, :], ALU.mult).then_inc(silu_ready, 1)

            def layer_norm(b):
                dve.wait_ge(x_loaded[b], 16)
                for t in range(TB):
                    last = dve.bn_stats(st[:, t, :], x_sb[:, b * TB + t, :])
                link(last)
                for t in range(TB):
                    last = dve.bn_aggr(mv[:, t, :], st[:, t, :])
                last.then_inc(var_ready, 1)
                dve.wait_ge(rstd_ready, b + 1)
                link(dve.scalar_tensor_tensor(nbias[:, :], mv[:, :, 0], -1.0, rstd[:, :], ALU.mult, ALU.mult))
                if b >= 2:
                    dve.wait_ge(xT_done, b - 1)
                for t in range(TB):
                    last = dve.tensor_scalar(xn[:, b % 2, t, :], x_sb[:, b * TB + t, :],
                                             rstd[:, t:t + 1], nbias[:, t:t + 1], ALU.mult, ALU.add)
                last.then_inc(xn_ready, 1)

            layer_norm(0)
            dve.wait_ge(modrow_done, 1)
            link(dve.tensor_copy(mod_r[:, :], ps[0:B, 4:7, :].rearrange("b k n -> b (k n)")))
            rows = mod_r[:, :].rearrange("b (a s n) -> b a s n", a=2, s=3)
            link(dve.tensor_scalar(rows[:, :, 1, :], rows[:, :, 1, :], 1.0, None, ALU.add))
            gates = rows[:, :, 2, :]
            link(dve.tensor_scalar(sgn[:, :, :], gates, 0.0, 2.0, ALU.is_ge, ALU.mult))
            link(dve.tensor_scalar(sgn[:, :, :], sgn[:, :, :], -1.0, None, ALU.add))
            link(dve.scalar_tensor_tensor(gates, gates, -1.0, gates, ALU.mult, ALU.max))
            dve.scalar_tensor_tensor(gates, gates, 0.25, sgn[:, :, :], ALU.max, ALU.mult).then_inc(modrow_ready, 1)
            dve.wait_ge(modT_done, 1)
            dve.tensor_copy(modT[:, :, :], ps[:, 7, 0:4 * B].rearrange("p (c b) -> p c b", b=B)).then_inc(modT_ready, 1)
            layer_norm(1)

            def low_piece(n):
                dve.wait_ge(mid_ready, n + 1)
                dve.tensor_tensor(pieces[:, n % 4, 2, :], rest[:, n % 2, :], pieces[:, n % 4, 1, :],
                                  ALU.subtract).then_inc(lo_ready, 1)

            for b in range(B):
                for m in range(4):
                    n = 4 * b + m
                    dve.wait_ge(hi_ready, n + 1)
                    if n >= 2:
                        dve.wait_ge(lo_ready, n - 1)
                    dve.scalar_tensor_tensor(rest[:, n % 2, :], ps[:, 2 + m, :], HN ** -0.5 if m < 2 else 1.0,
                                             pieces[:, m, 0, :], ALU.mult, ALU.subtract).then_inc(rest_ready, 1)
                    if n >= 1:
                        low_piece(n - 1)
                if b + 2 < B:
                    layer_norm(b + 2)
            low_piece(4 * B - 1)

            def reduce(j, s, par2):
                dve.wait_ge(s_ready, 16 * j + s + 1)
                dve.reduce_max(negm[:, par2, s:s + 1], ps[:, S_BANK + s % 2, :], AX, negate=True).then_inc(s_reduced, 1)

            for j in range(2):
                for s in range(16):
                    reduce(j, s, j)

            def quad(it, u):
                j = 4 * it + u + 2
                dve.wait_ge(m_split, j - 1)
                for s in range(16):
                    reduce(j, s, u % 2)

            with dve.Fori(0, 3) as it:
                for u in range(4):
                    quad(it, u)
            for u in range(2):
                quad(3, u)

            for b in range(B):
                dve.wait_ge(ctx_loaded[b], 64)
                link(dve.reciprocal(sums[:, :, b, :], sums[:, :, b, :]))
                dve.tensor_tensor(ctx_n[:, :, b, :], ctx_n[:, :, b, :], sums[:, :, b, :], ALU.mult)\
                   .then_inc(ctx_ready, 1)

            def over(v, n):
                return v.unsqueeze(2).to_broadcast([P, v.shape[1], n])

            dve.wait_ge(const_ready, 4)
            link(dve.tensor_copy(start, seg_0[:, :]))
            for b in range(B):
                tiles = slice(b * TB, (b + 1) * TB)
                for t in range(TB):
                    dve.wait_ge(x1_ready, b * TB + t + 1)
                    last = dve.bn_stats(st2[:, t, :], x_sb[:, b * TB + t, :])
                link(last)
                for t in range(TB):
                    last = dve.bn_aggr(mv2[:, t, :], st2[:, t, :])
                last.then_inc(var2_ready, 1)
                dve.wait_ge(rstd2_ready, b + 1)
                dve.scalar_tensor_tensor(nbias2, mv2[:, :, 0], -1.0, rstd2, ALU.mult, ALU.mult).then_inc(nbias2_ready, 1)
                dve.wait_ge(normed2, b + 1)
                link(dve.tensor_tensor(h2[:, tiles, :], h2[:, tiles, :], mod_b[:, 2, b, :].unsqueeze(1).to_broadcast([P, TB, H]), ALU.mult))
                dve.tensor_tensor(h2[:, tiles, :], h2[:, tiles, :], mod_b[:, 1, b, :].unsqueeze(1).to_broadcast([P, TB, H]), ALU.add)\
                   .then_inc(h2_ready, 1)
                dve.wait_ge(logit_done, TB * (b + 1))
                dve.wait_ge(rrms_ready, b + 1)
                ins = dve.tensor_tensor(logit, ps[:, 4 + b % 2, 0:TB * E].rearrange("p (t e) -> p t e", t=TB),
                                        over(rrms[:, tiles], E), ALU.mult)
                link(ins)
                one = logit.unsqueeze(3).to_broadcast([P, TB, E, E])
                other = logit.unsqueeze(2).to_broadcast([P, TB, E, E])
                dve.tensor_tensor(above, other, one, ALU.is_gt)
                dve.tensor_tensor(equal, other, one, ALU.is_equal)
                link(dve.reduce_max(top, logit, AX))
                dve.tensor_tensor(equal, equal, earlier[:, :].rearrange("p (a b) -> p a b", a=E).unsqueeze(1).to_broadcast([P, TB, E, E]), ALU.mult)
                link(dve.tensor_tensor(logit, logit, over(top, E), ALU.subtract))
                dve.sem_inc(d_ready, 1) if False else None
                dve.tensor_tensor(above, above, equal, ALU.add).then_inc(d_ready, 1)
                dve.wait_ge(d_ready, b + 1)
                link(dve.reduce_sum(count, above, AX))
                dve.tensor_scalar(chosen, count, 2.0, None, ALU.is_lt).then_inc(chosen_ready, 1)
                dve.wait_ge(e_ready, b + 1)
                link(dve.reduce_sum(total, prob, AX))
                link(dve.reciprocal(total, total))
                link(dve.tensor_tensor(prob, prob, over(total, E), ALU.mult))
                dve.wait_ge(chosen_ready, b + 1)
                link(dve.tensor_tensor(prob, prob, chosen, ALU.mult))
                link(dve.reduce_sum(total, prob, AX))
                link(dve.tensor_scalar(guard, total, 0.0, None, ALU.is_le))
                link(dve.tensor_tensor(total, total, guard, ALU.max))
                link(dve.reciprocal(total, total))
                link(dve.tensor_tensor(prob, prob, over(total, E), ALU.mult))
                link(dve.tensor_tensor(prob, prob, e_scale[:, :].unsqueeze(1).to_broadcast([P, TB, E]), ALU.mult))
                dve.wait_ge(counted, b + 1)
                link(dve.tensor_copy(totals, ps[:, 7, 0:TB * E].rearrange("p (t e) -> p e t", t=TB)))
                link(dve.tensor_tensor(totals[:, :, 0], totals[:, :, 0], start, ALU.add))
                link(dve.tensor_tensor_scan(upto.rearrange("p e t -> p (e t)"), after_0[:, :], totals.rearrange("p e t -> p (e t)"),
                                            0.0, ALU.mult, ALU.add))
                dve.tensor_copy(start, upto[:, :, TB - 1])
                link(dve.tensor_tensor(place, ps[:, 6, 0:TB * E].rearrange("p (t e) -> p t e", t=TB),
                                       upto.rearrange("p e t -> p t e"), ALU.add))
                for c, by, best in ((0, 1.0, ALU.max), (1, -BIG, ALU.min)):
                    link(dve.scalar_tensor_tensor(mark, place, by, chosen, ALU.add, ALU.mult))
                    link(dve.tensor_reduce(slot_f[:, c, tiles], mark, AX, best))
                    dve.tensor_scalar(slot_i[:, c, tiles], slot_f[:, c, tiles], -by, None, ALU.add)
                    link(dve.tensor_tensor(hit, mark, over(slot_f[:, c, tiles], E), ALU.is_equal))
                    dve.tensor_copy(hits[:, c, tiles, :], hit)
                    link(dve.tensor_tensor(hit, hit, prob, ALU.mult))
                    last = dve.reduce_sum(slot_w[:, c, tiles], hit, AX)
                    link(last) if c == 0 else last.then_inc(slot_ready, 1)
                dve.wait_ge(slot_ready, b + 1)

            dve.tensor_copy(run_i[:, :], start[0:1, :])
            link(dve.tensor_tensor(filled[:, :], start, seg_0[:, :], ALU.subtract))
            fits = above.rearrange("p t a b -> p (t a b)")[:, 0:E * 16].rearrange("p (e m) -> p e m", e=E)
            link(dve.tensor_tensor(fits, over(filled[:, :], 16), m_rows[:, :].rearrange("p (e m) -> p e m", e=E), ALU.is_gt))
            link(dve.reduce_sum(filled[:, :], fits, AX))
            link(dve.tensor_tensor_scan(ends[:, :], ones[:, 0:E], filled[:, :], 0.0, ALU.mult, ALU.add))
            link(dve.tensor_tensor(firsts[:, :], ends[:, :], filled[:, :], ALU.subtract))
            tau, number, mine, use, row = (v.rearrange("o (t e) -> o t e", e=E)
                                           for v in (tab[:, 0, :], tab[:, 1, :], work[:, 0, :], work[:, 1, :], work[:, 2, :]))

            def all_tiles(v):
                return v[0:1, :].unsqueeze(1).to_broadcast([1, 40, E])

            dve.tensor_tensor(mine, tau, all_tiles(firsts), ALU.is_ge)
            dve.tensor_tensor(use, tau, all_tiles(ends), ALU.is_lt)
            link(dve.scalar_tensor_tensor(shift[:, :], firsts[:, :], -float(P), seg_0[:, :], ALU.mult, ALU.add))
            spare = float(DUMMY - FULL * P)
            link(dve.tensor_tensor(mine, mine, use, ALU.mult))
            dve.tensor_tensor(use, mine, number, ALU.mult)
            link(dve.scalar_tensor_tensor(row, all_tiles(shift), -spare, mine, ALU.add, ALU.mult))
            dve.reduce_sum(tab_f[:, 0:40], row, AX)
            link(dve.reduce_sum(tab_f[:, 40:80], use, AX))
            link(dve.scalar_tensor_tensor(tab_f[:, 0:40], tau[:, :, 0], float(P), tab_f[:, 0:40], ALU.mult, ALU.add))
            dve.tensor_scalar(tab_i[:, 0:40], tab_f[:, 0:40], spare, None, ALU.add)
            dve.tensor_copy(tab_i[:, 40:80], tab_f[:, 40:80]).then_inc(tab_ready, 1)

            def rows_made():
                for c, over_by in ((0, 1.0), (1, -BIG)):
                    link(dve.tensor_tensor(hits[:, c], hits[:, c], shift[:, :].unsqueeze(1).to_broadcast([P, NT, E]), ALU.mult))
                    link(dve.reduce_sum(row_shift[:, :], hits[:, c], AX))
                    link(dve.tensor_tensor(slot_f[:, c, :], slot_f[:, c, :], row_shift[:, :], ALU.subtract))
                    last = dve.tensor_scalar(slot_b[:, c, :], slot_f[:, c, :], -over_by, None, ALU.add)
                last.then_inc(rows_ready, 1)

            def take_actsT(t):
                dve.wait_ge(acts_turned, t + 1)
                dve.tensor_copy(actsT[:, :, :], ps[:, 1, 0:H].rearrange("p (k x) -> p k x", k=KC)).then_inc(actsT_ready, 1)

            def do_acts(t, u):
                dve.wait_ge(gelu_ready, t + 1)
                dve.tensor_tensor(acts[:, u, :], ps[:, 2 + u, H:2 * H], gelu[:, u, :], ALU.mult).then_inc(acts_ready, 1)

            do_acts(0, 0)
            rows_made()
            with dve.Fori(0, CAP // 2) as it:
                for u in range(2):
                    t = 2 * it + u
                    take_actsT(t)
                    do_acts(t + 1, 1 - u)
            take_actsT(CAP - 1)

            for n in range(NT):
                dve.wait_ge(back_loaded[n % 8], 32 * (n // 8 + 1))
                b0, b1 = back[:, n % 8, 0, :], back[:, n % 8, 1, :]
                link(dve.tensor_scalar(b0, b0, slot_w[:, 0, n:n + 1], None, ALU.mult))
                link(dve.scalar_tensor_tensor(b1, b1, slot_w[:, 1, n:n + 1], b0, ALU.mult, ALU.add))
                link(dve.tensor_tensor(b1, b1, mod_b[:, 3, n // TB, :], ALU.mult))
                dve.tensor_tensor(x_sb[:, n, :], x_sb[:, n, :], b1, ALU.add).then_inc(out_ready, 1)

        @block.tensor
        def _(pe):
            pe.wait_ge(ident_ready, 1)
            pe.wait_ge(w_loaded, 160)
            for s in range(3):
                for k in range(KC):
                    for half in range(2):
                        last = pe.transpose(ps[:, s, (2 * k + half) * P:(2 * k + half + 1) * P],
                                            w_raw[:, 2 * s + half, k * P:(k + 1) * P], ident[:, :])
                last.then_inc(wT_done, 1)
            pe.wait_ge(wp_loaded, 16)
            for k in range(KC):
                for half in range(2):
                    last = pe.transpose(ps[:, 3, (2 * k + half) * P:(2 * k + half + 1) * P],
                                        wp_raw[:, half, k * P:(k + 1) * P], ident[:, :])
            last.then_inc(wT_done, 1)
            pe.wait_ge(silu_ready, 1)
            for n in range(3):
                for k in range(KC):
                    last = pe.matmul(ps[0:B, 4 + n, :], sig[:, k, :], wmod[:, k, n * 512:(n + 1) * 512],
                                     start=k == 0, stop=k == KC - 1)
            last.then_inc(modrow_done, 1)
            pe.wait_ge(modrow_ready, 1)
            for c in range(4):
                last = pe.transpose(ps[:, 7, c * B:(c + 1) * B], mod_r[:, c * P:(c + 1) * P], ident[0:B, 0:B])
            last.then_inc(modT_done, 1)

            def turn_x(b):
                pe.wait_ge(xn_ready, b + 1)
                if b == 0:
                    pe.wait_ge(wT_evac, 4)
                else:
                    pe.wait_ge(hT_ready, b)
                for k in range(KC):
                    for t in range(TB):
                        last = pe.transpose(ps[:, k, t * P:(t + 1) * P], xn[:, b % 2, t, k * P:(k + 1) * P], ident[:, :])
                last.then_inc(xT_done, 1)

            turn_x(0)
            pe.wait_ge(modT_ready, 1)
            for b in range(B):
                pe.wait_ge(hT_ready, b + 1)
                for m in range(4):
                    if b >= 1:
                        pe.wait_ge(rest_ready, 4 * (b - 1) + m + 1)
                    if b == 2:
                        pe.wait_ge(gate_evac, 3 + m // 2)
                    for k in range(KC):
                        last = pe.matmul(ps[:, 2 + m, :], w_T[:, k, m * P:(m + 1) * P], hT[:, b % 2, k, :],
                                         start=k == 0, stop=k == KC - 1)
                    last.then_inc(qk_done, 1)
                if b + 1 < B:
                    turn_x(b + 1)
                for hf in range(2):
                    if b >= 1:
                        pe.wait_ge(v_evac, 2 * (b - 1) + hf + 1)
                    for tt in range(2):
                        t = 2 * hf + tt
                        for k in range(KC):
                            last = pe.matmul(ps[:, 6 + hf, tt * H:(tt + 1) * H], hT[:, b % 2, k, t * P:(t + 1) * P],
                                             w_T[:, k, 2 * H:3 * H], start=k == 0, stop=k == KC - 1)
                    last.then_inc(v_done, 1)
                if b % 2:
                    pe.wait_ge(rest_ready, 4 * (b + 1))
                    pe.wait_ge(gate_loaded, 64 * (b + 1) // 2)
                    for e in range(2 * (b - 1), 2 * (b + 1)):
                        if e % 4 >= 2:
                            pe.wait_ge(gate_evac, e - 1)
                        for k in range(KC):
                            for c in range(4):
                                last = pe.transpose(ps[:, 2 + 2 * (e % 2) + k, c * P:(c + 1) * P],
                                                    gate_raw[:, e % 4, c, k * P:(k + 1) * P], ident[:, :])
                        last.then_inc(gate_turned, 1)

            def s_tile(j, s, par, first=False):
                g, t = s // 4, s % 4
                if not (first and s < 2):
                    pe.wait_ge(s_reduced, 16 * j + s - 1)
                pe.matmul(ps[:, S_BANK + s % 2, :], qst[0:PR, par, g * SQ + t * P:g * SQ + (t + 1) * P],
                          kst[0:PR, par, g * SQ:(g + 1) * SQ], start=True, stop=True).then_inc(s_ready, 1)

            def st_pair(i, kt, pair, par, first=False):
                if not first:
                    pe.wait_ge(exp_done, 8 * i + 2 * kt + pair - 1)
                for n in range(2):
                    g = 2 * pair + n
                    last = pe.matmul(ps[:, ST_BANK + g, :], kst[0:PR + MR, par, g * SQ + kt * P:g * SQ + (kt + 1) * P],
                                     qst[0:PR + MR, par, g * SQ:(g + 1) * SQ], start=True, stop=True)
                last.then_inc(st_ready, 1)

            def pv(i, kt, par2):
                pe.wait_ge(exp_done, 8 * i + 2 * kt + 2)
                for g in range(4):
                    last = pe.matmul(ps[32 * g:32 * g + 32, PV_BANK, :], v_st[:, par2, kt * P + 32 * g:kt * P + 32 * g + 32],
                                     probs[:, kt % 2, g * SQ:(g + 1) * SQ], start=kt == 0, stop=kt == 3)
                last.then_inc(pv_done, 1)

            def turn_m(j, par2):
                pe.wait_ge(m_split, j + 1)
                pe.transpose(m_ps, mpc[:, par2, :], identb[:, :]).then_inc(m_turned, 1)

            pe.wait_ge(rest_ready, 4 * B)
            pe.wait_ge(v_evac, 2 * B)
            pe.wait_ge(ident_ready, 2)
            for j in range(2):
                pe.wait_ge(stack_loaded[j], 96)
                for s in range(16):
                    s_tile(j, s, j, first=j == 0)
            turn_m(0, 0)
            pe.wait_ge(v_init, 2)
            pe.wait_ge(mrow_loaded[0], 16)
            st_pair(0, 0, 0, 0, True)
            st_pair(0, 0, 1, 0, True)

            def quad(it, u, more):
                i = 4 * it + u
                ahead = more or u < 2
                if ahead:
                    pe.wait_ge(stack_loaded[(u + 2) % 4], 96 * (it + 1 + (u + 2) // 4))
                for k in range(4):
                    here = k < 3
                    nxt = here or more or u < 3
                    if not here and nxt:
                        pe.wait_ge(mrow_loaded[(u + 1) % 4], 16 * (it + 1 + (u + 1) // 4))
                    args = (i, k + 1, u) if here else (i + 1, 0, (u + 1) % 4)
                    if ahead:
                        s_tile(i + 2, 4 * k, (u + 2) % 4)
                    if nxt:
                        st_pair(args[0], args[1], 0, args[2])
                    if ahead:
                        s_tile(i + 2, 4 * k + 1, (u + 2) % 4)
                    if k == 0:
                        pe.wait_ge(v_staged, i + 1)
                        pe.wait_ge(ctx_evac, ONE + i)
                    pv(i, k, u % 2)
                    if ahead:
                        s_tile(i + 2, 4 * k + 2, (u + 2) % 4)
                    if nxt:
                        st_pair(args[0], args[1], 1, args[2])
                    if ahead:
                        s_tile(i + 2, 4 * k + 3, (u + 2) % 4)
                    if k == 1 and (more or u < 3):
                        pe.wait_ge(m_evac, i + 1)
                        turn_m(i + 1, (u + 1) % 2)

            with pe.Fori(0, 3) as it:
                for u in range(4):
                    quad(it, u, True)
            for u in range(4):
                quad(3, u, False)

            def project(b):
                pe.wait_ge(ctx_ready, b + 1)
                for t in range(TB):
                    n = b * TB + t
                    if n >= 2:
                        pe.wait_ge(x1_ready, n - 1)
                    for k in range(KC):
                        pe.matmul(ps[:, n % 2, 0:H], ctx_n[:, k, b, t * P:(t + 1) * P], wp_g[:, b, k, :],
                                  start=k == 0, stop=False)
                    pe.matmul(ps[:, n % 2, 0:H], ident[:, :], x_sb[:, n, :], start=False, stop=True).then_inc(proj_done, 1)

            pe.wait_ge(exp_done, 8 * NQ)
            pe.wait_ge(s_reduced, 16 * NQ)
            pe.wait_ge(m_evac, NQ)
            pe.wait_ge(ctx_evac, ONE + NQ)
            pe.wait_ge(xb_ready, B)
            pe.wait_ge(wpg_ready, B)
            pe.wait_ge(const_ready, 4)
            pe.wait_ge(rw_ready, 1)
            project(0)
            for b in range(B):
                if b + 1 < B:
                    project(b + 1)
                pe.wait_ge(h2_ready, b + 1)
                for t in range(TB):
                    n = b * TB + t
                    if n >= 2:
                        pe.wait_ge(h2T_ready, n - 1)
                    for k in range(KC):
                        last = pe.transpose(ps[:, 2 + n % 2, k * P:(k + 1) * P], h2[:, n, k * P:(k + 1) * P], ident[:, :])
                    last.then_inc(h2_turned, 1)
                if b >= 2:
                    pe.wait_ge(chosen_ready, b - 1)
                for t in range(TB):
                    n = b * TB + t
                    pe.wait_ge(h2T_ready, n + 1)
                    for k in range(KC):
                        last = pe.matmul(ps[:, 4 + b % 2, t * E:(t + 1) * E], h2T[:, n % 4, k, :], r_w[:, k, :],
                                         start=k == 0, stop=k == KC - 1)
                    last.then_inc(logit_done, 1)
                pe.wait_ge(chosen_ready, b + 1)
                if b >= 1:
                    pe.wait_ge(slot_ready, b)
                flat = chosen.rearrange("p t e -> p (t e)")
                pe.matmul(ps[:, 6, 0:TB * E], minus_geq[:, :], flat, start=True, stop=True)
                pe.matmul(ps[:, 7, 0:TB * E], ones[:, :], flat, start=True, stop=True).then_inc(counted, 1)

            def turn_slots(t, u, before):
                pe.wait_ge(xs_loaded[u], 16 * (before + 1))
                if isinstance(t, int) and t == 0:
                    pe.wait_ge(x1_ready, NT)
                else:
                    pe.wait_ge(xsT_ready, t)
                for k in range(KC):
                    last = pe.transpose(ps[:, 0, k * P:(k + 1) * P], xs[:, u, k * P:(k + 1) * P], ident[:, :])
                last.then_inc(xs_turned, 1)

            def expert(t):
                return pe.value_load(tab_i[0:1, bass.ds(t + 40, 1)], min_val=0, max_val=E - 1)

            def gate(t, u, e):
                pe.wait_ge(xsT_ready, t + 1)
                if isinstance(t, int) and t == 0:
                    pe.wait_ge(h2T_ready, NT)
                for k in range(KC):
                    last = pe.matmul(ps[:, 2 + u, :], xsT[:, u, k, :], gate_T[:, bass.ds(e, 1), k, :].rearrange("p o n -> p (o n)"),
                                     start=k == 0, stop=k == KC - 1)
                last.then_inc(gate_done, 1)

            def turn_acts(t, u):
                pe.wait_ge(acts_ready, t + 1)
                for k in range(KC):
                    last = pe.transpose(ps[:, 1, k * P:(k + 1) * P], acts[:, u, k * P:(k + 1) * P], ident[:, :])
                last.then_inc(acts_turned, 1)

            def down(t, e):
                pe.wait_ge(actsT_ready, t + 1)
                for k in range(KC):
                    last = pe.matmul(ps[:, 4, 0:H], actsT[:, k, :], lin[:, bass.ds(e, 1), k, :].rearrange("p o n -> p (o n)"),
                                     start=k == 0, stop=k == KC - 1)
                last.then_inc(down_done, 1)

            pe.wait_ge(tab_ready, 1)
            pe.wait_ge(lin_loaded, 16)
            turn_slots(0, 0, 0)
            gate(0, 0, expert(0))
            with pe.Fori(0, CAP // 2) as it:
                for u in range(2):
                    t = 2 * it + u
                    turn_slots(t + 1, 1 - u, it + u)
                    turn_acts(t, u)
                    gate(t + 1, 1 - u, expert(t + 1))
                    down(t, expert(t))
            turn_acts(CAP - 1, 0)
            pe.wait_ge(made_ready, CAP - 1)
            down(CAP - 1, expert(CAP - 1))


_INS = ["L0_attn_query", "L0_attn_Wqkv", "L0_attn_Wproj", "L0_attn_bproj", "L0_ffn_router_logits",
        "L0_ffn_gating_einsum", "L0_ffn_linear", "L0_ffn_per_expert_scale", "L0_ffn_router_scale", "L0_c", "L0_wmod"]
_OUTS = [((B, SQ, H), "float32")]


def kernel(**inputs):
    import numpy as _np
    import concourse.bacc as _bacc
    from concourse import mybir as _mybir
    from concourse.bass_utils import run_bass_kernel_spmd as _run

    nc = _bacc.Bacc("TRN2", target_bir_lowering=False, num_devices=1)
    arrays, args = {}, []
    for name in _INS:
        a = _np.ascontiguousarray(inputs[name])
        arrays[f"in_{name}_dram"] = a
        args.append(nc.dram_tensor(f"in_{name}_dram", a.shape, _mybir.dt.from_np(a.dtype), kind="ExternalInput").ap())
    for i, (shape, dtype) in enumerate(_OUTS):
        dt = _mybir.dt.from_np(_np.dtype(dtype))
        args.append(nc.dram_tensor(f"out_{i}_dram", shape, dt, kind="ExternalOutput").ap())
    adaln_block(nc, *args)
    r = _run(nc, [arrays], core_ids=[0])
    got = tuple(r.results[0][f"out_{i}_dram"] for i in range(len(_OUTS)))
    return got[0]
```

```python
from contextlib import ExitStack

import concourse.bass as bass
from concourse import mybir

F32 = mybir.dt.float32
BF16 = mybir.dt.bfloat16
U32 = mybir.dt.uint32
I32 = mybir.dt.int32
ACT = mybir.ActivationFunctionType
ALU = mybir.AluOpType
AX = mybir.AxisListType.X

P = 128
B, SQ, H = 4, 512, 256
NH, HN = 16, 16
TB = SQ // P
NT = B * TB
KC = H // P
NQ = B * NH // 4
PR = 6 * HN
MR = 3
E = 8
CAP = (B * SQ * 2 + E * (P - 1)) // P
SEG = B * SQ + P
FULL = B * SQ * 2 // P
DUMMY = E * SEG
ROWS = DUMMY + (CAP - FULL) * P
ONE = 1
BIG = 32768.0
EPS_LN, EPS_RMS = 1e-5, 1e-6
EARLY = NQ - 2
NG = 2
GT = NT // NG
SA, CA, GA, SB, CB, GB = range(6)


def adaln_block(nc, query, w_qkv, w_proj, b_proj, router_w, gating, linear,
                expert_scale, router_scale, cond, w_mod, out):
    ctx = ExitStack()
    with ctx:
        def sb(name, shape, dt=F32):
            return ctx.enter_context(nc.sbuf_tensor(name, shape, dt))

        def sem(name):
            return ctx.enter_context(nc.semaphore(name))

        def dram(name, shape, dt=F32):
            return nc.dram_tensor(name, shape, dt, kind="Internal").ap()

        qk_d = dram("qk_d", [2, NQ, 3, 64, SQ], BF16)
        ctx_d = dram("ctx_d", [EARLY, P, SQ])
        inv_d = dram("inv_d", [EARLY, B, SQ])
        mod_d = dram("mod_d", [B, 6 * H])
        slots_d = dram("slots_d", [ROWS, H])
        made_d = dram("made_d", [CAP * P, H])

        ident = sb("ident", [P, P])
        minus_half = sb("minus_half", [P, 16])
        identb = sb("identb", [P, P], BF16)
        x_sb = sb("x_sb", [P, NT, H])
        w_T = sb("w_T", [P, KC, 3 * H])
        wp_T = sb("wp_T", [P, KC, H])
        lin = sb("lin", [P, E, KC, H])
        lin_flat = lin[:, :, :, :].rearrange("p e k n -> p (e k n)")
        wmod = lin_flat[:, 0:12 * H].rearrange("p (k n) -> p k n", k=KC)
        wp_raw = lin_flat[:, 12 * H:14 * H].rearrange("p (k n) -> p k n", k=KC)
        gate_T = sb("gate_T", [P, E, KC, 2 * H])
        cT = sb("cT", [P, KC, B])
        sig = sb("sig", [P, KC, B])
        area = sb("area", [P, 8 * H])
        mod_r = area[0:B, 0:6 * H]
        sgn = sb("sgn", [B, 2, H])
        modT = sb("modT", [P, 4, B])
        mod_b = sb("mod_b", [P, 4, B, H])
        mod_flat = mod_b[:, :, :, :].rearrange("p r b n -> p (r b n)")
        bp_b = sb("bp_b", [P, H])
        st = sb("st", [P, TB, 6])
        mv = sb("mv", [P, TB, 2])
        rstd = sb("rstd", [P, TB])
        nbias = sb("nbias", [P, TB])
        xn = mod_flat[:, 0:8 * H].rearrange("p (n t h) -> p n t h", n=2, t=TB)
        hT = mod_flat[:, 8 * H:16 * H].rearrange("p (n k x) -> p n k x", n=2, k=KC)
        space = sb("space", [P, 12 * H])
        w_raw = space[:, 0:6 * H].rearrange("p (s n) -> p s n", s=6)
        pieces = space[:, :].bitcast(BF16).rearrange("p (m c x) -> p m c x", m=4, c=3)
        wp_g = space[:, 0:8 * H].rearrange("p (b k n) -> p b k n", b=B, k=KC)
        rest = sb("rest", [P, 2, SQ])
        sum_rows, inv_rows = rest[0:EARLY * B, 0, :], rest[0:EARLY * B, 1, :]
        bias_row = space[:, 8 * H:9 * H]
        inv_o = space[:, 8 * H:12 * H].rearrange("p (n x) -> p n x", n=2)
        v_all = sb("v_all", [P, NQ, TB, P])
        v_st = area[:, 0:4 * H].rearrange("p (n x) -> p n x", n=2)
        qst = sb("qst", [P, 4, 4 * SQ], BF16)
        kst = sb("kst", [P, 4, 4 * SQ], BF16)
        negm = sb("negm", [P, 2, 16])
        mrest = sb("mrest", [P, 2, 16])
        mpc = sb("mpc", [P, 2, P], BF16)
        m_T = sb("m_T", [48, 2, P], BF16)
        probs = sb("probs", [P, 2, 4 * SQ])
        gate_raw = probs[:, :, :].rearrange("p n x -> p (n x)").rearrange("p (e c f) -> p e c f", e=4, c=4)
        h2 = qst[:, :, :].rearrange("p n x -> p (n x)").bitcast(F32).rearrange("p (n h) -> p n h", n=NT)
        ctx_o = area[:, 4 * H:8 * H].rearrange("p (n x) -> p n x", n=2)
        v_flat = v_all[:, :, :, :].rearrange("p q t c -> p (q t c)")
        ctx_n = v_flat[:, 0:KC * B * SQ].rearrange("p (k b x) -> p k b x", k=KC, b=B)
        inv_0 = v_flat[:, KC * B * SQ:(KC + 1) * B * SQ].rearrange("p (b x) -> p b x", b=B)
        ranks = v_flat[:, (KC + 1) * B * SQ:(KC + 1) * B * SQ + 2 * GT * E * E].rearrange(
            "p (n t a b) -> p n t a b", n=2, t=GT, a=E)

        late = kst[:, :, :].rearrange("p n x -> p (n x)").bitcast(F32)
        inv_1 = late[:, 0:B * SQ].rearrange("p (b x) -> p b x", b=B)
        h2T = late[:, 0:4 * H].rearrange("p (n k x) -> p n k x", n=4, k=KC)
        squares = late[:, 4 * H:5 * H]
        xs = late[:, 5 * H:7 * H].rearrange("p (n h) -> p n h", n=2)
        xsT = late[:, 7 * H:9 * H].rearrange("p (n k x) -> p n k x", n=2, k=KC)
        gelu = late[:, 9 * H:11 * H].rearrange("p (n h) -> p n h", n=2)
        acts = late[:, 11 * H:13 * H].rearrange("p (n h) -> p n h", n=2)
        actsT = late[:, 13 * H:14 * H].rearrange("p (k x) -> p k x", k=KC)
        made = late[:, 14 * H:16 * H].rearrange("p (n h) -> p n h", n=2)
        back = probs[:, :, :].rearrange("p n x -> p (n x)").rearrange("p (n c h) -> p n c h", n=8, c=2)
        taken = [0]

        def small(*shape, dt=F32):
            n = 1
            for d in shape:
                n *= d
            v = area[:, taken[0]:taken[0] + n]
            taken[0] += n
            assert taken[0] <= 8 * H
            v = v if dt == F32 else v.bitcast(dt)
            if len(shape) == 2:
                v = v.rearrange("p (a b) -> p a b", a=shape[0])
            if len(shape) == 3:
                v = v.rearrange("p (a b c) -> p a b c", a=shape[0], b=shape[1])
            return v

        st2, mv2 = small(NT, 6), small(NT, 2)
        rstd2, nbias2 = small(NT), small(NT)
        ssq, rrms = small(NT), small(NT)
        logit, prob, chosen = small(NT, E), small(NT, E), small(NT, E)
        top, total, picked = small(NT), small(NT), small(NT)
        count, totals, upto, place = small(GT, E), small(E, GT), small(E, GT), small(GT, E)
        before = small(E, GT)
        start = before[:, :, 0]
        marks, hits = small(2, NT, E), small(2, NT, E)
        slot_b = small(2, NT, dt=U32)
        slot_f, slot_w = small(2, NT), small(2, NT)
        slot_i = small(2, NT, dt=U32)
        above, equal = ranks[:, 0], ranks[:, 1]
        earlier = sb("earlier", [P, E * E])
        after_0 = sb("after_0", [P, E * GT])
        minus_geq = sb("minus_geq", [P, P])
        ones = sb("ones", [P, P])
        seg_0 = sb("seg_0", [P, E])
        zeros = sb("zeros", [P, H])
        tab = sb("tab", [1, 2, 40 * E])
        m_rows = sb("m_rows", [P, E * 16])
        work = v_flat[0:1, 0:3 * 40 * E].rearrange("o (a b) -> o a b", a=3)
        ends, firsts, filled, shift = (sb(n, [P, E]) for n in ("ends", "firsts", "filled", "shift"))
        tab_f = sb("tab_f", [1, 2 * 40])
        row_shift = sb("row_shift", [P, 2, NT])
        tab_i = sb("tab_i", [1, 2 * 40], I32)
        run_i = sb("run_i", [1, E], I32)
        r_w = sb("r_w", [P, KC, E])
        r_scale = sb("r_scale", [P, KC])
        e_scale = sb("e_scale", [P, E])

        ps = ctx.enter_context(nc.psum_tensor("ps", [P, 8, 512], F32))

        x_loaded = [sem(f"x_loaded{b}") for b in range(B)]
        w_loaded = sem("w_loaded")
        wp_loaded = sem("wp_loaded")
        mod_loaded = sem("mod_loaded")
        bp_loaded = sem("bp_loaded")
        pool_step = sem("pool_step")
        ident_ready = sem("ident_ready")
        v_init = sem("v_init")
        sig_exp = sem("sig_exp")
        silu_ready = sem("silu_ready")
        dve_chain = sem("dve_chain")
        wT_done = sem("wT_done")
        wT_evac = sem("wT_evac")
        modrow_done = sem("modrow_done")
        modrow_ready = sem("modrow_ready")
        modT_done = sem("modT_done")
        modT_ready = sem("modT_ready")
        mod_stored = sem("mod_stored")
        modb_loaded = sem("modb_loaded")
        var_ready = sem("var_ready")
        var_eps = sem("var_eps")
        rstd_ready = sem("rstd_ready")
        xn_ready = sem("xn_ready")
        xT_done = sem("xT_done")
        hT_ready = sem("hT_ready")
        qk_done = sem("qk_done")
        hi_ready = sem("hi_ready")
        rest_ready = sem("rest_ready")
        mid_ready = sem("mid_ready")
        lo_ready = sem("lo_ready")
        qk_stored = [sem(f"qk_stored{n}") for n in range(4)]
        v_done = sem("v_done")
        v_evac = sem("v_evac")
        stack_loaded = [sem(f"stack_loaded{n}") for n in range(4)]
        mrow_loaded = [sem(f"mrow_loaded{n}") for n in range(4)]
        s_ready = sem("s_ready")
        s_reduced = sem("s_reduced")
        split1, split2, split3, m_split = (sem(n) for n in ("split1", "split2", "split3", "m_split"))
        m_turned = sem("m_turned")
        m_evac = sem("m_evac")
        st_ready = sem("st_ready")
        exp_done = sem("exp_done")
        v_staged = sem("v_staged")
        pv_done = sem("pv_done")
        ctx_evac = sem("ctx_evac")
        ctx_stored = [sem(f"ctx_stored{n}") for n in range(2)]
        ctx_loaded = [sem(f"ctx_loaded{k}") for k in range(KC)]
        sums_loaded, inverse_ready, inverse_stored, half_ready = (
            sem(n) for n in ("sums_loaded", "inverse_ready", "inverse_stored", "half_ready"))
        ctx_ready = sem("ctx_ready")
        proj_done = sem("proj_done")
        x1_ready = sem("x1_ready")
        xb_ready = sem("xb_ready")
        out_stored = sem("out_stored")
        gate_loaded = sem("gate_loaded")
        gate_turned = sem("gate_turned")
        gate_evac = sem("gate_evac")
        lin_loaded = sem("lin_loaded")
        router_loaded = sem("router_loaded")
        rw_ready = sem("rw_ready")
        const_ready = sem("const_ready")
        wpg_ready = sem("wpg_ready")
        var2_ready, var2_eps, rstd2_ready, nbias2_ready = (sem(n) for n in ("var2_ready", "var2_eps", "rstd2_ready", "nbias2_ready"))
        normed2 = sem("normed2")
        h2_ready = sem("h2_ready")
        ssq_ready, ssq_eps, rrms_ready = (sem(n) for n in ("ssq_ready", "ssq_eps", "rrms_ready"))
        h2_turned, h2T_ready, logit_done, logit_read = (sem(n) for n in ("h2_turned", "h2T_ready", "logit_done", "logit_read"))
        d_ready, e_ready = sem("d_ready"), sem("e_ready")
        chosen_ready, counted, slot_ready = sem("chosen_ready"), sem("counted"), sem("slot_ready")
        sent = sem("sent")
        pad_stored = sem("pad_stored")
        tab_ready = sem("tab_ready")
        xs_loaded = [sem(f"xs_loaded{n}") for n in range(2)]
        xs_turned, xsT_ready, gate_done, gelu_ready, acts_ready, acts_turned, actsT_ready, down_done, made_ready = (
            sem(n) for n in ("xs_turned", "xsT_ready", "gate_done", "gelu_ready", "acts_ready", "acts_turned",
                             "actsT_ready", "down_done", "made_ready"))
        made_stored = [sem(f"made_stored{n}") for n in range(2)]
        back_loaded = [sem(f"back_loaded{n}") for n in range(8)]
        out_ready = sem("out_ready")
        squared = sem("squared")
        rows_ready = sem("rows_ready")

        block = ctx.enter_context(nc.Block())

        S_BANK, ST_BANK, PV_BANK, M_BANK = 0, 4, 6, 7
        m_ps = ps[:, M_BANK, 0:P // 2].bitcast(BF16)

        STACK = [(0, 3), (3 * HN, 2), (5 * HN, 1)]

        @block.sync
        def _(sp):
            x_v = query.rearrange("b (t p) h -> b p t h", p=P)
            sp.dma_start(x_sb[:, 0:TB, :], x_v[0]).then_inc(x_loaded[0], 16)
            for k in range(KC):
                sp.dma_start(cT[:, k, :], cond[:, k * P:(k + 1) * P].rearrange("b p -> p b"),
                             allow_slow_non_contiguous=True).then_inc(mod_loaded, 16)
            sp.dma_start(wmod[:, :, :], w_mod.rearrange("(k p) n -> p k n", p=P)).then_inc(mod_loaded, 16)
            for side in range(2):
                for quad in range(4):
                    rows = w_qkv.rearrange("(q h s d) i -> q s d h i", q=4, h=4, s=3)[quad, side]
                    sp.dma_start(w_raw[64 * (quad % 2):64 * (quad % 2) + 64, 2 * side + quad // 2, :],
                                 rows).then_inc(w_loaded, 16)
            for half in range(2):
                rows = w_qkv.rearrange("(n h s d) i -> n s h d i", n=2, h=8, s=3)[half, 2]
                sp.dma_start(w_raw[:, 4 + half, :], rows).then_inc(w_loaded, 16)
            for b in range(1, B):
                sp.dma_start(x_sb[:, b * TB:(b + 1) * TB, :], x_v[b]).then_inc(x_loaded[b], 16)
            sp.dma_start(wp_raw[:, :, :], w_proj.rearrange("(k p) n -> p k n", p=P)).then_inc(wp_loaded, 16)
            sp.dma_start(bp_b[:, :], b_proj.partition_broadcast(P)).then_inc(bp_loaded, 16)
            gate_v = gating.rearrange("e s (c p) f -> p e (s c) f", p=P)
            for e in range(4):
                sp.dma_start(gate_raw[:, e], gate_v[:, e]).then_inc(gate_loaded, 16)
            for k in range(KC):
                sp.dma_start(r_w[:, k, :], router_w[k * P:(k + 1) * P, :]).then_inc(router_loaded, 16)
                sp.dma_start(r_scale[:, k:k + 1], router_scale[k * P:(k + 1) * P].rearrange("(p o) -> p o", o=1)).then_inc(router_loaded, 16)
            sp.dma_start(e_scale[:, :], expert_scale.partition_broadcast(P)).then_inc(router_loaded, 16)
            sp.wait_ge(modrow_ready, 1)
            sp.dma_start(mod_d, mod_r[:, :]).then_inc(mod_stored, 16)
            sp.wait_ge(mod_stored, 16)

            for b in range(B):
                for m in range(4):
                    n = 4 * b + m
                    side, half = m // 2, m % 2
                    sp.wait_ge(lo_ready, n + 1)
                    for q in range(2):
                        sp.dma_start(qk_d[side, 4 * b + 2 * half + q].rearrange("p r x -> r p x"),
                                     pieces[64 * q:64 * q + 64, m, :, :]).then_inc(qk_stored[m], 16)
                if b == 2:
                    sp.wait_ge(gate_turned, 4)
                    for e in range(4):
                        sp.dma_start(gate_raw[:, e], gate_v[:, 4 + e]).then_inc(gate_loaded, 16)

            def load_stack(i, par):
                for side, stack in ((0, qst), (1, kst)):
                    rows = qk_d[side, i] if isinstance(i, int) else \
                        qk_d[side, bass.ds(i, 1)].rearrange("o p r x -> (o p) r x")
                    rows = rows.rearrange("p (d h) x -> p d (h x)", d=HN)
                    for piece, (r0, n) in enumerate(STACK):
                        src = rows[0:n] if side == 0 else rows[piece:piece + 1].to_broadcast([n, HN, 4 * SQ])
                        sp.dma_start(stack[r0:r0 + n * HN, par, :], src).then_inc(stack_loaded[par], 16)

            def load_mrow(par4, par2):
                sp.dma_start(qst[PR:PR + MR, par4, :], m_T[:, par2, :]).then_inc(mrow_loaded[par4], 16)

            for m in range(4):
                sp.wait_ge(qk_stored[m], 32)
            for i in range(4):
                load_stack(i, i)
            sp.wait_ge(v_done, 2 * B)
            for n, row in enumerate((GA, SB, CB, GB)):
                sp.dma_start(mod_b[:, n, :, :],
                             mod_d[:, row * H:(row + 1) * H].partition_broadcast(P)).then_inc(modb_loaded, 16)
            sp.wait_ge(wT_done, 4)
            sp.dma_start(lin[:, :, :, :], linear.rearrange("e (k p) f -> p e k f", p=P)).then_inc(lin_loaded, 16)
            sp.wait_ge(const_ready, 1)
            for n in range(CAP - FULL):
                sp.dma_start(slots_d[DUMMY + n * P:DUMMY + (n + 1) * P, :], zeros[:, :]).then_inc(pad_stored, 16)
            sp.wait_ge(m_evac, 1)
            load_mrow(0, 0)
            for m in range(4):
                sp.wait_ge(qk_stored[m], 32 * B)

            def quad(it, u, more):
                i = 4 * it + u
                if more or u < 3:
                    sp.wait_ge(m_evac, i + 2)
                    load_mrow((u + 1) % 4, (u + 1) % 2)
                if more:
                    sp.wait_ge(st_ready, 16 * i + 16)
                    load_stack(i + 4, u)
                if not more and i >= EARLY:
                    return
                sp.wait_ge(ctx_evac, ONE + i + 1)
                dst = ctx_d[i] if isinstance(i, int) else ctx_d[bass.ds(i, 1)]
                sp.dma_start(dst, ctx_o[:, u % 2, :]).then_inc(ctx_stored[u % 2], 16)

            with sp.Fori(0, 3) as it:
                for u in range(4):
                    quad(it, u, True)
            def load_ctx(kc, first, n):
                p0 = (first - 8 * kc) * HN
                for b in range(B):
                    sp.dma_start(ctx_n[p0:p0 + n * HN, kc, b, :],
                                 ctx_d[first:first + n, 32 * b:32 * b + HN, :]).then_inc(ctx_loaded[kc], 16)

            def load_inverses(kc, first, n, rows):
                p0 = (first - 8 * kc) * HN
                for b in range(B):
                    src = inv_d[first:first + n, b:b + 1, :].to_broadcast([n, HN, SQ])
                    sp.dma_start(rows[p0:p0 + n * HN, b, :], src).then_inc(ctx_loaded[kc], 16)

            def move_ctx(i):
                p0 = (i - 8) * HN
                sp.wait_ge(ctx_evac, ONE + i + 1)
                for b in range(B):
                    sp.dma_start(ctx_n[p0:p0 + HN, 1, b, :], ctx_o[32 * b:32 * b + HN, i % 2, :]).then_inc(ctx_loaded[1], 16)
                sp.wait_ge(inverse_ready, i - EARLY + 2)
                for b in range(B):
                    sp.dma_start(inv_1[p0:p0 + HN, b, :], inv_o[32 * b + HN:32 * b + 2 * HN, i % 2, :])\
                        .then_inc(ctx_loaded[1], 16)

            quad(3, 0, False)
            for n in range(2):
                sp.wait_ge(ctx_stored[n], ONE + 16 * 4)
            sp.wait_ge(v_staged, 12)
            load_ctx(0, 0, 8)
            quad(3, 1, False)
            for n in range(2):
                sp.wait_ge(ctx_stored[n], ONE + 16 * EARLY // 2)
            sp.dma_start(sum_rows, ctx_d.rearrange("i (b s r) x -> s r i b x", b=B, s=2)[1, 0]).then_inc(sums_loaded, 16)
            load_ctx(1, 8, EARLY - 8)
            quad(3, 2, False)
            sp.wait_ge(inverse_ready, 1)
            sp.dma_start(inv_d.rearrange("i b x -> (i b) x"), inv_rows).then_inc(inverse_stored, 16)
            sp.wait_ge(st_ready, 16 * 14)
            sp.wait_ge(inverse_stored, 16)
            load_inverses(0, 0, 8, inv_0)
            load_inverses(1, 8, EARLY - 8, inv_1)
            move_ctx(14)
            move_ctx(15)

            sp.wait_ge(tab_ready, 1)
            for e in range(E):
                row = sp.value_load(run_i[0:1, e:e + 1], min_val=e * SEG, max_val=e * SEG + B * SQ)
                sp.dma_start(slots_d[bass.ds(row, P), :], zeros[:, :]).then_inc(pad_stored, 16)
            sp.wait_ge(pad_stored, 16 * (E + CAP - FULL))
            sp.wait_ge(sent, 16 * 2 * NT)

            def load_slots(t, u):
                row = sp.value_load(tab_i[0:1, bass.ds(t, 1)], min_val=0, max_val=ROWS - P)
                sp.dma_start(xs[:, u, :], slots_d[bass.ds(row, P), :]).then_inc(xs_loaded[u], 16)

            def store_made(t, u):
                sp.wait_ge(made_ready, t + 1)
                sp.dma_start(made_d[bass.ds(t * P, P), :], made[:, u, :]).then_inc(made_stored[u], 16)

            load_slots(0, 0)
            load_slots(1, 1)

            def tile(t, u, more):
                if more:
                    sp.wait_ge(xs_turned, t + 1)
                    load_slots(t + 2, u)
                store_made(t, u)

            with sp.Fori(0, (CAP - 3) // 2) as it:
                for u in range(2):
                    tile(2 * it + u, u, True)
            for t in range(CAP - 3, CAP):
                tile(t, t % 2, t + 2 < CAP)

            out_v = out.rearrange("b (t p) h -> (b t) p h", p=P)
            for n in range(NT):
                sp.wait_ge(out_ready, n + 1)
                sp.dma_start(out_v[n], x_sb[:, n, :]).then_inc(out_stored, 16)
            sp.wait_ge(out_stored, 16 * NT)

        @block.gpsimd
        def _(pool):
            pool.memset(minus_half[:, :], -0.5)
            pool.memset(ident[:, :], 0.0).then_inc(pool_step, 1)
            pool.wait_ge(pool_step, 1)
            pool.affine_select(out=ident[:, :], in_=ident[:, :], compare_op=ALU.not_equal, fill=1.0,
                               base=0, pattern=[[-1, P]], channel_multiplier=1).then_inc(ident_ready, 1)
            pool.wait_ge(ident_ready, 1)
            pool.tensor_copy(identb[:, :], ident[:, :]).then_inc(ident_ready, 1)

            def inverse_deviation(b):
                pool.wait_ge(var_ready, b + 1)
                pool.tensor_scalar(rstd[:, :], mv[:, :, 1], EPS_LN, None, ALU.add).then_inc(var_eps, 1)
                pool.wait_ge(var_eps, b + 1)
                pool.tensor_tensor(rstd[:, :], rstd[:, :], minus_half[:, 0:TB], ALU.pow).then_inc(rstd_ready, 1)

            inverse_deviation(0)
            inverse_deviation(1)
            pool.memset(v_all[:, :, :, :], 1.0).then_inc(v_init, 1)
            pool.wait_ge(v_init, 1)
            pool.memset(kst[PR:PR + MR, :, :], 1.0).then_inc(v_init, 1)
            pool.wait_ge(v_init, 2)
            pool.memset(zeros[:, :], 0.0)
            pool.memset(mpc[:, :, :], 0.0)
            for e in range(E):
                pool.memset(seg_0[:, e:e + 1], float(e * SEG))
            pool.memset(ones[:, :], 1.0)
            pool.memset(minus_geq[:, :], -1.0)
            pool.memset(after_0[:, :], 1.0)
            pool.memset(earlier[:, :], 1.0).then_inc(const_ready, 1)
            pool.wait_ge(const_ready, 1)
            pool.affine_select(out=minus_geq[:, :], in_=minus_geq[:, :], compare_op=ALU.is_ge, fill=0.0,
                               base=0, pattern=[[-1, P]], channel_multiplier=1)
            pool.affine_select(out=after_0[:, :], in_=after_0[:, :], compare_op=ALU.is_gt, fill=0.0,
                               base=0, pattern=[[0, E], [1, GT]], channel_multiplier=0)
            pool.affine_select(out=earlier[:, :], in_=earlier[:, :], compare_op=ALU.is_gt, fill=0.0,
                               base=0, pattern=[[1, E], [-1, E]], channel_multiplier=0).then_inc(const_ready, 1)
            pool.wait_ge(const_ready, 2)
            pool.iota(m_rows[:, :], pattern=[[0, E], [P, 16]], base=0, channel_multiplier=0,
                      allow_small_or_imprecise_dtypes=True).then_inc(const_ready, 1)
            pool.wait_ge(const_ready, 3)
            pool.iota(tab[:, 0, :], pattern=[[1, 40], [0, E]], base=0, channel_multiplier=0,
                      allow_small_or_imprecise_dtypes=True)
            pool.iota(tab[:, 1, :], pattern=[[0, 40], [1, E]], base=0, channel_multiplier=0,
                      allow_small_or_imprecise_dtypes=True).then_inc(const_ready, 1)
            pool.wait_ge(router_loaded, 80)
            for k in range(KC):
                last = pool.tensor_scalar(r_w[:, k, :], r_w[:, k, :], r_scale[:, k:k + 1], H ** -0.5, ALU.mult, ALU.mult)
            last.then_inc(rw_ready, 1)
            pool.wait_ge(rw_ready, 1)
            for n in range(4 * B):
                if n in (4, 8):
                    inverse_deviation(1 + n // 4)
                pool.wait_ge(rest_ready, n + 1)
                pool.tensor_scalar(pieces[:, n % 4, 1, :], rest[:, n % 2, :], 1.0, None, ALU.mult)\
                    .then_inc(mid_ready, 1)

            def stage_v(i, par2):
                pool.wait_ge(v_init, 2)
                pool.tensor_copy(v_st[:, par2, :], v_all[:, bass.ds(i, 1), :, :].rearrange("p o t c -> p (o t c)"))\
                    .then_inc(v_staged, 1)

            def split_max(j, par2):
                pc = mpc[:, par2, 0:48].rearrange("p (s n) -> p s n", s=MR)
                pool.tensor_tensor(pc[:, 0, :], negm[:, par2, :], ones[:, 0:16], ALU.mult).then_inc(split1, 1)
                pool.wait_ge(split1, j + 1)
                pool.tensor_tensor(mrest[:, par2, :], negm[:, par2, :], pc[:, 0, :], ALU.subtract).then_inc(split2, 1)
                pool.wait_ge(split2, j + 1)
                pool.tensor_tensor(pc[:, 1, :], mrest[:, par2, :], ones[:, 0:16], ALU.mult).then_inc(split3, 1)
                pool.wait_ge(split3, j + 1)
                pool.tensor_tensor(pc[:, 2, :], mrest[:, par2, :], pc[:, 1, :], ALU.subtract).then_inc(m_split, 1)

            pool.wait_ge(v_evac, 2 * B)
            stage_v(0, 0)
            for j in range(2):
                pool.wait_ge(s_reduced, 8 * (j + 1))
                split_max(j, j)

            def quad(it, u, more):
                i = 4 * it + u
                if more or u < 3:
                    if not more:
                        pool.wait_ge(pv_done, 4 * i)
                    stage_v(i + 1, (u + 1) % 2)
                if more or u < 2:
                    pool.wait_ge(s_reduced, 8 * (i + 3))
                    pool.wait_ge(m_turned, i + 1)
                    split_max(i + 2, u % 2)

            with pool.Fori(0, 3) as it:
                for u in range(4):
                    quad(it, u, True)
            pool.wait_ge(modb_loaded, 64)
            pool.wait_ge(bp_loaded, 16)
            pool.wait_ge(xn_ready, B)
            pool.wait_ge(lo_ready, 4 * B)
            for m in range(4):
                pool.wait_ge(qk_stored[m], 32 * B)
            for u in range(4):
                quad(3, u, False)
                if u < 2:
                    for b in range(2 * u, 2 * u + 2):
                        pool.tensor_tensor(bias_row[:, :], mod_b[:, 0, b, :], bp_b[:, :], ALU.mult).then_inc(pool_step, 1)
                        pool.wait_ge(pool_step, 2 + b)
                        x_rows = x_sb[:, b * TB:(b + 1) * TB, :]
                        pool.tensor_tensor(x_rows, x_rows, bias_row[:, :].unsqueeze(1).to_broadcast([P, TB, H]), ALU.add)\
                            .then_inc(xb_ready, 1)
                        pool.wait_ge(xb_ready, b + 1)
                if u == 2:
                    for b in range(B):
                        last = pool.tensor_tensor(wp_g[:, b], wp_T[:, :, :], mod_b[:, 0, b, :].unsqueeze(1).to_broadcast([P, KC, H]), ALU.mult)
                    last.then_inc(wpg_ready, 1)

            def power(out_, in_, scale, eps, added, ready, n):
                pool.tensor_scalar(out_, in_, scale, eps, ALU.mult, ALU.add).then_inc(added, 1)
                pool.wait_ge(added, n)
                pool.tensor_tensor(out_, out_, minus_half[:, 0:out_.shape[1]], ALU.pow).then_inc(ready, 1)

            for b in range(B):
                pool.wait_ge(var2_ready, b + 1)
                power(rstd2[:, b * TB:(b + 1) * TB], mv2[:, b * TB:(b + 1) * TB, 1], 1.0, EPS_LN, var2_eps, rstd2_ready, b + 1)
            for g in range(NG):
                if g == NG - 1:
                    pool.wait_ge(squared, NT)
                    power(rrms, ssq, 1.0 / H, EPS_RMS, ssq_eps, rrms_ready, 1)
                pool.wait_ge(slot_ready, g + 1)
                for n in range(g * GT, (g + 1) * GT):
                    for c in range(2):
                        pool.indirect_dma_start(out=slots_d, out_offset=bass.IndirectOffsetOnAxis(ap=slot_i[:, c, n:n + 1], axis=0),
                                                in_=h2[:, n, :], in_offset=None).then_inc(sent, 16)
            pool.wait_ge(rows_ready, 1)
            for n in range(2):
                pool.wait_ge(made_stored[n], ONE + 16 * (CAP // 2 + (CAP % 2 if n == 0 else 0)))
            for n in range(NT):
                if n >= 8:
                    pool.wait_ge(out_ready, n - 7)
                for c in range(2):
                    pool.indirect_dma_start(out=back[:, n % 8, c, :], out_offset=None, in_=made_d,
                                            in_offset=bass.IndirectOffsetOnAxis(ap=slot_b[:, c, n:n + 1], axis=0))\
                        .then_inc(back_loaded[n % 8], 16)

        @block.scalar
        def _(act):
            act.sem_inc(ctx_evac, ONE)
            for n in range(2):
                act.sem_inc(ctx_stored[n], ONE)
                act.sem_inc(made_stored[n], ONE)
            act.wait_ge(mod_loaded, 48)
            act.activation(sig[:, :, :], cT[:, :, :], ACT.Exp, scale=-1.0).then_inc(sig_exp, 1)
            for s in range(4):
                act.wait_ge(wT_done, s + 1)
                dst = w_T[:, :, s * H:(s + 1) * H] if s < 3 else wp_T[:, :, :]
                act.activation(dst, ps[:, s, :].rearrange("p (k n) -> p k n", k=KC), ACT.Copy).then_inc(wT_evac, 1)

            act.wait_ge(modT_ready, 1)
            act.wait_ge(v_init, 2)

            def evac_hT(b):
                act.wait_ge(xT_done, b + 1)
                if b >= 2:
                    act.wait_ge(v_done, 2 * (b - 1))
                for k in range(KC):
                    last = act.activation(hT[:, b % 2, k, :], ps[:, k, :], ACT.Identity,
                                          bias=modT[:, SA * KC + k, b:b + 1], scale=modT[:, CA * KC + k, b:b + 1])
                last.then_inc(hT_ready, 1)

            evac_hT(0)
            for b in range(B):
                for m in range(4):
                    n = 4 * b + m
                    act.wait_ge(qk_done, n + 1)
                    if b >= 1:
                        act.wait_ge(qk_stored[m], 32 * b)
                    act.activation(pieces[:, m, 0, :], ps[:, 2 + m, :], ACT.Copy,
                                   scale=HN ** -0.5 if m < 2 else 1.0).then_inc(hi_ready, 1)
                if b + 1 < B:
                    evac_hT(b + 1)
                for hf in range(2):
                    act.wait_ge(v_done, 2 * b + hf + 1)
                    for tt in range(2):
                        dst = v_all[:, 4 * b:4 * b + 4, 2 * hf + tt, :].rearrange("p q (h c) -> p q h c", h=4)
                        last = act.activation(dst[:, :, :, 0:HN],
                                              ps[:, 6 + hf, tt * H:(tt + 1) * H].rearrange("p (q h d) -> p q h d", q=4, h=4),
                                              ACT.Copy)
                    last.then_inc(v_evac, 1)
                if b % 2:
                    for e in range(2 * (b - 1), 2 * (b + 1)):
                        act.wait_ge(gate_turned, e + 1)
                        act.activation(gate_T[:, e, :, :], ps[:, 2 + 2 * (e % 2):4 + 2 * (e % 2), :], ACT.Copy)\
                            .then_inc(gate_evac, 1)

            def exps(i, kt):
                for g in range(4):
                    act.wait_ge(st_ready, 16 * i + 4 * kt + g + 1)
                    act.activation(probs[:, kt % 2, g * SQ:(g + 1) * SQ], ps[:, ST_BANK + g % 2, :],
                                   ACT.Exp).then_inc(exp_done, 1)

            def evac_m(j, par2):
                act.wait_ge(m_turned, j + 1)
                act.activation(m_T[:, par2, :], m_ps[0:48, :], ACT.Copy).then_inc(m_evac, 1)

            def evac_ctx(i, par2):
                act.wait_ge(pv_done, 4 * i + 4)
                act.activation(ctx_o[:, par2, :], ps[:, PV_BANK, :], ACT.Copy).then_inc(ctx_evac, 1)

            evac_m(0, 0)
            exps(0, 0)

            def quad(it, u, more):
                i = 4 * it + u
                for k in range(4):
                    if k < 3:
                        exps(i, k + 1)
                    elif more or u < 3:
                        exps(i + 1, 0)
                    if k == 0 and (more or u < 3):
                        evac_m(i + 1, (u + 1) % 2)
                act.wait_ge(ctx_stored[u % 2], ONE + 16 * (2 * it + u // 2))
                evac_ctx(i, u % 2)

            with act.Fori(0, 3) as it:
                for u in range(4):
                    quad(it, u, True)
            for u in range(4):
                quad(3, u, False)

            def x1_out(pair):
                act.wait_ge(proj_done, pair + 1)
                act.activation(x_sb[:, 2 * pair:2 * pair + 2, :], ps[:, pair % 4, :].rearrange("p (n h) -> p n h", n=2),
                               ACT.Copy).then_inc(x1_ready, 1)

            def normalise(b):
                act.wait_ge(nbias2_ready, b + 1)
                for n in range(b * TB, (b + 1) * TB):
                    last = act.activation(h2[:, n, :], x_sb[:, n, :], ACT.Identity,
                                          bias=nbias2[:, n:n + 1], scale=rstd2[:, n:n + 1])
                last.then_inc(normed2, 1)

            def take_h2T(b):
                for n in range(b * TB, (b + 1) * TB):
                    act.wait_ge(h2_turned, n + 1)
                    if n >= 4:
                        act.wait_ge(logit_done, n - 3)
                    act.activation(h2T[:, n % 4, :, :], ps[:, 4 + n % 2, 0:H].rearrange("p (k x) -> p k x", k=KC),
                                   ACT.Copy).then_inc(h2T_ready, 1)

            for pair in range(4):
                x1_out(pair)
            normalise(0)
            normalise(1)
            x1_out(4)
            x1_out(5)
            take_h2T(0)
            x1_out(6)
            x1_out(7)
            normalise(2)
            take_h2T(1)
            normalise(3)
            take_h2T(2)
            take_h2T(3)
            for n in range(NT):
                if n:
                    act.wait_ge(squared, n)
                act.activation(squares, h2[:, n, :], ACT.Square, accum_out=ssq[:, n:n + 1]).then_inc(squared, 1)
            act.wait_ge(d_ready, 1)
            act.activation(prob[:, :, :], prob[:, :, :], ACT.Exp).then_inc(e_ready, 1)

            def take_xsT(t, u):
                act.wait_ge(xs_turned, t + 1)
                act.activation(xsT[:, u, :, :], ps[:, 0, 0:H].rearrange("p (k x) -> p k x", k=KC), ACT.Copy).then_inc(xsT_ready, 1)

            def do_gelu(t, u):
                act.wait_ge(gate_done, t + 1)
                act.activation(gelu[:, u, :], ps[:, 2 + u, 0:H], ACT.Gelu_apprx_tanh).then_inc(gelu_ready, 1)

            def take_made(t, u, before):
                act.wait_ge(down_done, t + 1)
                act.wait_ge(made_stored[u], ONE + 16 * before)
                act.activation(made[:, u, :], ps[:, 4, 0:H], ACT.Copy).then_inc(made_ready, 1)

            take_xsT(0, 0)
            do_gelu(0, 0)
            with act.Fori(0, CAP // 2) as it:
                for u in range(2):
                    t = 2 * it + u
                    take_xsT(t + 1, 1 - u)
                    do_gelu(t + 1, 1 - u)
                    take_made(t, u, it)
            take_made(CAP - 1, 0, CAP // 2)

        @block.vector
        def _(dve):
            chain = [0]

            def link(ins):
                chain[0] += 1
                ins.then_inc(dve_chain, 1)
                dve.wait_ge(dve_chain, chain[0])

            dve.wait_ge(sig_exp, 1)
            link(dve.tensor_scalar(sig[:, :, :], sig[:, :, :], 1.0, None, ALU.add))
            link(dve.reciprocal(sig[:, :, :], sig[:, :, :]))
            dve.tensor_tensor(sig[:, :, :], cT[:, :, :], sig[:, :, :], ALU.mult).then_inc(silu_ready, 1)

            def layer_norm(b):
                dve.wait_ge(x_loaded[b], 16)
                for t in range(TB):
                    last = dve.bn_stats(st[:, t, :], x_sb[:, b * TB + t, :])
                link(last)
                for t in range(TB):
                    last = dve.bn_aggr(mv[:, t, :], st[:, t, :])
                last.then_inc(var_ready, 1)
                dve.wait_ge(rstd_ready, b + 1)
                link(dve.scalar_tensor_tensor(nbias[:, :], mv[:, :, 0], -1.0, rstd[:, :], ALU.mult, ALU.mult))
                if b >= 2:
                    dve.wait_ge(xT_done, b - 1)
                for t in range(TB):
                    last = dve.tensor_scalar(xn[:, b % 2, t, :], x_sb[:, b * TB + t, :],
                                             rstd[:, t:t + 1], nbias[:, t:t + 1], ALU.mult, ALU.add)
                last.then_inc(xn_ready, 1)

            layer_norm(0)
            dve.wait_ge(modrow_done, 1)
            link(dve.tensor_copy(mod_r[:, :], ps[0:B, 4:7, :].rearrange("b k n -> b (k n)")))
            rows = mod_r[:, :].rearrange("b (a s n) -> b a s n", a=2, s=3)
            link(dve.tensor_scalar(rows[:, :, 1, :], rows[:, :, 1, :], 1.0, None, ALU.add))
            gates = rows[:, :, 2, :]
            link(dve.tensor_scalar(sgn[:, :, :], gates, 0.0, 2.0, ALU.is_ge, ALU.mult))
            link(dve.tensor_scalar(sgn[:, :, :], sgn[:, :, :], -1.0, None, ALU.add))
            link(dve.scalar_tensor_tensor(gates, gates, -1.0, gates, ALU.mult, ALU.max))
            dve.scalar_tensor_tensor(gates, gates, 0.25, sgn[:, :, :], ALU.max, ALU.mult).then_inc(modrow_ready, 1)
            dve.wait_ge(modT_done, 1)
            dve.tensor_copy(modT[:, :, :], ps[:, 7, 0:4 * B].rearrange("p (c b) -> p c b", b=B)).then_inc(modT_ready, 1)
            layer_norm(1)

            def low_piece(n):
                dve.wait_ge(mid_ready, n + 1)
                dve.tensor_tensor(pieces[:, n % 4, 2, :], rest[:, n % 2, :], pieces[:, n % 4, 1, :],
                                  ALU.subtract).then_inc(lo_ready, 1)

            for b in range(B):
                for m in range(4):
                    n = 4 * b + m
                    dve.wait_ge(hi_ready, n + 1)
                    if n >= 2:
                        dve.wait_ge(lo_ready, n - 1)
                    dve.scalar_tensor_tensor(rest[:, n % 2, :], ps[:, 2 + m, :], HN ** -0.5 if m < 2 else 1.0,
                                             pieces[:, m, 0, :], ALU.mult, ALU.subtract).then_inc(rest_ready, 1)
                    if n >= 1:
                        low_piece(n - 1)
                if b + 2 < B:
                    layer_norm(b + 2)
            low_piece(4 * B - 1)

            def reduce(j, pair, par2):
                dve.wait_ge(s_ready, 8 * j + pair + 1)
                bank = S_BANK + 2 * (pair % 2)
                dve.reduce_max(negm[:, par2, 2 * pair:2 * pair + 2], ps[:, bank:bank + 2, :], AX, negate=True)\
                    .then_inc(s_reduced, 1)

            for j in range(2):
                for pair in range(8):
                    reduce(j, pair, j)

            def quad(it, u):
                j = 4 * it + u + 2
                dve.wait_ge(m_split, j - 1)
                for pair in range(8):
                    reduce(j, pair, u % 2)

            with dve.Fori(0, 3) as it:
                for u in range(4):
                    quad(it, u)
            for u in range(2):
                quad(3, u)

            def over(v, n):
                return v.unsqueeze(2).to_broadcast([P, v.shape[1], n])

            dve.wait_ge(const_ready, 4)

            def statistics(b):
                for n in range(b * TB, (b + 1) * TB):
                    dve.wait_ge(x1_ready, n // 2 + 1)
                    last = dve.bn_stats(st2[:, n, :], x_sb[:, n, :])
                link(last)
                for n in range(b * TB, (b + 1) * TB):
                    last = dve.bn_aggr(mv2[:, n, :], st2[:, n, :])
                last.then_inc(var2_ready, 1)

            def norm_bias(b):
                tiles = slice(b * TB, (b + 1) * TB)
                dve.wait_ge(rstd2_ready, b + 1)
                dve.scalar_tensor_tensor(nbias2[:, tiles], mv2[:, tiles, 0], -1.0, rstd2[:, tiles], ALU.mult, ALU.mult)\
                    .then_inc(nbias2_ready, 1)

            def modulate(b):
                rows = h2[:, b * TB:(b + 1) * TB, :]
                dve.wait_ge(normed2, b + 1)
                link(dve.tensor_tensor(rows, rows, mod_b[:, 2, b, :].unsqueeze(1).to_broadcast([P, TB, H]), ALU.mult))
                dve.tensor_tensor(rows, rows, mod_b[:, 1, b, :].unsqueeze(1).to_broadcast([P, TB, H]), ALU.add)\
                    .then_inc(h2_ready, 1)

            def route(g):
                tiles = slice(g * GT, (g + 1) * GT)
                mine = chosen[:, tiles, :]
                dve.wait_ge(logit_done, GT * (g + 1))
                link(dve.tensor_copy(logit[:, tiles, :], ps[:, 6, g * GT * E:(g + 1) * GT * E].rearrange("p (t e) -> p t e", t=GT)))
                one = logit[:, tiles, :].unsqueeze(3).to_broadcast([P, GT, E, E])
                other = logit[:, tiles, :].unsqueeze(2).to_broadcast([P, GT, E, E])
                dve.tensor_tensor(equal, other, one, ALU.is_equal)
                link(dve.tensor_tensor(above, other, one, ALU.is_gt))
                link(dve.tensor_tensor(equal, equal, earlier[:, :].rearrange("p (a b) -> p a b", a=E).unsqueeze(1).to_broadcast([P, GT, E, E]), ALU.mult))
                link(dve.tensor_tensor(above, above, equal, ALU.add))
                link(dve.reduce_sum(count, above, AX))
                dve.tensor_scalar(mine, count, 2.0, None, ALU.is_lt).then_inc(chosen_ready, 1)
                dve.wait_ge(chosen_ready, g + 1)
                dve.wait_ge(counted, g + 1)
                link(dve.tensor_tensor(totals, ps[:, 7, GT * E:2 * GT * E].rearrange("p (t e) -> p e t", t=GT), before, ALU.add))
                link(dve.tensor_tensor_scan(upto.rearrange("p e t -> p (e t)"), after_0[:, :], totals.rearrange("p e t -> p (e t)"),
                                            0.0, ALU.mult, ALU.add))
                link(dve.tensor_tensor(place, ps[:, 7, 0:GT * E].rearrange("p (t e) -> p t e", t=GT),
                                       upto.rearrange("p e t -> p t e"), ALU.add))
                ways = ((0, 1.0, ALU.max), (1, -BIG, ALU.min))
                for c, by, _ in ways:
                    last = dve.scalar_tensor_tensor(marks[:, c, tiles, :], place, by, mine, ALU.add, ALU.mult)
                link(last)
                for c, _, best in ways:
                    last = dve.tensor_reduce(slot_f[:, c, tiles], marks[:, c, tiles, :], AX, best)
                link(last)
                for c, by, _ in ways:
                    last = dve.tensor_scalar(slot_i[:, c, tiles], slot_f[:, c, tiles], -by, None, ALU.add)
                last.then_inc(slot_ready, 1)
                link(dve.tensor_copy(start, upto[:, :, GT - 1]))

            dve.wait_ge(sums_loaded, 16)
            dve.reciprocal(inv_rows, sum_rows).then_inc(inverse_ready, 1)
            dve.wait_ge(xb_ready, B)
            dve.wait_ge(ctx_evac, ONE + 15)
            dve.reciprocal(inv_o[:, 0, :], ctx_o[:, 0, :]).then_inc(inverse_ready, 1)
            dve.wait_ge(ctx_loaded[0], 16 * 2 * B)
            for b in range(B):
                dve.tensor_tensor(ctx_n[:, 0, b, :], ctx_n[:, 0, b, :], inv_0[:, b, :], ALU.mult).then_inc(half_ready, 1)
            dve.wait_ge(ctx_evac, ONE + 16)
            dve.reciprocal(inv_o[:, 1, :], ctx_o[:, 1, :]).then_inc(inverse_ready, 1)
            dve.wait_ge(ctx_loaded[1], 16 * (2 * B + 4 * B))
            for b in range(B):
                dve.tensor_tensor(ctx_n[:, 1, b, :], ctx_n[:, 1, b, :], inv_1[:, b, :], ALU.mult).then_inc(ctx_ready, 1)
            link(dve.memset(before, 0.0))
            link(dve.tensor_copy(start, seg_0[:, :]))
            statistics(0)
            statistics(1)
            norm_bias(0)
            norm_bias(1)
            modulate(0)
            statistics(2)
            modulate(1)
            norm_bias(2)
            statistics(3)
            norm_bias(3)
            modulate(2)
            route(0)
            modulate(3)
            route(1)

            dve.tensor_copy(run_i[:, :], start[0:1, :])
            link(dve.tensor_tensor(filled[:, :], start, seg_0[:, :], ALU.subtract))
            fits = above.rearrange("p t a b -> p (t a b)")[:, 0:E * 16].rearrange("p (e m) -> p e m", e=E)
            link(dve.tensor_tensor(fits, over(filled[:, :], 16), m_rows[:, :].rearrange("p (e m) -> p e m", e=E), ALU.is_gt))
            link(dve.reduce_sum(filled[:, :], fits, AX))
            link(dve.tensor_tensor_scan(ends[:, :], ones[:, 0:E], filled[:, :], 0.0, ALU.mult, ALU.add))
            link(dve.tensor_tensor(firsts[:, :], ends[:, :], filled[:, :], ALU.subtract))
            tau, number, mine, use, row = (v.rearrange("o (t e) -> o t e", e=E)
                                           for v in (tab[:, 0, :], tab[:, 1, :], work[:, 0, :], work[:, 1, :], work[:, 2, :]))

            def all_tiles(v):
                return v[0:1, :].unsqueeze(1).to_broadcast([1, 40, E])

            dve.tensor_tensor(mine, tau, all_tiles(firsts), ALU.is_ge)
            dve.tensor_tensor(use, tau, all_tiles(ends), ALU.is_lt)
            link(dve.scalar_tensor_tensor(shift[:, :], firsts[:, :], -float(P), seg_0[:, :], ALU.mult, ALU.add))
            spare = float(DUMMY - FULL * P)
            link(dve.tensor_tensor(mine, mine, use, ALU.mult))
            dve.tensor_tensor(use, mine, number, ALU.mult)
            link(dve.scalar_tensor_tensor(row, all_tiles(shift), -spare, mine, ALU.add, ALU.mult))
            dve.reduce_sum(tab_f[:, 0:40], row, AX)
            link(dve.reduce_sum(tab_f[:, 40:80], use, AX))
            link(dve.scalar_tensor_tensor(tab_f[:, 0:40], tau[:, :, 0], float(P), tab_f[:, 0:40], ALU.mult, ALU.add))
            dve.tensor_scalar(tab_i[:, 0:40], tab_f[:, 0:40], spare, None, ALU.add)
            dve.tensor_copy(tab_i[:, 40:80], tab_f[:, 40:80]).then_inc(tab_ready, 1)

            dve.wait_ge(rrms_ready, 1)
            link(dve.tensor_tensor(prob, logit, over(rrms, E), ALU.mult))
            link(dve.reduce_max(top, prob, AX))
            dve.tensor_tensor(prob, prob, over(top, E), ALU.subtract).then_inc(d_ready, 1)
            for c in range(2):
                last = dve.tensor_tensor(hits[:, c], marks[:, c], over(slot_f[:, c, :], E), ALU.is_equal)
            link(last)
            for c in range(2):
                last = dve.tensor_tensor(marks[:, c], hits[:, c], shift[:, :].unsqueeze(1).to_broadcast([P, NT, E]), ALU.mult)
            link(last)
            for c in range(2):
                last = dve.reduce_sum(row_shift[:, c, :], marks[:, c], AX)
            link(last)
            link(dve.tensor_tensor(slot_f, slot_f, row_shift[:, :, :], ALU.subtract))
            for c, by in ((0, 1.0), (1, -BIG)):
                last = dve.tensor_scalar(slot_b[:, c, :], slot_f[:, c, :], -by, None, ALU.add)
            last.then_inc(rows_ready, 1)
            dve.wait_ge(e_ready, 1)
            dve.reduce_sum(total, prob, AX)
            link(dve.tensor_tensor(logit, prob, chosen, ALU.mult))
            dve.reduce_sum(picked, logit, AX)
            dve.tensor_tensor(prob, prob, e_scale[:, :].unsqueeze(1).to_broadcast([P, NT, E]), ALU.mult)
            link(dve.reciprocal(total, total))
            link(dve.tensor_tensor(picked, picked, total, ALU.mult))
            link(dve.tensor_scalar(top, picked, 0.0, None, ALU.is_le))
            link(dve.tensor_tensor(picked, picked, top, ALU.max))
            link(dve.reciprocal(picked, picked))
            link(dve.tensor_tensor(total, total, picked, ALU.mult))
            for c in range(2):
                last = dve.tensor_tensor(hits[:, c], hits[:, c], prob, ALU.mult)
            link(last)
            for c in range(2):
                last = dve.reduce_sum(slot_w[:, c, :], hits[:, c], AX)
            link(last)
            link(dve.tensor_tensor(slot_w, slot_w, total.unsqueeze(1).to_broadcast([P, 2, NT]), ALU.mult))

            def take_actsT(t):
                dve.wait_ge(acts_turned, t + 1)
                dve.tensor_copy(actsT[:, :, :], ps[:, 1, 0:H].rearrange("p (k x) -> p k x", k=KC)).then_inc(actsT_ready, 1)

            def do_acts(t, u):
                dve.wait_ge(gelu_ready, t + 1)
                dve.tensor_tensor(acts[:, u, :], ps[:, 2 + u, H:2 * H], gelu[:, u, :], ALU.mult).then_inc(acts_ready, 1)

            do_acts(0, 0)
            with dve.Fori(0, CAP // 2) as it:
                for u in range(2):
                    t = 2 * it + u
                    take_actsT(t)
                    do_acts(t + 1, 1 - u)
            take_actsT(CAP - 1)

            for n in range(NT):
                dve.wait_ge(back_loaded[n % 8], 32 * (n // 8 + 1))
                b0, b1 = back[:, n % 8, 0, :], back[:, n % 8, 1, :]
                link(dve.tensor_scalar(b0, b0, slot_w[:, 0, n:n + 1], None, ALU.mult))
                link(dve.scalar_tensor_tensor(b1, b1, slot_w[:, 1, n:n + 1], b0, ALU.mult, ALU.add))
                link(dve.tensor_tensor(b1, b1, mod_b[:, 3, n // TB, :], ALU.mult))
                dve.tensor_tensor(x_sb[:, n, :], x_sb[:, n, :], b1, ALU.add).then_inc(out_ready, 1)

        @block.tensor
        def _(pe):
            pe.wait_ge(ident_ready, 1)
            pe.wait_ge(w_loaded, 160)
            for s in range(3):
                for k in range(KC):
                    for half in range(2):
                        last = pe.transpose(ps[:, s, (2 * k + half) * P:(2 * k + half + 1) * P],
                                            w_raw[:, 2 * s + half, k * P:(k + 1) * P], ident[:, :])
                last.then_inc(wT_done, 1)
            pe.wait_ge(wp_loaded, 16)
            for k in range(KC):
                for half in range(2):
                    last = pe.transpose(ps[:, 3, (2 * k + half) * P:(2 * k + half + 1) * P],
                                        wp_raw[:, half, k * P:(k + 1) * P], ident[:, :])
            last.then_inc(wT_done, 1)
            pe.wait_ge(silu_ready, 1)
            for n in range(3):
                for k in range(KC):
                    last = pe.matmul(ps[0:B, 4 + n, :], sig[:, k, :], wmod[:, k, n * 512:(n + 1) * 512],
                                     start=k == 0, stop=k == KC - 1)
            last.then_inc(modrow_done, 1)
            pe.wait_ge(modrow_ready, 1)
            for c in range(4):
                last = pe.transpose(ps[:, 7, c * B:(c + 1) * B], mod_r[:, c * P:(c + 1) * P], ident[0:B, 0:B])
            last.then_inc(modT_done, 1)

            def turn_x(b):
                pe.wait_ge(xn_ready, b + 1)
                if b == 0:
                    pe.wait_ge(wT_evac, 4)
                else:
                    pe.wait_ge(hT_ready, b)
                for k in range(KC):
                    for t in range(TB):
                        last = pe.transpose(ps[:, k, t * P:(t + 1) * P], xn[:, b % 2, t, k * P:(k + 1) * P], ident[:, :])
                last.then_inc(xT_done, 1)

            turn_x(0)
            pe.wait_ge(modT_ready, 1)
            for b in range(B):
                pe.wait_ge(hT_ready, b + 1)
                for m in range(4):
                    if b >= 1:
                        pe.wait_ge(rest_ready, 4 * (b - 1) + m + 1)
                    if b == 2:
                        pe.wait_ge(gate_evac, 3 + m // 2)
                    for k in range(KC):
                        last = pe.matmul(ps[:, 2 + m, :], w_T[:, k, m * P:(m + 1) * P], hT[:, b % 2, k, :],
                                         start=k == 0, stop=k == KC - 1)
                    last.then_inc(qk_done, 1)
                if b + 1 < B:
                    turn_x(b + 1)
                for hf in range(2):
                    if b >= 1:
                        pe.wait_ge(v_evac, 2 * (b - 1) + hf + 1)
                    for tt in range(2):
                        t = 2 * hf + tt
                        for k in range(KC):
                            last = pe.matmul(ps[:, 6 + hf, tt * H:(tt + 1) * H], hT[:, b % 2, k, t * P:(t + 1) * P],
                                             w_T[:, k, 2 * H:3 * H], start=k == 0, stop=k == KC - 1)
                    last.then_inc(v_done, 1)
                if b % 2:
                    pe.wait_ge(rest_ready, 4 * (b + 1))
                    pe.wait_ge(gate_loaded, 64 * (b + 1) // 2)
                    for e in range(2 * (b - 1), 2 * (b + 1)):
                        if e % 4 >= 2:
                            pe.wait_ge(gate_evac, e - 1)
                        for k in range(KC):
                            for c in range(4):
                                last = pe.transpose(ps[:, 2 + 2 * (e % 2) + k, c * P:(c + 1) * P],
                                                    gate_raw[:, e % 4, c, k * P:(k + 1) * P], ident[:, :])
                        last.then_inc(gate_turned, 1)

            def s_tile(j, s, par, first=False):
                g, t = s // 4, s % 4
                if s % 2 == 0 and not (first and s < 4):
                    pe.wait_ge(s_reduced, 8 * j + s // 2 - 1)
                last = pe.matmul(ps[:, S_BANK + s % 4, :], qst[0:PR, par, g * SQ + t * P:g * SQ + (t + 1) * P],
                                 kst[0:PR, par, g * SQ:(g + 1) * SQ], start=True, stop=True)
                if s % 2:
                    last.then_inc(s_ready, 1)

            def st_tile(i, kt, g, par):
                if not (isinstance(i, int) and i == 0 and kt == 0 and g < 2):
                    pe.wait_ge(exp_done, 16 * i + 4 * kt + g - 1)
                pe.matmul(ps[:, ST_BANK + g % 2, :], kst[0:PR + MR, par, g * SQ + kt * P:g * SQ + (kt + 1) * P],
                          qst[0:PR + MR, par, g * SQ:(g + 1) * SQ], start=True, stop=True).then_inc(st_ready, 1)

            def pv(i, kt, par2):
                pe.wait_ge(exp_done, 16 * i + 4 * kt + 4)
                for g in range(4):
                    last = pe.matmul(ps[32 * g:32 * g + 32, PV_BANK, :], v_st[:, par2, kt * P + 32 * g:kt * P + 32 * g + 32],
                                     probs[:, kt % 2, g * SQ:(g + 1) * SQ], start=kt == 0, stop=kt == 3)
                last.then_inc(pv_done, 1)

            def turn_m(j, par2):
                pe.wait_ge(m_split, j + 1)
                pe.transpose(m_ps, mpc[:, par2, :], identb[:, :]).then_inc(m_turned, 1)

            pe.wait_ge(rest_ready, 4 * B)
            pe.wait_ge(v_evac, 2 * B)
            pe.wait_ge(gate_evac, E)
            pe.wait_ge(ident_ready, 2)
            for j in range(2):
                pe.wait_ge(stack_loaded[j], 96)
                for s in range(16):
                    s_tile(j, s, j, first=j == 0)
            turn_m(0, 0)
            pe.wait_ge(v_init, 2)
            pe.wait_ge(mrow_loaded[0], 16)
            for g in range(4):
                st_tile(0, 0, g, 0)

            def quad(it, u, more):
                i = 4 * it + u
                ahead = more or u < 2
                if ahead:
                    pe.wait_ge(stack_loaded[(u + 2) % 4], 96 * (it + 1 + (u + 2) // 4))
                for k in range(4):
                    here = k < 3
                    nxt = here or more or u < 3
                    if not here and nxt:
                        pe.wait_ge(mrow_loaded[(u + 1) % 4], 16 * (it + 1 + (u + 1) // 4))
                    args = (i, k + 1, u) if here else (i + 1, 0, (u + 1) % 4)
                    if ahead:
                        s_tile(i + 2, 4 * k, (u + 2) % 4)
                        s_tile(i + 2, 4 * k + 1, (u + 2) % 4)
                    if nxt:
                        st_tile(*args[0:2], 0, args[2])
                        st_tile(*args[0:2], 1, args[2])
                    if k == 0:
                        pe.wait_ge(v_staged, i + 1)
                        pe.wait_ge(ctx_evac, ONE + i)
                    pv(i, k, u % 2)
                    if nxt:
                        st_tile(*args[0:2], 2, args[2])
                        st_tile(*args[0:2], 3, args[2])
                    if ahead:
                        s_tile(i + 2, 4 * k + 2, (u + 2) % 4)
                        s_tile(i + 2, 4 * k + 3, (u + 2) % 4)
                    if k == 0 and (more or u < 3):
                        pe.wait_ge(m_evac, i + 1)
                        turn_m(i + 1, (u + 1) % 2)

            with pe.Fori(0, 3) as it:
                for u in range(4):
                    quad(it, u, True)
            for u in range(4):
                quad(3, u, False)

            def project_half(pair):
                bank = ps[:, pair % 4, :]
                if pair >= 4:
                    pe.wait_ge(x1_ready, pair - 3)
                pe.matmul(bank, ident[:, :], x_sb[:, 2 * pair:2 * pair + 2, :].rearrange("p n h -> p (n h)"), start=True, stop=False)
                project_slots(pair, 0)

            def project_slots(pair, kc):
                b = pair // 2
                for n in range(2):
                    t = 2 * (pair % 2) + n
                    last = pe.matmul(ps[:, pair % 4, n * H:(n + 1) * H], ctx_n[:, kc, b, t * P:(t + 1) * P], wp_g[:, b, kc, :],
                                     start=False, stop=kc == KC - 1 and n == 1)
                if kc == KC - 1:
                    last.then_inc(proj_done, 1)

            def turn_h2(b):
                pe.wait_ge(h2_ready, b + 1)
                for n in range(b * TB, (b + 1) * TB):
                    if n >= 2:
                        pe.wait_ge(h2T_ready, n - 1)
                    for k in range(KC):
                        last = pe.transpose(ps[:, 4 + n % 2, k * P:(k + 1) * P], h2[:, n, k * P:(k + 1) * P], ident[:, :])
                    last.then_inc(h2_turned, 1)

            def logits(b):
                for n in range(b * TB, (b + 1) * TB):
                    pe.wait_ge(h2T_ready, n + 1)
                    for k in range(KC):
                        last = pe.matmul(ps[:, 6, n * E:(n + 1) * E], h2T[:, n % 4, k, :], r_w[:, k, :],
                                         start=k == 0, stop=k == KC - 1)
                    last.then_inc(logit_done, 1)

            def counts(g):
                pe.wait_ge(chosen_ready, g + 1)
                if g >= 1:
                    pe.wait_ge(slot_ready, g)
                flat = chosen[:, g * GT:(g + 1) * GT, :].rearrange("p t e -> p (t e)")
                pe.matmul(ps[:, 7, 0:GT * E], minus_geq[:, :], flat, start=True, stop=True)
                pe.matmul(ps[:, 7, GT * E:2 * GT * E], ones[:, :], flat, start=True, stop=True).then_inc(counted, 1)

            pe.wait_ge(s_reduced, 8 * NQ)
            pe.wait_ge(xb_ready, B)
            pe.wait_ge(wpg_ready, 1)
            pe.wait_ge(half_ready, B)
            for pair in range(4):
                project_half(pair)
            for pair in range(4):
                pe.wait_ge(ctx_ready, pair // 2 + 1)
                project_slots(pair, 1)
            pe.wait_ge(ctx_ready, B)
            for pair in (4, 5):
                project_half(pair)
                project_slots(pair, 1)
            pe.wait_ge(exp_done, 16 * NQ)
            turn_h2(0)
            for pair in (6, 7):
                project_half(pair)
                project_slots(pair, 1)
            pe.wait_ge(ctx_evac, ONE + NQ)
            pe.wait_ge(m_evac, NQ)
            pe.wait_ge(const_ready, 4)
            pe.wait_ge(rw_ready, 1)
            logits(0)
            turn_h2(1)
            logits(1)
            counts(0)
            turn_h2(2)
            logits(2)
            turn_h2(3)
            logits(3)
            counts(1)

            def turn_slots(t, u, before):
                pe.wait_ge(xs_loaded[u], 16 * (before + 1))
                if isinstance(t, int) and t == 0:
                    pe.wait_ge(x1_ready, NT // 2)
                else:
                    pe.wait_ge(xsT_ready, t)
                for k in range(KC):
                    last = pe.transpose(ps[:, 0, k * P:(k + 1) * P], xs[:, u, k * P:(k + 1) * P], ident[:, :])
                last.then_inc(xs_turned, 1)

            def expert(t):
                return pe.value_load(tab_i[0:1, bass.ds(t + 40, 1)], min_val=0, max_val=E - 1)

            def gate(t, u, e):
                pe.wait_ge(xsT_ready, t + 1)
                if isinstance(t, int) and t == 0:
                    pe.wait_ge(h2T_ready, NT)
                for k in range(KC):
                    last = pe.matmul(ps[:, 2 + u, :], xsT[:, u, k, :], gate_T[:, bass.ds(e, 1), k, :].rearrange("p o n -> p (o n)"),
                                     start=k == 0, stop=k == KC - 1)
                last.then_inc(gate_done, 1)

            def turn_acts(t, u):
                pe.wait_ge(acts_ready, t + 1)
                for k in range(KC):
                    last = pe.transpose(ps[:, 1, k * P:(k + 1) * P], acts[:, u, k * P:(k + 1) * P], ident[:, :])
                last.then_inc(acts_turned, 1)

            def down(t, e):
                pe.wait_ge(actsT_ready, t + 1)
                for k in range(KC):
                    last = pe.matmul(ps[:, 4, 0:H], actsT[:, k, :], lin[:, bass.ds(e, 1), k, :].rearrange("p o n -> p (o n)"),
                                     start=k == 0, stop=k == KC - 1)
                last.then_inc(down_done, 1)

            pe.wait_ge(tab_ready, 1)
            pe.wait_ge(lin_loaded, 16)
            turn_slots(0, 0, 0)
            gate(0, 0, expert(0))
            with pe.Fori(0, CAP // 2) as it:
                for u in range(2):
                    t = 2 * it + u
                    turn_slots(t + 1, 1 - u, it + u)
                    turn_acts(t, u)
                    gate(t + 1, 1 - u, expert(t + 1))
                    down(t, expert(t))
            turn_acts(CAP - 1, 0)
            pe.wait_ge(made_ready, CAP - 1)
            down(CAP - 1, expert(CAP - 1))


_INS = ["L0_attn_query", "L0_attn_Wqkv", "L0_attn_Wproj", "L0_attn_bproj", "L0_ffn_router_logits",
        "L0_ffn_gating_einsum", "L0_ffn_linear", "L0_ffn_per_expert_scale", "L0_ffn_router_scale", "L0_c", "L0_wmod"]
_OUTS = [((B, SQ, H), "float32")]


def kernel(**inputs):
    import numpy as _np
    import concourse.bacc as _bacc
    from concourse import mybir as _mybir
    from concourse.bass_utils import run_bass_kernel_spmd as _run

    nc = _bacc.Bacc("TRN2", target_bir_lowering=False, num_devices=1)
    arrays, args = {}, []
    for name in _INS:
        a = _np.ascontiguousarray(inputs[name])
        arrays[f"in_{name}_dram"] = a
        args.append(nc.dram_tensor(f"in_{name}_dram", a.shape, _mybir.dt.from_np(a.dtype), kind="ExternalInput").ap())
    for i, (shape, dtype) in enumerate(_OUTS):
        dt = _mybir.dt.from_np(_np.dtype(dtype))
        args.append(nc.dram_tensor(f"out_{i}_dram", shape, dt, kind="ExternalOutput").ap())
    adaln_block(nc, *args)
    r = _run(nc, [arrays], core_ids=[0])
    got = tuple(r.results[0][f"out_{i}_dram"] for i in range(len(_OUTS)))
    return got[0]
```

```python
from contextlib import ExitStack

import concourse.bass as bass
from concourse import mybir

F32 = mybir.dt.float32
BF16 = mybir.dt.bfloat16
U32 = mybir.dt.uint32
I32 = mybir.dt.int32
ACT = mybir.ActivationFunctionType
ALU = mybir.AluOpType
AX = mybir.AxisListType.X

P = 128
B, SQ, H = 4, 512, 256
NH, HN = 16, 16
TB = SQ // P
NT = B * TB
KC = H // P
NQ = B * NH // 4
PR = 6 * HN
MR = 3
E = 8
CAP = (B * SQ * 2 + E * (P - 1)) // P
SEG = B * SQ + P
FULL = B * SQ * 2 // P
DUMMY = E * SEG
ROWS = DUMMY + (CAP - FULL) * P
ONE = 1
BIG = 32768.0
TOKENS = B * SQ
HX = H + 2
EPS_LN, EPS_RMS = 1e-5, 1e-6
TABLE = CAP + CAP % 2
EARLY = NQ - 2
NG, GT = B, TB
SA, CA, GA, SB, CB, GB = range(6)


def adaln_block(nc, query, w_qkv, w_proj, b_proj, router_w, gating, linear,
                expert_scale, router_scale, cond, w_mod, out):
    ctx = ExitStack()
    with ctx:
        def sb(name, shape, dt=F32):
            return ctx.enter_context(nc.sbuf_tensor(name, shape, dt))

        def sem(name):
            return ctx.enter_context(nc.semaphore(name))

        def dram(name, shape, dt=F32):
            return nc.dram_tensor(name, shape, dt, kind="Internal").ap()

        qk_d = dram("qk_d", [2, NQ, 3, 64, SQ], BF16)
        ctx_d = dram("ctx_d", [EARLY, P, SQ])
        inv_d = dram("inv_d", [EARLY, B, SQ])
        mod_d = dram("mod_d", [B, 6 * H])
        slots_d = dram("slots_d", [ROWS, HX])
        made_d = dram("made_d", [2 * TOKENS + (E + CAP - FULL) * P, H])

        ident = sb("ident", [P, P])
        minus_half = sb("minus_half", [P, 16])
        identb = sb("identb", [P, P], BF16)
        x_sb = sb("x_sb", [P, NT, H])
        w_T = sb("w_T", [P, KC, 3 * H])
        wp_T = sb("wp_T", [P, KC, H])
        lin = sb("lin", [P, E, KC, H])
        lin_flat = lin[:, :, :, :].rearrange("p e k n -> p (e k n)")
        wmod = lin_flat[:, 0:12 * H].rearrange("p (k n) -> p k n", k=KC)
        wp_raw = lin_flat[:, 12 * H:14 * H].rearrange("p (k n) -> p k n", k=KC)
        gate_T = sb("gate_T", [P, E, KC, 2 * H])
        cT = sb("cT", [P, KC, B])
        sig = sb("sig", [P, KC, B])
        area = sb("area", [P, 8 * H])
        mod_r = area[0:B, 0:6 * H]
        sgn = sb("sgn", [B, 2, H])
        modT = sb("modT", [P, 4, B])
        mod_b = sb("mod_b", [P, 4, B, H])
        mod_flat = mod_b[:, :, :, :].rearrange("p r b n -> p (r b n)")
        bp_b = sb("bp_b", [P, H])
        st = sb("st", [P, TB, 6])
        mv = sb("mv", [P, TB, 2])
        rstd = sb("rstd", [P, TB])
        nbias = sb("nbias", [P, TB])
        xn = mod_flat[:, 0:8 * H].rearrange("p (n t h) -> p n t h", n=2, t=TB)
        hT = mod_flat[:, 8 * H:16 * H].rearrange("p (n k x) -> p n k x", n=2, k=KC)
        space = sb("space", [P, 12 * H])
        w_raw = space[:, 0:6 * H].rearrange("p (s n) -> p s n", s=6)
        pieces = space[:, :].bitcast(BF16).rearrange("p (m c x) -> p m c x", m=4, c=3)
        wp_g = space[:, 0:8 * H].rearrange("p (b k n) -> p b k n", b=B, k=KC)
        rest = sb("rest", [P, 2, SQ])
        sum_rows, inv_rows = rest[0:EARLY * B, 0, :], rest[0:EARLY * B, 1, :]
        bias_row = space[:, 8 * H:9 * H]
        inv_o = space[:, 8 * H:12 * H].rearrange("p (n x) -> p n x", n=2)
        v_all = sb("v_all", [P, NQ, TB, P])
        v_st = area[:, 0:4 * H].rearrange("p (n x) -> p n x", n=2)
        stacks = sb("stacks", [P, 2, 4, 4 * SQ], BF16)
        qst, kst = stacks[:, 0], stacks[:, 1]
        stacks_flat = stacks[:, :, :, :].rearrange("p s n x -> p (s n x)").bitcast(F32)
        negm = sb("negm", [P, 2, 16])
        mrest = sb("mrest", [P, 2, 16])
        mpc = sb("mpc", [P, 2, P], BF16)
        m_T = sb("m_T", [48, 2, P], BF16)
        probs = sb("probs", [P, 2, 4 * SQ])
        gate_raw = probs[:, :, :].rearrange("p n x -> p (n x)").rearrange("p (e c f) -> p e c f", e=4, c=4)
        h2x = stacks_flat[:, 0:NT * HX].rearrange("p (n h) -> p n h", n=NT)
        h2 = h2x[:, :, 0:H]
        ctx_o = area[:, 4 * H:8 * H].rearrange("p (n x) -> p n x", n=2)
        v_flat = v_all[:, :, :, :].rearrange("p q t c -> p (q t c)")
        ctx_n = v_flat[:, 0:KC * B * SQ].rearrange("p (k b x) -> p k b x", k=KC, b=B)
        inv_0 = v_flat[:, KC * B * SQ:(KC + 1) * B * SQ].rearrange("p (b x) -> p b x", b=B)
        ranks = v_flat[:, (KC + 1) * B * SQ:(KC + 1) * B * SQ + 2 * GT * E * E].rearrange(
            "p (n t a b) -> p n t a b", n=2, t=GT, a=E)

        inv_1 = stacks_flat[:, 16 * H:16 * H + B * SQ].rearrange("p (b x) -> p b x", b=B)
        late = stacks_flat[:, NT * HX:NT * HX + 14 * H]
        h2T = late[:, 0:4 * H].rearrange("p (n k x) -> p n k x", n=4, k=KC)
        squares = late[:, 4 * H:5 * H]
        xs = late[:, 0:2 * HX].rearrange("p (n h) -> p n h", n=2)
        xsT = late[:, 5 * H:7 * H].rearrange("p (n k x) -> p n k x", n=2, k=KC)
        gelu = late[:, 7 * H:9 * H].rearrange("p (n h) -> p n h", n=2)
        acts = late[:, 9 * H:11 * H].rearrange("p (n h) -> p n h", n=2)
        actsT = late[:, 11 * H:12 * H].rearrange("p (k x) -> p k x", k=KC)
        made = late[:, 12 * H:14 * H].rearrange("p (n h) -> p n h", n=2)
        back = probs[:, :, :].rearrange("p n x -> p (n x)").rearrange("p (n c h) -> p n c h", n=8, c=2)
        taken = [0]

        def small(*shape, dt=F32):
            n = 1
            for d in shape:
                n *= d
            v = area[:, taken[0]:taken[0] + n]
            taken[0] += n
            assert taken[0] <= 8 * H
            v = v if dt == F32 else v.bitcast(dt)
            if len(shape) == 2:
                v = v.rearrange("p (a b) -> p a b", a=shape[0])
            if len(shape) == 3:
                v = v.rearrange("p (a b c) -> p a b c", a=shape[0], b=shape[1])
            return v

        st2, mv2 = small(NT, 6), small(NT, 2)
        rstd2, nbias2 = small(NT), small(NT)
        ssq, rrms = small(NT), small(NT)
        logit, prob, chosen = small(NT, E), small(NT, E), small(NT, E)
        top, total, picked = small(NT), small(NT), small(NT)
        count, totals, upto, place = small(GT, E), small(E, GT), small(E, GT), small(GT, E)
        before = small(E, GT)
        start = before[:, :, 0]
        marks, hits = small(2, NT, E), small(2, NT, E)
        target = small(4, 1, dt=U32)
        slot_f, slot_w = small(2, NT), small(2, NT)
        slot_i = small(2, NT, dt=U32)
        above, equal = ranks[:, 0], ranks[:, 1]
        earlier = sb("earlier", [P, E * E])
        after_0 = sb("after_0", [P, E * GT])
        minus_geq = sb("minus_geq", [P, P])
        ones = sb("ones", [P, P])
        seg_0 = sb("seg_0", [P, E])
        padding = sb("padding", [P, H])
        pad_ids = sb("pad_ids", [P, E + CAP - FULL, 2])
        token_2 = sb("token_2", [P, NT])
        run_pads = v_flat[:, 1024:1024 + E * HX].rearrange("p (e h) -> p e h", e=E)
        tab_0 = (KC + 1) * B * SQ + 2 * GT * E * E
        tab = v_flat[:, tab_0:tab_0 + 2 * TABLE * E].rearrange("p (n x) -> p n x", n=2)
        m_rows = sb("m_rows", [P, E * 16])
        work = v_flat[:, 0:3 * TABLE * E].rearrange("o (a b) -> o a b", a=3)
        ends, firsts, filled, shift = (sb(n, [P, E]) for n in ("ends", "firsts", "filled", "shift"))
        tab_f = sb("tab_f", [P, 2 * TABLE])
        base = sb("base", [P, TABLE])
        tab_i = sb("tab_i", [1, 2 * TABLE], I32)
        run_i = sb("run_i", [1, E], I32)
        r_w = sb("r_w", [P, KC, E])
        r_scale = sb("r_scale", [P, KC])
        e_scale = sb("e_scale", [P, E])

        ps = ctx.enter_context(nc.psum_tensor("ps", [P, 8, 512], F32))

        x_loaded = [sem(f"x_loaded{b}") for b in range(B)]
        w_loaded = sem("w_loaded")
        wp_loaded = sem("wp_loaded")
        c_loaded = sem("c_loaded")
        wmod_loaded = [sem(f"wmod_loaded{n}") for n in range(2)]
        bp_loaded = sem("bp_loaded")
        pool_step = sem("pool_step")
        ident_ready = sem("ident_ready")
        v_init, k_init = sem("v_init"), sem("k_init")
        sig_exp = sem("sig_exp")
        silu_ready = sem("silu_ready")
        dve_chain = sem("dve_chain")
        wT_done = sem("wT_done")
        wT_evac = sem("wT_evac")
        modrow_done = sem("modrow_done")
        modrow_evac = sem("modrow_evac")
        modrow_ready = sem("modrow_ready")
        modT_done = sem("modT_done")
        modT_ready = sem("modT_ready")
        mod_stored = sem("mod_stored")
        modb_loaded = sem("modb_loaded")
        var_ready = sem("var_ready")
        var_eps = sem("var_eps")
        rstd_ready = sem("rstd_ready")
        xn_ready = sem("xn_ready")
        xT_done = sem("xT_done")
        hT_ready = sem("hT_ready")
        qk_done = sem("qk_done")
        hi_ready = sem("hi_ready")
        rest_ready = sem("rest_ready")
        mid_ready = sem("mid_ready")
        lo_ready = sem("lo_ready")
        qk_stored = [sem(f"qk_stored{n}") for n in range(4)]
        v_done = sem("v_done")
        v_evac = sem("v_evac")
        stack_loaded = [sem(f"stack_loaded{n}") for n in range(4)]
        mrow_loaded = [sem(f"mrow_loaded{n}") for n in range(4)]
        s_ready = sem("s_ready")
        s_reduced = sem("s_reduced")
        split1, split2, split3, m_split = (sem(n) for n in ("split1", "split2", "split3", "m_split"))
        m_turned = sem("m_turned")
        m_evac = sem("m_evac")
        st_ready = sem("st_ready")
        exp_done = sem("exp_done")
        v_staged = sem("v_staged")
        pv_done = sem("pv_done")
        ctx_evac = sem("ctx_evac")
        ctx_stored = [sem(f"ctx_stored{n}") for n in range(2)]
        ctx_loaded = [sem(f"ctx_loaded{k}") for k in range(KC)]
        sums_loaded, inverse_ready, inverse_stored, half_ready = (
            sem(n) for n in ("sums_loaded", "inverse_ready", "inverse_stored", "half_ready"))
        ctx_ready = sem("ctx_ready")
        proj_done = sem("proj_done")
        x1_ready = sem("x1_ready")
        xb_ready = sem("xb_ready")
        out_stored = sem("out_stored")
        gate_loaded = sem("gate_loaded")
        gate_turned = sem("gate_turned")
        gate_evac = sem("gate_evac")
        lin_loaded = sem("lin_loaded")
        router_loaded = sem("router_loaded")
        rw_ready = sem("rw_ready")
        const_ready = sem("const_ready")
        wpg_ready = sem("wpg_ready")
        var2_ready, var2_eps, rstd2_ready, nbias2_ready = (sem(n) for n in ("var2_ready", "var2_eps", "rstd2_ready", "nbias2_ready"))
        normed2 = sem("normed2")
        h2_ready = sem("h2_ready")
        ssq_eps, rrms_ready = sem("ssq_eps"), sem("rrms_ready")
        h2_turned, h2T_ready, logit_done = (sem(n) for n in ("h2_turned", "h2T_ready", "logit_done"))
        d_ready, e_ready = sem("d_ready"), sem("e_ready")
        chosen_ready, counted, slot_ready = sem("chosen_ready"), sem("counted"), sem("slot_ready")
        sent = sem("sent")
        pad_stored = sem("pad_stored")
        tab_ready = sem("tab_ready")
        xs_loaded = [sem(f"xs_loaded{n}") for n in range(2)]
        xs_turned, xsT_ready, gate_done, gelu_ready, acts_ready, acts_turned, actsT_ready, down_done, made_ready = (
            sem(n) for n in ("xs_turned", "xsT_ready", "gate_done", "gelu_ready", "acts_ready", "acts_turned",
                             "actsT_ready", "down_done", "made_ready"))
        made_stored = [sem(f"made_stored{n}") for n in range(2)]
        back_loaded = [sem(f"back_loaded{n}") for n in range(8)]
        out_ready = sem("out_ready")
        squared = sem("squared")
        token_ready, tau_ready, target_ready = sem("token_ready"), sem("tau_ready"), sem("target_ready")
        halved = sem("halved")
        run_ready, pads_ready = sem("run_ready"), sem("pads_ready")
        bent, sending = sem("bent"), sem("sending")

        block = ctx.enter_context(nc.Block())

        S_BANK, ST_BANK, PV_BANK, M_BANK = 0, 4, 6, 7

        def gate_bank(e):
            return 2 + 2 * (e % 2) if e < 4 else 4

        m_ps = ps[:, M_BANK, 0:P // 2].bitcast(BF16)

        STACK = [(0, 3), (3 * HN, 2), (5 * HN, 1)]

        @block.sync
        def _(sp):
            x_v = query.rearrange("b (t p) h -> b p t h", p=P)
            sp.dma_start(x_sb[:, 0:TB, :], x_v[0]).then_inc(x_loaded[0], 16)
            for k in range(KC):
                sp.dma_start(cT[:, k, :], cond[:, k * P:(k + 1) * P].rearrange("b p -> p b"),
                             allow_slow_non_contiguous=True).then_inc(c_loaded, 16)
            for side in range(2):
                for quad in range(4):
                    rows = w_qkv.rearrange("(q h s d) i -> q s d h i", q=4, h=4, s=3)[quad, side]
                    sp.dma_start(w_raw[64 * (quad % 2):64 * (quad % 2) + 64, 2 * side + quad // 2, :],
                                 rows).then_inc(w_loaded, 16)
            for half in range(2):
                rows = w_qkv.rearrange("(n h s d) i -> n s h d i", n=2, h=8, s=3)[half, 2]
                sp.dma_start(w_raw[:, 4 + half, :], rows).then_inc(w_loaded, 16)
            w_mod_v = w_mod.rearrange("(k p) n -> p k n", p=P)
            sp.dma_start(wmod[:, :, 0:2 * H], w_mod_v[:, :, 0:2 * H]).then_inc(wmod_loaded[0], 16)
            sp.dma_start(wp_raw[:, :, :], w_proj.rearrange("(k p) n -> p k n", p=P)).then_inc(wp_loaded, 16)
            sp.dma_start(wmod[:, :, 2 * H:], w_mod_v[:, :, 2 * H:]).then_inc(wmod_loaded[1], 16)
            for b in range(1, B):
                sp.dma_start(x_sb[:, b * TB:(b + 1) * TB, :], x_v[b]).then_inc(x_loaded[b], 16)
            sp.dma_start(bp_b[:, :], b_proj.partition_broadcast(P)).then_inc(bp_loaded, 16)
            gate_v = gating.rearrange("e s (c p) f -> p e (s c) f", p=P)
            for e in range(4):
                sp.dma_start(gate_raw[:, e], gate_v[:, e]).then_inc(gate_loaded, 16)
            for k in range(KC):
                sp.dma_start(r_w[:, k, :], router_w[k * P:(k + 1) * P, :]).then_inc(router_loaded, 16)
                sp.dma_start(r_scale[:, k:k + 1], router_scale[k * P:(k + 1) * P].rearrange("(p o) -> p o", o=1)).then_inc(router_loaded, 16)
            sp.dma_start(e_scale[:, :], expert_scale.partition_broadcast(P)).then_inc(router_loaded, 16)
            def load_stack(i, par):
                for side, stack in ((0, qst), (1, kst)):
                    rows = qk_d[side, i] if isinstance(i, int) else \
                        qk_d[side, bass.ds(i, 1)].rearrange("o p r x -> (o p) r x")
                    rows = rows.rearrange("p (d h) x -> p d (h x)", d=HN)
                    for piece, (r0, n) in enumerate(STACK):
                        src = rows[0:n] if side == 0 else rows[piece:piece + 1].to_broadcast([n, HN, 4 * SQ])
                        sp.dma_start(stack[r0:r0 + n * HN, par, :], src).then_inc(stack_loaded[par], 16)

            for b in range(B):
                for m in range(4):
                    n = 4 * b + m
                    side, half = m // 2, m % 2
                    sp.wait_ge(lo_ready, n + 1)
                    for q in range(2):
                        sp.dma_start(qk_d[side, 4 * b + 2 * half + q].rearrange("p r x -> r p x"),
                                     pieces[64 * q:64 * q + 64, m, :, :]).then_inc(qk_stored[m], 16)
                if b == 1:
                    sp.wait_ge(modrow_ready, 1)
                    sp.dma_start(mod_d, mod_r[:, :]).then_inc(mod_stored, 16)
                    sp.wait_ge(gate_turned, 4)
                    for e in range(4):
                        sp.dma_start(gate_raw[:, e], gate_v[:, 4 + e]).then_inc(gate_loaded, 16)
                if b == 2:
                    for m in range(4):
                        sp.wait_ge(qk_stored[m], 32 * (b + 1))
                    load_stack(0, 0)
                    load_stack(1, 1)

            def load_mrow(par4, par2):
                sp.dma_start(qst[PR:PR + MR, par4, :], m_T[:, par2, :]).then_inc(mrow_loaded[par4], 16)

            load_stack(2, 2)
            load_stack(3, 3)
            sp.wait_ge(m_evac, 1)
            load_mrow(0, 0)
            sp.wait_ge(mod_stored, 16)
            sp.wait_ge(v_done, 2 * B)
            for n, row in enumerate((GA, SB, CB, GB)):
                sp.dma_start(mod_b[:, n, :, :],
                             mod_d[:, row * H:(row + 1) * H].partition_broadcast(P)).then_inc(modb_loaded, 16)
            for m in range(4):
                sp.wait_ge(qk_stored[m], 32 * B)

            def quad(it, u, more):
                i = 4 * it + u
                if more or u < 3:
                    sp.wait_ge(m_evac, i + 2)
                    load_mrow((u + 1) % 4, (u + 1) % 2)
                if more:
                    sp.wait_ge(st_ready, 16 * i + 16)
                    load_stack(i + 4, u)
                if not more and i >= EARLY:
                    return
                sp.wait_ge(ctx_evac, ONE + i + 1)
                dst = ctx_d[i] if isinstance(i, int) else ctx_d[bass.ds(i, 1)]
                sp.dma_start(dst, ctx_o[:, u % 2, :]).then_inc(ctx_stored[u % 2], 16)

            with sp.Fori(0, 3) as it:
                for u in range(4):
                    quad(it, u, True)
            def load_ctx(kc, first, n):
                p0 = (first - 8 * kc) * HN
                for b in range(B):
                    sp.dma_start(ctx_n[p0:p0 + n * HN, kc, b, :],
                                 ctx_d[first:first + n, 32 * b:32 * b + HN, :]).then_inc(ctx_loaded[kc], 16)

            def load_inverses(kc, first, n, rows):
                p0 = (first - 8 * kc) * HN
                for b in range(B):
                    src = inv_d[first:first + n, b:b + 1, :].to_broadcast([n, HN, SQ])
                    sp.dma_start(rows[p0:p0 + n * HN, b, :], src).then_inc(ctx_loaded[kc], 16)

            def move_ctx(i):
                p0 = (i - 8) * HN
                sp.wait_ge(ctx_evac, ONE + i + 1)
                for b in range(B):
                    sp.dma_start(ctx_n[p0:p0 + HN, 1, b, :], ctx_o[32 * b:32 * b + HN, i % 2, :]).then_inc(ctx_loaded[1], 16)
                sp.wait_ge(inverse_ready, i - EARLY + 2)
                for b in range(B):
                    sp.dma_start(inv_1[p0:p0 + HN, b, :], inv_o[32 * b + HN:32 * b + 2 * HN, i % 2, :])\
                        .then_inc(ctx_loaded[1], 16)

            quad(3, 0, False)
            for n in range(2):
                sp.wait_ge(ctx_stored[n], ONE + 16 * 4)
            sp.wait_ge(v_staged, 12)
            load_ctx(0, 0, 8)
            quad(3, 1, False)
            for n in range(2):
                sp.wait_ge(ctx_stored[n], ONE + 16 * EARLY // 2)
            sp.dma_start(sum_rows, ctx_d.rearrange("i (b s r) x -> s r i b x", b=B, s=2)[1, 0]).then_inc(sums_loaded, 16)
            load_ctx(1, 8, EARLY - 8)
            quad(3, 2, False)
            sp.wait_ge(inverse_ready, 1)
            sp.dma_start(inv_d.rearrange("i b x -> (i b) x"), inv_rows).then_inc(inverse_stored, 16)
            sp.wait_ge(st_ready, 16 * 14)
            sp.wait_ge(inverse_stored, 16)
            load_inverses(0, 0, 8, inv_0)
            load_inverses(1, 8, EARLY - 8, inv_1)
            move_ctx(14)
            move_ctx(15)

            sp.wait_ge(wT_done, 4)
            sp.wait_ge(modrow_done, 3)
            sp.dma_start(lin[:, :, :, :], linear.rearrange("e (k p) f -> p e k f", p=P)).then_inc(lin_loaded, 16)


            def pad(rows, n):
                sp.dma_start(rows[:, 0:H], padding[:, :]).then_inc(pad_stored, 16)
                sp.dma_start(rows[:, H:HX], pad_ids[:, n, :]).then_inc(pad_stored, 16)

            sp.wait_ge(token_ready, 1)
            for n in range(CAP - FULL):
                pad(slots_d[DUMMY + n * P:DUMMY + (n + 1) * P, :], E + n)
            sp.wait_ge(run_ready, 1)
            sp.wait_ge(pads_ready, 2)
            for e in range(E):
                row = sp.value_load(run_i[0:1, e:e + 1], min_val=e * SEG, max_val=e * SEG + B * SQ)
                sp.dma_start(slots_d[bass.ds(row, P), :], run_pads[:, e, :]).then_inc(pad_stored, 16)
            sp.wait_ge(tab_ready, 1)
            sp.wait_ge(pad_stored, 16 * (E + 2 * (CAP - FULL)))
            sp.wait_ge(sent, 16 * 2 * NT)

            def load_slots(t, u):
                row = sp.value_load(tab_i[0:1, bass.ds(t, 1)], min_val=0, max_val=ROWS - P)
                sp.dma_start(xs[:, u, :], slots_d[bass.ds(row, P), :]).then_inc(xs_loaded[u], 16)

            def tile(t, u):
                sp.wait_ge(xs_turned, t + 3)
                sp.wait_ge(target_ready, t + 3)
                load_slots(t + 4, u)

            for t in range(4):
                if t >= 2:
                    sp.wait_ge(xs_turned, t - 1)
                    sp.wait_ge(target_ready, t - 1)
                load_slots(t, t % 2)
            with sp.Fori(0, (CAP - 5) // 2) as it:
                for u in range(2):
                    tile(2 * it + u, u)
            tile(CAP - 5, 0)

            for n in range(2):
                sp.wait_ge(made_stored[n], 16 * ((CAP + 1 - n) // 2))
            out_v = out.rearrange("b (t p) h -> (b t) p h", p=P)
            for n in range(NT + 7):
                if n < NT:
                    if n >= 8:
                        sp.wait_ge(out_ready, n - 7)
                    sp.dma_start(back[:, n % 8], made_d[2 * n * P:2 * (n + 1) * P, :].rearrange("(p c) h -> p c h", c=2))\
                        .then_inc(back_loaded[n % 8], 16)
                if n >= 7:
                    sp.wait_ge(out_ready, n - 6)
                    sp.dma_start(out_v[n - 7], x_sb[:, n - 7, :]).then_inc(out_stored, 16)
            sp.wait_ge(out_stored, 16 * NT)

        @block.gpsimd
        def _(pool):
            pool.memset(minus_half[:, :], -0.5)
            pool.memset(ident[:, :], 0.0).then_inc(pool_step, 1)
            pool.wait_ge(pool_step, 1)
            pool.affine_select(out=ident[:, :], in_=ident[:, :], compare_op=ALU.not_equal, fill=1.0,
                               base=0, pattern=[[-1, P]], channel_multiplier=1).then_inc(ident_ready, 1)
            pool.wait_ge(ident_ready, 1)
            pool.tensor_copy(identb[:, :], ident[:, :]).then_inc(ident_ready, 1)

            def inverse_deviation(b):
                pool.wait_ge(var_ready, b + 1)
                pool.tensor_scalar(rstd[:, :], mv[:, :, 1], EPS_LN, None, ALU.add).then_inc(var_eps, 1)
                pool.wait_ge(var_eps, b + 1)
                pool.tensor_tensor(rstd[:, :], rstd[:, :], minus_half[:, 0:TB], ALU.pow).then_inc(rstd_ready, 1)

            pool.memset(v_all[:, :, :, :], 1.0).then_inc(v_init, 1)
            inverse_deviation(0)
            inverse_deviation(1)
            pool.memset(padding[:, :], 0.0)
            pool.memset(mpc[:, :, :], 0.0)
            for e in range(E):
                pool.memset(seg_0[:, e:e + 1], float(e * SEG))
            pool.memset(ones[:, :], 1.0)
            pool.memset(minus_geq[:, :], -1.0)
            pool.memset(after_0[:, :], 1.0)
            pool.memset(earlier[:, :], 1.0).then_inc(const_ready, 1)
            pool.wait_ge(const_ready, 1)
            pool.affine_select(out=minus_geq[:, :], in_=minus_geq[:, :], compare_op=ALU.is_ge, fill=0.0,
                               base=0, pattern=[[-1, P]], channel_multiplier=1)
            pool.affine_select(out=after_0[:, :], in_=after_0[:, :], compare_op=ALU.is_gt, fill=0.0,
                               base=0, pattern=[[0, E], [1, GT]], channel_multiplier=0)
            pool.affine_select(out=earlier[:, :], in_=earlier[:, :], compare_op=ALU.is_gt, fill=0.0,
                               base=0, pattern=[[1, E], [-1, E]], channel_multiplier=0).then_inc(const_ready, 1)
            pool.wait_ge(const_ready, 2)
            pool.iota(m_rows[:, :], pattern=[[0, E], [P, 16]], base=0, channel_multiplier=0,
                      allow_small_or_imprecise_dtypes=True).then_inc(const_ready, 1)
            pool.wait_ge(const_ready, 3)
            pool.memset(pad_ids[:, :, 1], 4 * BIG)
            pool.iota(pad_ids[:, :, 0], pattern=[[P, E + CAP - FULL]], base=2 * TOKENS, channel_multiplier=1,
                      allow_small_or_imprecise_dtypes=True).then_inc(token_ready, 1)
            pool.iota(token_2[:, :], pattern=[[2 * P, NT]], base=0, channel_multiplier=2,
                      allow_small_or_imprecise_dtypes=True).then_inc(const_ready, 1)
            pool.wait_ge(router_loaded, 80)
            for k in range(KC):
                last = pool.tensor_scalar(r_w[:, k, :], r_w[:, k, :], r_scale[:, k:k + 1], H ** -0.5, ALU.mult, ALU.mult)
            last.then_inc(rw_ready, 1)
            pool.wait_ge(rw_ready, 1)
            for n in range(4 * B):
                if n in (4, 8):
                    inverse_deviation(1 + n // 4)
                if n == 4:
                    pool.wait_ge(rstd_ready, 3)
                    pool.memset(kst[PR:PR + MR, :, :], 1.0).then_inc(k_init, 1)
                    pool.wait_ge(k_init, 1)
                pool.wait_ge(rest_ready, n + 1)
                pool.tensor_scalar(pieces[:, n % 4, 1, :], rest[:, n % 2, :], 1.0, None, ALU.mult)\
                    .then_inc(mid_ready, 1)

            def stage_v(i, par2):
                pool.wait_ge(v_init, 1)
                pool.tensor_copy(v_st[:, par2, :], v_all[:, bass.ds(i, 1), :, :].rearrange("p o t c -> p (o t c)"))\
                    .then_inc(v_staged, 1)

            def split_max(j, par2):
                pc = mpc[:, par2, 0:48].rearrange("p (s n) -> p s n", s=MR)
                pool.tensor_tensor(pc[:, 0, :], negm[:, par2, :], ones[:, 0:16], ALU.mult).then_inc(split1, 1)
                pool.wait_ge(split1, j + 1)
                pool.tensor_tensor(mrest[:, par2, :], negm[:, par2, :], pc[:, 0, :], ALU.subtract).then_inc(split2, 1)
                pool.wait_ge(split2, j + 1)
                pool.tensor_tensor(pc[:, 1, :], mrest[:, par2, :], ones[:, 0:16], ALU.mult).then_inc(split3, 1)
                pool.wait_ge(split3, j + 1)
                pool.tensor_tensor(pc[:, 2, :], mrest[:, par2, :], pc[:, 1, :], ALU.subtract).then_inc(m_split, 1)

            pool.wait_ge(mod_stored, 16)
            pool.wait_ge(v_evac, 2 * B)
            stage_v(0, 0)
            for j in range(2):
                pool.wait_ge(s_reduced, 8 * (j + 1))
                split_max(j, j)

            def quad(it, u, more):
                i = 4 * it + u
                if more or u < 3:
                    if not more:
                        pool.wait_ge(pv_done, 4 * i)
                    stage_v(i + 1, (u + 1) % 2)
                if more or u < 2:
                    pool.wait_ge(s_reduced, 8 * (i + 3))
                    pool.wait_ge(m_turned, i + 1)
                    split_max(i + 2, u % 2)

            with pool.Fori(0, 3) as it:
                for u in range(4):
                    quad(it, u, True)
            pool.wait_ge(modb_loaded, 64)
            pool.wait_ge(bp_loaded, 16)
            pool.wait_ge(xn_ready, B)
            pool.wait_ge(lo_ready, 4 * B)
            for m in range(4):
                pool.wait_ge(qk_stored[m], 32 * B)
            for u in range(4):
                quad(3, u, False)
                if u < 2:
                    for b in range(2 * u, 2 * u + 2):
                        pool.tensor_tensor(bias_row[:, :], mod_b[:, 0, b, :], bp_b[:, :], ALU.mult).then_inc(pool_step, 1)
                        pool.wait_ge(pool_step, 2 + b)
                        x_rows = x_sb[:, b * TB:(b + 1) * TB, :]
                        pool.tensor_tensor(x_rows, x_rows, bias_row[:, :].unsqueeze(1).to_broadcast([P, TB, H]), ALU.add)\
                            .then_inc(xb_ready, 1)
                        pool.wait_ge(xb_ready, b + 1)
                if u == 2:
                    pool.wait_ge(v_staged, NQ)
                    pool.iota(tab[:, 0, :], pattern=[[1, TABLE], [0, E]], base=0, channel_multiplier=0,
                              allow_small_or_imprecise_dtypes=True)
                    pool.iota(tab[:, 1, :], pattern=[[0, TABLE], [1, E]], base=0, channel_multiplier=0,
                              allow_small_or_imprecise_dtypes=True).then_inc(tau_ready, 1)
                    for b in range(B):
                        last = pool.tensor_tensor(wp_g[:, b], wp_T[:, :, :], mod_b[:, 0, b, :].unsqueeze(1).to_broadcast([P, KC, H]), ALU.mult)
                    last.then_inc(wpg_ready, 1)

            def power(out_, in_, scale, eps, added, ready, n):
                pool.tensor_scalar(out_, in_, scale, eps, ALU.mult, ALU.add).then_inc(added, 1)
                pool.wait_ge(added, n)
                pool.tensor_tensor(out_, out_, minus_half[:, 0:out_.shape[1]], ALU.pow).then_inc(ready, 1)

            def inverse_deviation_2(b):
                pool.wait_ge(var2_ready, b + 1)
                power(rstd2[:, b * TB:(b + 1) * TB], mv2[:, b * TB:(b + 1) * TB, 1], 1.0, EPS_LN, var2_eps, rstd2_ready, b + 1)

            for b in range(B - 1):
                inverse_deviation_2(b)
            for g in range(NG):
                pool.wait_ge(slot_ready, g + 1)
                for n in range(g * GT, (g + 1) * GT):
                    for c in range(2):
                        pool.indirect_dma_start(out=slots_d, out_offset=bass.IndirectOffsetOnAxis(ap=slot_i[:, c, n:n + 1], axis=0),
                                                in_=h2x[:, n, :], in_offset=None).then_inc(sent, 16)
                if g == 0:
                    inverse_deviation_2(B - 1)
            pool.wait_ge(squared, NT)
            power(rrms, ssq, 1.0 / H, EPS_RMS, ssq_eps, rrms_ready, 1)

            def send_made(t, v):
                pool.wait_ge(target_ready, t + 1)
                pool.wait_ge(made_ready, ONE + t + 1)
                pool.sem_inc(sending, 1)
                pool.indirect_dma_start(out=made_d, out_offset=bass.IndirectOffsetOnAxis(ap=target[:, v, :], axis=0),
                                        in_=made[:, v % 2, :], in_offset=None).then_inc(made_stored[v % 2], 16)

            with pool.Fori(0, CAP // 4) as it:
                for v in range(4):
                    send_made(4 * it + v, v)
            for t in range(CAP // 4 * 4, CAP):
                send_made(t, t % 4)
            for n in range(NT):
                pool.wait_ge(bent, n + 1)
                pool.tensor_tensor(x_sb[:, n, :], x_sb[:, n, :], back[:, n % 8, 1, :], ALU.add).then_inc(out_ready, 1)

        @block.scalar
        def _(act):
            act.sem_inc(ctx_evac, ONE)
            for n in range(2):
                act.sem_inc(ctx_stored[n], ONE)
            act.sem_inc(made_ready, ONE)
            act.wait_ge(c_loaded, 32)
            act.activation(sig[:, :, :], cT[:, :, :], ACT.Exp, scale=-1.0).then_inc(sig_exp, 1)
            for s in range(4):
                act.wait_ge(wT_done, s + 1)
                dst = w_T[:, :, s * H:(s + 1) * H] if s < 3 else wp_T[:, :, :]
                act.activation(dst, ps[:, s, :].rearrange("p (k n) -> p k n", k=KC), ACT.Copy).then_inc(wT_evac, 1)

            act.wait_ge(modT_ready, 1)

            def evac_hT(b):
                act.wait_ge(xT_done, b + 1)
                if b >= 2:
                    act.wait_ge(v_done, 2 * (b - 1))
                for k in range(KC):
                    last = act.activation(hT[:, b % 2, k, :], ps[:, k, :], ACT.Identity,
                                          bias=modT[:, SA * KC + k, b:b + 1], scale=modT[:, CA * KC + k, b:b + 1])
                last.then_inc(hT_ready, 1)

            def take_gate(e):
                act.wait_ge(gate_turned, e + 1)
                act.activation(gate_T[:, e, :, :], ps[:, gate_bank(e):gate_bank(e) + 2, :], ACT.Copy).then_inc(gate_evac, 1)

            evac_hT(0)
            act.wait_ge(v_init, 1)
            for b in range(B):
                for m in range(4):
                    n = 4 * b + m
                    act.wait_ge(qk_done, n + 1)
                    if b >= 1:
                        act.wait_ge(qk_stored[m], 32 * b)
                    act.activation(pieces[:, m, 0, :], ps[:, 2 + m, :], ACT.Copy,
                                   scale=HN ** -0.5 if m < 2 else 1.0).then_inc(hi_ready, 1)
                if b + 1 < B:
                    evac_hT(b + 1)
                for hf in range(2):
                    act.wait_ge(v_done, 2 * b + hf + 1)
                    for tt in range(2):
                        dst = v_all[:, 4 * b:4 * b + 4, 2 * hf + tt, :].rearrange("p q (h c) -> p q h c", h=4)
                        last = act.activation(dst[:, :, :, 0:HN],
                                              ps[:, 6 + hf, tt * H:(tt + 1) * H].rearrange("p (q h d) -> p q h d", q=4, h=4),
                                              ACT.Copy)
                    last.then_inc(v_evac, 1)
                if b == 0:
                    for n in range(3):
                        act.wait_ge(modrow_done, n + 1)
                        act.activation(mod_r[:, n * 512:(n + 1) * 512], ps[0:B, 2 + n, :], ACT.Copy).then_inc(modrow_evac, 1)
                if b == 1:
                    for e in range(4):
                        take_gate(e)
            for e in range(4, E - 1):
                take_gate(e)

            def exps(i, kt, heads=(0, 1, 2, 3)):
                for g in heads:
                    act.wait_ge(st_ready, 16 * i + 4 * kt + g + 1)
                    act.activation(probs[:, kt % 2, g * SQ:(g + 1) * SQ], ps[:, ST_BANK + g % 2, :],
                                   ACT.Exp).then_inc(exp_done, 1)

            def evac_m(j, par2):
                act.wait_ge(m_turned, j + 1)
                act.activation(m_T[:, par2, :], m_ps[0:48, :], ACT.Copy).then_inc(m_evac, 1)

            def evac_ctx(i, par2):
                act.wait_ge(pv_done, 4 * i + 4)
                act.activation(ctx_o[:, par2, :], ps[:, PV_BANK, :], ACT.Copy).then_inc(ctx_evac, 1)

            evac_m(0, 0)
            take_gate(E - 1)
            exps(0, 0)

            def quad(it, u, more):
                i = 4 * it + u
                for k in range(4):
                    if k < 3:
                        exps(i, k + 1)
                    elif more or u < 3:
                        exps(i + 1, 0, (0, 1))
                    if k == 0 and (more or u < 3):
                        evac_m(i + 1, (u + 1) % 2)
                act.wait_ge(ctx_stored[u % 2], ONE + 16 * (2 * it + u // 2))
                evac_ctx(i, u % 2)
                if more or u < 3:
                    exps(i + 1, 0, (2, 3))

            with act.Fori(0, 3) as it:
                for u in range(4):
                    quad(it, u, True)
            for u in range(4):
                quad(3, u, False)

            def x1_out(pair):
                act.wait_ge(proj_done, pair + 1)
                act.activation(x_sb[:, 2 * pair:2 * pair + 2, :], ps[:, pair % 4, :].rearrange("p (n h) -> p n h", n=2),
                               ACT.Copy).then_inc(x1_ready, 1)

            def normalise(b):
                act.wait_ge(nbias2_ready, b + 1)
                for n in range(b * TB, (b + 1) * TB):
                    last = act.activation(h2[:, n, :], x_sb[:, n, :], ACT.Identity,
                                          bias=nbias2[:, n:n + 1], scale=rstd2[:, n:n + 1])
                last.then_inc(normed2, 1)

            def take_h2T(b):
                for n in range(b * TB, (b + 1) * TB):
                    act.wait_ge(h2_turned, n + 1)
                    if n >= 4:
                        act.wait_ge(logit_done, n - 3)
                    act.activation(h2T[:, n % 4, :, :], ps[:, 4 + n % 2, 0:H].rearrange("p (k x) -> p k x", k=KC),
                                   ACT.Copy).then_inc(h2T_ready, 1)

            for pair in range(4):
                x1_out(pair)
            normalise(0)
            normalise(1)
            x1_out(4)
            x1_out(5)
            take_h2T(0)
            take_h2T(1)
            normalise(2)
            x1_out(6)
            x1_out(7)
            take_h2T(2)
            normalise(3)
            take_h2T(3)
            for n in range(NT):
                if n:
                    act.wait_ge(squared, n)
                act.activation(squares, h2[:, n, :], ACT.Square, accum_out=ssq[:, n:n + 1]).then_inc(squared, 1)
            act.activation(run_pads[:, :, 0:H], padding[:, :].unsqueeze(1).to_broadcast([P, E, H]), ACT.Copy).then_inc(pads_ready, 1)
            act.activation(run_pads[:, :, H:HX], pad_ids[:, 0:E, :], ACT.Copy).then_inc(pads_ready, 1)
            act.wait_ge(d_ready, 1)
            act.activation(prob[:, :, :], prob[:, :, :], ACT.Exp).then_inc(e_ready, 1)

            def take_xsT(t, u):
                act.wait_ge(xs_turned, t + 1)
                act.activation(xsT[:, u, :, :], ps[:, 0, 0:H].rearrange("p (k x) -> p k x", k=KC), ACT.Copy).then_inc(xsT_ready, 1)

            def do_gelu(t, u):
                act.wait_ge(gate_done, t + 1)
                act.activation(gelu[:, u, :], ps[:, 2 + u, 0:H], ACT.Gelu_apprx_tanh).then_inc(gelu_ready, 1)

            def take_made(t, u, before):
                act.wait_ge(down_done, t + 1)
                if not isinstance(t, int) or t >= 2:
                    act.wait_ge(made_stored[u], 16 * before)
                act.activation(made[:, u, :], ps[:, 4, 0:H], ACT.Copy).then_inc(made_ready, 1)

            take_xsT(0, 0)
            take_xsT(1, 1)
            do_gelu(0, 0)

            def tile(t, u, before, more):
                if more > 1:
                    do_gelu(t + 1, 1 - u)
                if more > 2:
                    take_xsT(t + 2, u)
                take_made(t, u, before)

            for t in range(2):
                tile(t, t, 0, 3)
            with act.Fori(1, (CAP - 3) // 2) as it:
                for u in range(2):
                    tile(2 * it + u, u, it, 3)
            for t in range(CAP - 3, CAP):
                tile(t, t % 2, t // 2, CAP - t)
            for n in range(NT):
                act.wait_ge(back_loaded[n % 8], 16 * (n // 8 + 1))
                act.activation(back[:, n % 8, 0, :], back[:, n % 8, 0, :], ACT.Copy, scale=slot_w[:, 0, n:n + 1]).then_inc(halved, 1)

        @block.vector
        def _(dve):
            chain = [0]

            def link(ins):
                chain[0] += 1
                ins.then_inc(dve_chain, 1)
                dve.wait_ge(dve_chain, chain[0])

            dve.wait_ge(sig_exp, 1)
            link(dve.tensor_scalar(sig[:, :, :], sig[:, :, :], 1.0, None, ALU.add))
            link(dve.reciprocal(sig[:, :, :], sig[:, :, :]))
            dve.tensor_tensor(sig[:, :, :], cT[:, :, :], sig[:, :, :], ALU.mult).then_inc(silu_ready, 1)

            def layer_norm(b):
                dve.wait_ge(x_loaded[b], 16)
                for t in range(TB):
                    last = dve.bn_stats(st[:, t, :], x_sb[:, b * TB + t, :])
                link(last)
                for t in range(TB):
                    last = dve.bn_aggr(mv[:, t, :], st[:, t, :])
                last.then_inc(var_ready, 1)
                dve.wait_ge(rstd_ready, b + 1)
                link(dve.scalar_tensor_tensor(nbias[:, :], mv[:, :, 0], -1.0, rstd[:, :], ALU.mult, ALU.mult))
                if b >= 2:
                    dve.wait_ge(xT_done, b - 1)
                for t in range(TB):
                    last = dve.tensor_scalar(xn[:, b % 2, t, :], x_sb[:, b * TB + t, :],
                                             rstd[:, t:t + 1], nbias[:, t:t + 1], ALU.mult, ALU.add)
                last.then_inc(xn_ready, 1)

            layer_norm(0)
            dve.wait_ge(modT_done, 1)
            link(dve.tensor_copy(modT[:, :, :], ps[:, 7, 0:4 * B].rearrange("p (c b) -> p c b", b=B)))
            dve.tensor_scalar(modT[:, CA * KC:(CA + 1) * KC, :], modT[:, CA * KC:(CA + 1) * KC, :], 1.0, None, ALU.add)\
                .then_inc(modT_ready, 1)
            layer_norm(1)
            def low_piece(n):
                dve.wait_ge(mid_ready, n + 1)
                dve.tensor_tensor(pieces[:, n % 4, 2, :], rest[:, n % 2, :], pieces[:, n % 4, 1, :],
                                  ALU.subtract).then_inc(lo_ready, 1)

            def gate_rows():
                dve.wait_ge(modrow_evac, 3)
                rows = mod_r[:, :].rearrange("b (a s n) -> b a s n", a=2, s=3)
                link(dve.tensor_scalar(rows[:, :, 1, :], rows[:, :, 1, :], 1.0, None, ALU.add))
                gates = rows[:, :, 2, :]
                link(dve.tensor_scalar(sgn[:, :, :], gates, 0.0, 2.0, ALU.is_ge, ALU.mult))
                link(dve.tensor_scalar(sgn[:, :, :], sgn[:, :, :], -1.0, None, ALU.add))
                link(dve.scalar_tensor_tensor(gates, gates, -1.0, gates, ALU.mult, ALU.max))
                dve.scalar_tensor_tensor(gates, gates, 0.25, sgn[:, :, :], ALU.max, ALU.mult).then_inc(modrow_ready, 1)

            for b in range(B):
                for m in range(4):
                    n = 4 * b + m
                    dve.wait_ge(hi_ready, n + 1)
                    if n >= 2:
                        dve.wait_ge(lo_ready, n - 1)
                    dve.scalar_tensor_tensor(rest[:, n % 2, :], ps[:, 2 + m, :], HN ** -0.5 if m < 2 else 1.0,
                                             pieces[:, m, 0, :], ALU.mult, ALU.subtract).then_inc(rest_ready, 1)
                    if m >= 1:
                        low_piece(n - 1)
                if b + 2 < B:
                    layer_norm(b + 2)
                low_piece(4 * b + 3)
                if b == 0:
                    gate_rows()

            def reduce(j, pair, par2):
                dve.wait_ge(s_ready, 8 * j + pair + 1)
                bank = S_BANK + 2 * (pair % 2)
                dve.reduce_max(negm[:, par2, 2 * pair:2 * pair + 2], ps[:, bank:bank + 2, :], AX, negate=True)\
                    .then_inc(s_reduced, 1)

            for j in range(2):
                for pair in range(8):
                    reduce(j, pair, j)

            def quad(it, u):
                j = 4 * it + u + 2
                dve.wait_ge(m_split, j - 1)
                for pair in range(8):
                    reduce(j, pair, u % 2)

            with dve.Fori(0, 3) as it:
                for u in range(4):
                    quad(it, u)
            for u in range(2):
                quad(3, u)

            def over(v, n):
                return v.unsqueeze(2).to_broadcast([P, v.shape[1], n])

            dve.wait_ge(const_ready, 4)

            def statistics(b):
                for n in range(b * TB, (b + 1) * TB):
                    dve.wait_ge(x1_ready, n // 2 + 1)
                    last = dve.bn_stats(st2[:, n, :], x_sb[:, n, :])
                link(last)
                for n in range(b * TB, (b + 1) * TB):
                    last = dve.bn_aggr(mv2[:, n, :], st2[:, n, :])
                last.then_inc(var2_ready, 1)

            def norm_bias(b):
                tiles = slice(b * TB, (b + 1) * TB)
                dve.wait_ge(rstd2_ready, b + 1)
                dve.scalar_tensor_tensor(nbias2[:, tiles], mv2[:, tiles, 0], -1.0, rstd2[:, tiles], ALU.mult, ALU.mult)\
                    .then_inc(nbias2_ready, 1)

            def modulate(b):
                rows = h2[:, b * TB:(b + 1) * TB, :]
                dve.wait_ge(normed2, b + 1)
                link(dve.tensor_tensor(rows, rows, mod_b[:, 2, b, :].unsqueeze(1).to_broadcast([P, TB, H]), ALU.mult))
                dve.tensor_tensor(rows, rows, mod_b[:, 1, b, :].unsqueeze(1).to_broadcast([P, TB, H]), ALU.add)\
                    .then_inc(h2_ready, 1)

            def choose(g):
                tiles = slice(g * GT, (g + 1) * GT)
                mine = chosen[:, tiles, :]
                dve.wait_ge(logit_done, GT * (g + 1))
                link(dve.tensor_copy(logit[:, tiles, :], ps[:, 6 + g % 2, 0:GT * E].rearrange("p (t e) -> p t e", t=GT)))
                one = logit[:, tiles, :].unsqueeze(3).to_broadcast([P, GT, E, E])
                other = logit[:, tiles, :].unsqueeze(2).to_broadcast([P, GT, E, E])
                dve.tensor_tensor(equal, other, one, ALU.is_equal)
                link(dve.tensor_tensor(above, other, one, ALU.is_gt))
                link(dve.tensor_tensor(equal, equal, earlier[:, :].rearrange("p (a b) -> p a b", a=E).unsqueeze(1).to_broadcast([P, GT, E, E]), ALU.mult))
                link(dve.tensor_tensor(above, above, equal, ALU.add))
                link(dve.reduce_sum(count, above, AX))
                dve.tensor_scalar(mine, count, 2.0, None, ALU.is_lt).then_inc(chosen_ready, 1)

            def place_rows(g):
                tiles = slice(g * GT, (g + 1) * GT)
                mine = chosen[:, tiles, :]
                dve.wait_ge(chosen_ready, g + 1)
                dve.wait_ge(counted, g + 1)
                link(dve.tensor_tensor(totals, ps[:, 6 + g % 2, 2 * GT * E:3 * GT * E].rearrange("p (t e) -> p e t", t=GT), before, ALU.add))
                link(dve.tensor_tensor_scan(upto.rearrange("p e t -> p (e t)"), after_0[:, :], totals.rearrange("p e t -> p (e t)"),
                                            0.0, ALU.mult, ALU.add))
                link(dve.tensor_tensor(place, ps[:, 6 + g % 2, GT * E:2 * GT * E].rearrange("p (t e) -> p t e", t=GT),
                                       upto.rearrange("p e t -> p t e"), ALU.add))
                ways = ((0, -BIG, ALU.min), (1, 1.0, ALU.max))
                for c, by, _ in ways:
                    last = dve.scalar_tensor_tensor(marks[:, c, tiles, :], place, by, mine, ALU.add, ALU.mult)
                link(last)
                for c, _, best in ways:
                    last = dve.tensor_reduce(slot_f[:, c, tiles], marks[:, c, tiles, :], AX, best)
                link(last)
                dve.tensor_copy(h2x[:, tiles, H], token_2[:, tiles])
                dve.tensor_copy(h2x[:, tiles, H + 1], slot_f[:, 0, tiles])
                for c, by, _ in ways:
                    last = dve.tensor_scalar(slot_i[:, c, tiles], slot_f[:, c, tiles], -by, None, ALU.add)
                last.then_inc(slot_ready, 1)
                link(dve.tensor_copy(start, upto[:, :, GT - 1]))

            dve.wait_ge(sums_loaded, 16)
            dve.reciprocal(inv_rows, sum_rows).then_inc(inverse_ready, 1)
            dve.wait_ge(xb_ready, B)
            dve.wait_ge(ctx_evac, ONE + 15)
            dve.reciprocal(inv_o[:, 0, :], ctx_o[:, 0, :]).then_inc(inverse_ready, 1)
            dve.wait_ge(ctx_loaded[0], 16 * 2 * B)
            for b in range(B):
                dve.tensor_tensor(ctx_n[:, 0, b, :], ctx_n[:, 0, b, :], inv_0[:, b, :], ALU.mult).then_inc(half_ready, 1)
            dve.wait_ge(ctx_evac, ONE + 16)
            dve.reciprocal(inv_o[:, 1, :], ctx_o[:, 1, :]).then_inc(inverse_ready, 1)
            dve.wait_ge(ctx_loaded[1], 16 * (2 * B + 4 * B))
            for b in range(B):
                dve.tensor_tensor(ctx_n[:, 1, b, :], ctx_n[:, 1, b, :], inv_1[:, b, :], ALU.mult).then_inc(ctx_ready, 1)
            link(dve.memset(before, 0.0))
            link(dve.tensor_copy(start, seg_0[:, :]))
            statistics(0)
            statistics(1)
            norm_bias(0)
            norm_bias(1)
            modulate(0)
            modulate(1)
            statistics(2)
            choose(0)
            norm_bias(2)
            place_rows(0)
            modulate(2)
            choose(1)
            statistics(3)
            place_rows(1)
            norm_bias(3)
            choose(2)
            modulate(3)
            place_rows(2)
            choose(3)
            place_rows(3)

            dve.tensor_copy(run_i[:, :], start[0:1, :]).then_inc(run_ready, 1)
            link(dve.tensor_tensor(filled[:, :], start, seg_0[:, :], ALU.subtract))
            fits = above.rearrange("p t a b -> p (t a b)")[:, 0:E * 16].rearrange("p (e m) -> p e m", e=E)
            link(dve.tensor_tensor(fits, over(filled[:, :], 16), m_rows[:, :].rearrange("p (e m) -> p e m", e=E), ALU.is_gt))
            link(dve.reduce_sum(filled[:, :], fits, AX))
            link(dve.tensor_tensor_scan(ends[:, :], ones[:, 0:E], filled[:, :], 0.0, ALU.mult, ALU.add))
            link(dve.tensor_tensor(firsts[:, :], ends[:, :], filled[:, :], ALU.subtract))
            tau, number, mine, use, row = (v.rearrange("o (t e) -> o t e", e=E)
                                           for v in (tab[:, 0, :], tab[:, 1, :], work[:, 0, :], work[:, 1, :], work[:, 2, :]))

            def all_tiles(v):
                return v[:, :].unsqueeze(1).to_broadcast([P, TABLE, E])

            dve.wait_ge(tau_ready, 1)

            dve.tensor_tensor(mine, tau, all_tiles(firsts), ALU.is_ge)
            dve.tensor_tensor(use, tau, all_tiles(ends), ALU.is_lt)
            link(dve.scalar_tensor_tensor(shift[:, :], firsts[:, :], -float(P), seg_0[:, :], ALU.mult, ALU.add))
            spare = float(DUMMY - FULL * P)
            link(dve.tensor_tensor(mine, mine, use, ALU.mult))
            dve.tensor_tensor(use, mine, number, ALU.mult)
            link(dve.scalar_tensor_tensor(row, all_tiles(shift), -spare, mine, ALU.add, ALU.mult))
            dve.reduce_sum(tab_f[:, 0:TABLE], row, AX)
            link(dve.reduce_sum(tab_f[:, TABLE:2 * TABLE], use, AX))
            link(dve.scalar_tensor_tensor(tab_f[:, 0:TABLE], tau[:, :, 0], float(P), tab_f[:, 0:TABLE], ALU.mult, ALU.add))
            dve.tensor_scalar(tab_i[:, 0:TABLE], tab_f[0:1, 0:TABLE], spare, None, ALU.add)
            dve.tensor_copy(tab_i[:, TABLE:2 * TABLE], tab_f[0:1, TABLE:2 * TABLE]).then_inc(tab_ready, 1)
            link(dve.tensor_scalar(base[:, :], tab_f[:, 0:TABLE], spare - BIG, None, ALU.add))

            for c in range(2):
                last = dve.tensor_tensor(hits[:, c], marks[:, c], over(slot_f[:, c, :], E), ALU.is_equal)
            link(last)
            dve.wait_ge(rrms_ready, 1)
            link(dve.tensor_tensor(prob, logit, over(rrms, E), ALU.mult))
            link(dve.reduce_max(top, prob, AX))
            dve.tensor_tensor(prob, prob, over(top, E), ALU.subtract).then_inc(d_ready, 1)
            dve.wait_ge(e_ready, 1)
            dve.reduce_sum(total, prob, AX)
            link(dve.tensor_tensor(logit, prob, chosen, ALU.mult))
            dve.reduce_sum(picked, logit, AX)
            dve.tensor_tensor(prob, prob, e_scale[:, :].unsqueeze(1).to_broadcast([P, NT, E]), ALU.mult)
            link(dve.reciprocal(total, total))
            link(dve.tensor_tensor(picked, picked, total, ALU.mult))
            link(dve.tensor_scalar(top, picked, 0.0, None, ALU.is_le))
            link(dve.tensor_tensor(picked, picked, top, ALU.max))
            link(dve.reciprocal(picked, picked))
            link(dve.tensor_tensor(total, total, picked, ALU.mult))
            for c in range(2):
                last = dve.tensor_tensor(hits[:, c], hits[:, c], prob, ALU.mult)
            link(last)
            for c in range(2):
                last = dve.reduce_sum(slot_w[:, c, :], hits[:, c], AX)
            link(last)
            link(dve.tensor_tensor(slot_w, slot_w, total.unsqueeze(1).to_broadcast([P, 2, NT]), ALU.mult))

            def take_actsT(t):
                dve.wait_ge(acts_turned, t + 1)
                dve.tensor_copy(actsT[:, :, :], ps[:, 1, 0:H].rearrange("p (k x) -> p k x", k=KC)).then_inc(actsT_ready, 1)

            def do_acts(t, u):
                dve.wait_ge(gelu_ready, t + 1)
                dve.tensor_tensor(acts[:, u, :], ps[:, 2 + u, H:2 * H], gelu[:, u, :], ALU.mult).then_inc(acts_ready, 1)

            def aim(t, v, rounds):
                u = v % 2
                dve.wait_ge(xs_loaded[u], 16 * (rounds + 1))
                if not isinstance(t, int) or t >= 4:
                    dve.wait_ge(made_stored[u], 16 * (rounds - 1))
                dve.scalar_tensor_tensor(target[:, v, :], xs[:, u, H + 1:H + 2], base[:, bass.ds(t, 1)], xs[:, u, H:H + 1],
                                         ALU.is_lt, ALU.add).then_inc(target_ready, 1)

            aim(0, 0, 0)
            aim(1, 1, 0)
            do_acts(0, 0)

            def tile(t, v, rounds):
                take_actsT(t)
                aim(t + 2, (v + 2) % 4, rounds + 1)
                do_acts(t + 1, 1 - v % 2)

            for t in range(4):
                tile(t, t, t // 2)
            with dve.Fori(1, (CAP - 3) // 4) as it:
                for v in range(4):
                    tile(4 * it + v, v, 2 * it + v // 2)
            for t in range(CAP - 3, CAP):
                take_actsT(t)
                if t + 2 < CAP:
                    aim(t + 2, (t + 2) % 4, (t + 2) // 2)
                if t + 1 < CAP:
                    do_acts(t + 1, (t + 1) % 2)

            for n in range(NT):
                dve.wait_ge(halved, n + 1)
                link(dve.scalar_tensor_tensor(back[:, n % 8, 1, :], back[:, n % 8, 1, :], slot_w[:, 1, n:n + 1],
                                              back[:, n % 8, 0, :], ALU.mult, ALU.add))
                dve.tensor_tensor(back[:, n % 8, 1, :], back[:, n % 8, 1, :], mod_b[:, 3, n // TB, :], ALU.mult).then_inc(bent, 1)

        @block.tensor
        def _(pe):
            pe.wait_ge(ident_ready, 1)
            pe.wait_ge(w_loaded, 160)
            for s in range(3):
                for k in range(KC):
                    for half in range(2):
                        last = pe.transpose(ps[:, s, (2 * k + half) * P:(2 * k + half + 1) * P],
                                            w_raw[:, 2 * s + half, k * P:(k + 1) * P], ident[:, :])
                last.then_inc(wT_done, 1)
            pe.wait_ge(silu_ready, 1)
            pe.wait_ge(wmod_loaded[0], 16)
            for c in range(4):
                for k in range(KC):
                    last = pe.matmul(ps[:, 7, c * B:(c + 1) * B], wmod[:, k, c * P:(c + 1) * P], sig[:, k, :],
                                     start=k == 0, stop=k == KC - 1)
            last.then_inc(modT_done, 1)
            pe.wait_ge(wp_loaded, 16)
            for k in range(KC):
                for half in range(2):
                    last = pe.transpose(ps[:, 3, (2 * k + half) * P:(2 * k + half + 1) * P],
                                        wp_raw[:, half, k * P:(k + 1) * P], ident[:, :])
            last.then_inc(wT_done, 1)

            def turn_x(b):
                pe.wait_ge(xn_ready, b + 1)
                if b == 0:
                    pe.wait_ge(wT_evac, 4)
                else:
                    pe.wait_ge(hT_ready, b)
                for k in range(KC):
                    for t in range(TB):
                        last = pe.transpose(ps[:, k, t * P:(t + 1) * P], xn[:, b % 2, t, k * P:(k + 1) * P], ident[:, :])
                last.then_inc(xT_done, 1)

            turn_x(0)
            pe.wait_ge(modT_ready, 1)

            def turn_gate(e, k):
                for c in range(4):
                    last = pe.transpose(ps[:, gate_bank(e) + k, c * P:(c + 1) * P],
                                        gate_raw[:, e % 4, c, k * P:(k + 1) * P], ident[:, :])
                if k == KC - 1:
                    last.then_inc(gate_turned, 1)

            for b in range(B):
                pe.wait_ge(hT_ready, b + 1)
                for m in range(4):
                    if b >= 1:
                        pe.wait_ge(rest_ready, 4 * (b - 1) + m + 1)
                    if b == 1 and m < 3:
                        pe.wait_ge(modrow_evac, m + 1)
                    if b == 2:
                        pe.wait_ge(gate_evac, 3 + m // 2)
                    for k in range(KC):
                        last = pe.matmul(ps[:, 2 + m, :], w_T[:, k, m * P:(m + 1) * P], hT[:, b % 2, k, :],
                                         start=k == 0, stop=k == KC - 1)
                    last.then_inc(qk_done, 1)
                if b + 1 < B:
                    turn_x(b + 1)
                for hf in range(2):
                    if b >= 1:
                        pe.wait_ge(v_evac, 2 * (b - 1) + hf + 1)
                    for tt in range(2):
                        t = 2 * hf + tt
                        for k in range(KC):
                            last = pe.matmul(ps[:, 6 + hf, tt * H:(tt + 1) * H], hT[:, b % 2, k, t * P:(t + 1) * P],
                                             w_T[:, k, 2 * H:3 * H], start=k == 0, stop=k == KC - 1)
                    last.then_inc(v_done, 1)
                if b == 0:
                    pe.wait_ge(rest_ready, 3)
                    pe.wait_ge(wmod_loaded[1], 16)
                    for n in range(3):
                        for k in range(KC):
                            last = pe.matmul(ps[0:B, 2 + n, :], sig[:, k, :], wmod[:, k, n * 512:(n + 1) * 512],
                                             start=k == 0, stop=k == KC - 1)
                        last.then_inc(modrow_done, 1)
                if b == 1:
                    pe.wait_ge(rest_ready, 4 * (b + 1))
                    pe.wait_ge(gate_loaded, 64)
                    for e in range(4):
                        if e >= 2:
                            pe.wait_ge(gate_evac, e - 1)
                        for k in range(KC):
                            turn_gate(e, k)

            def s_tile(j, s, par, first=False):
                g, t = s // 4, s % 4
                if s % 2 == 0 and not (first and s < 4):
                    pe.wait_ge(s_reduced, 8 * j + s // 2 - 1)
                last = pe.matmul(ps[:, S_BANK + s % 4, :], qst[0:PR, par, g * SQ + t * P:g * SQ + (t + 1) * P],
                                 kst[0:PR, par, g * SQ:(g + 1) * SQ], start=True, stop=True)
                if s % 2:
                    last.then_inc(s_ready, 1)

            def st_tile(i, kt, g, par):
                if not (isinstance(i, int) and i == 0 and kt == 0 and g < 2):
                    pe.wait_ge(exp_done, 16 * i + 4 * kt + g - 1)
                pe.matmul(ps[:, ST_BANK + g % 2, :], kst[0:PR + MR, par, g * SQ + kt * P:g * SQ + (kt + 1) * P],
                          qst[0:PR + MR, par, g * SQ:(g + 1) * SQ], start=True, stop=True).then_inc(st_ready, 1)

            def pv(i, kt, par2):
                pe.wait_ge(exp_done, 16 * i + 4 * kt + 4)
                for g in range(4):
                    last = pe.matmul(ps[32 * g:32 * g + 32, PV_BANK, :], v_st[:, par2, kt * P + 32 * g:kt * P + 32 * g + 32],
                                     probs[:, kt % 2, g * SQ:(g + 1) * SQ], start=kt == 0, stop=kt == 3)
                last.then_inc(pv_done, 1)

            def turn_m(j, par2):
                pe.wait_ge(m_split, j + 1)
                pe.transpose(m_ps, mpc[:, par2, :], identb[:, :]).then_inc(m_turned, 1)

            pe.wait_ge(rest_ready, 4 * B)
            pe.wait_ge(v_evac, 2 * B)
            pe.wait_ge(ident_ready, 2)
            gate_after = {(0, 1): (4, 0), (0, 5): (4, 1), (0, 9): (5, 0), (0, 13): (5, 1),
                          (1, 1): (6, 0), (1, 5): (6, 1), (1, 7): (7, 0), (1, 11): (7, 1)}
            for j in range(2):
                pe.wait_ge(stack_loaded[j], 96)
                for s in range(16):
                    s_tile(j, s, j, first=j == 0)
                    if (j, s) in gate_after:
                        e, k = gate_after[j, s]
                        if e == 4:
                            pe.wait_ge(gate_loaded, 128)
                        else:
                            pe.wait_ge(gate_evac, e)
                        turn_gate(e, k)
                    if j == 1 and s == 7:
                        turn_m(0, 0)
            pe.wait_ge(gate_evac, E)
            pe.wait_ge(k_init, 1)
            pe.wait_ge(mrow_loaded[0], 16)
            for g in range(4):
                st_tile(0, 0, g, 0)

            def quad(it, u, more):
                i = 4 * it + u
                ahead = more or u < 2
                if ahead:
                    pe.wait_ge(stack_loaded[(u + 2) % 4], 96 * (it + 1 + (u + 2) // 4))
                for k in range(4):
                    here = k < 3
                    nxt = here or more or u < 3
                    if not here and nxt:
                        pe.wait_ge(mrow_loaded[(u + 1) % 4], 16 * (it + 1 + (u + 1) // 4))
                    args = (i, k + 1, u) if here else (i + 1, 0, (u + 1) % 4)
                    if ahead:
                        s_tile(i + 2, 4 * k, (u + 2) % 4)
                        s_tile(i + 2, 4 * k + 1, (u + 2) % 4)
                    if nxt:
                        st_tile(*args[0:2], 0, args[2])
                        st_tile(*args[0:2], 1, args[2])
                    if k == 0:
                        pe.wait_ge(v_staged, i + 1)
                        pe.wait_ge(ctx_evac, ONE + i)
                    pv(i, k, u % 2)
                    if nxt:
                        st_tile(*args[0:2], 2, args[2])
                        st_tile(*args[0:2], 3, args[2])
                    if ahead:
                        s_tile(i + 2, 4 * k + 2, (u + 2) % 4)
                        s_tile(i + 2, 4 * k + 3, (u + 2) % 4)
                    if k == 0 and (more or u < 3):
                        pe.wait_ge(m_evac, i + 1)
                        turn_m(i + 1, (u + 1) % 2)

            with pe.Fori(0, 3) as it:
                for u in range(4):
                    quad(it, u, True)
            for u in range(4):
                quad(3, u, False)

            def project_half(pair):
                bank = ps[:, pair % 4, :]
                if pair >= 4:
                    pe.wait_ge(x1_ready, pair - 3)
                pe.matmul(bank, ident[:, :], x_sb[:, 2 * pair:2 * pair + 2, :].rearrange("p n h -> p (n h)"), start=True, stop=False)
                project_slots(pair, 0)

            def project_slots(pair, kc):
                b = pair // 2
                for n in range(2):
                    t = 2 * (pair % 2) + n
                    last = pe.matmul(ps[:, pair % 4, n * H:(n + 1) * H], ctx_n[:, kc, b, t * P:(t + 1) * P], wp_g[:, b, kc, :],
                                     start=False, stop=kc == KC - 1 and n == 1)
                if kc == KC - 1:
                    last.then_inc(proj_done, 1)

            def turn_h2(b):
                pe.wait_ge(h2_ready, b + 1)
                for n in range(b * TB, (b + 1) * TB):
                    if n >= 2:
                        pe.wait_ge(h2T_ready, n - 1)
                    for k in range(KC):
                        last = pe.transpose(ps[:, 4 + n % 2, k * P:(k + 1) * P], h2[:, n, k * P:(k + 1) * P], ident[:, :])
                    last.then_inc(h2_turned, 1)

            def logits(b):
                if b >= 2:
                    pe.wait_ge(slot_ready, b - 1)
                for n in range(b * TB, (b + 1) * TB):
                    pe.wait_ge(h2T_ready, n + 1)
                    for k in range(KC):
                        last = pe.matmul(ps[:, 6 + b % 2, (n % TB) * E:(n % TB + 1) * E], h2T[:, n % 4, k, :], r_w[:, k, :],
                                         start=k == 0, stop=k == KC - 1)
                    last.then_inc(logit_done, 1)

            def counts(g):
                pe.wait_ge(chosen_ready, g + 1)
                flat = chosen[:, g * GT:(g + 1) * GT, :].rearrange("p t e -> p (t e)")
                pe.matmul(ps[:, 6 + g % 2, GT * E:2 * GT * E], minus_geq[:, :], flat, start=True, stop=True)
                pe.matmul(ps[:, 6 + g % 2, 2 * GT * E:3 * GT * E], ones[:, :], flat, start=True, stop=True).then_inc(counted, 1)

            pe.wait_ge(s_reduced, 8 * NQ)
            pe.wait_ge(xb_ready, B)
            pe.wait_ge(wpg_ready, 1)
            pe.wait_ge(half_ready, B)
            for pair in range(4):
                project_half(pair)
            for pair in range(4):
                pe.wait_ge(ctx_ready, pair // 2 + 1)
                project_slots(pair, 1)
            pe.wait_ge(ctx_ready, B)
            for pair in (4, 5):
                project_half(pair)
                project_slots(pair, 1)
            pe.wait_ge(exp_done, 16 * NQ)
            pe.wait_ge(ctx_evac, ONE + NQ)
            pe.wait_ge(m_evac, NQ)
            pe.wait_ge(const_ready, 4)
            pe.wait_ge(rw_ready, 1)
            turn_h2(0)
            logits(0)
            turn_h2(1)
            project_half(6)
            counts(0)
            project_slots(6, 1)
            logits(1)
            project_half(7)
            project_slots(7, 1)
            turn_h2(2)
            counts(1)
            logits(2)
            counts(2)
            turn_h2(3)
            logits(3)
            counts(3)

            def turn_slots(t, u, before):
                pe.wait_ge(xs_loaded[u], 16 * (before + 1))
                if isinstance(t, int) and t == 0:
                    pe.wait_ge(x1_ready, NT // 2)
                else:
                    pe.wait_ge(xsT_ready, t)
                for k in range(KC):
                    last = pe.transpose(ps[:, 0, k * P:(k + 1) * P], xs[:, u, k * P:(k + 1) * P], ident[:, :])
                last.then_inc(xs_turned, 1)

            def expert(t):
                return pe.value_load(tab_i[0:1, bass.ds(t + TABLE, 1)], min_val=0, max_val=E - 1)

            def gate(t, u, e, k):
                if k == 0:
                    pe.wait_ge(xsT_ready, t + 1)
                    if isinstance(t, int) and t == 0:
                        pe.wait_ge(h2T_ready, NT)
                ins = pe.matmul(ps[:, 2 + u, :], xsT[:, u, k, :], gate_T[:, bass.ds(e, 1), k, :].rearrange("p o n -> p (o n)"),
                                start=k == 0, stop=k == KC - 1)
                if k == KC - 1:
                    ins.then_inc(gate_done, 1)

            def turn_acts(t, u):
                pe.wait_ge(acts_ready, t + 1)
                for k in range(KC):
                    last = pe.transpose(ps[:, 1, k * P:(k + 1) * P], acts[:, u, k * P:(k + 1) * P], ident[:, :])
                last.then_inc(acts_turned, 1)

            def down(t, e):
                pe.wait_ge(actsT_ready, t + 1)
                pe.wait_ge(made_ready, ONE + t)
                for k in range(KC):
                    last = pe.matmul(ps[:, 4, 0:H], actsT[:, k, :], lin[:, bass.ds(e, 1), k, :].rearrange("p o n -> p (o n)"),
                                     start=k == 0, stop=k == KC - 1)
                last.then_inc(down_done, 1)

            pe.wait_ge(tab_ready, 1)
            pe.wait_ge(lin_loaded, 16)
            turn_slots(0, 0, 0)
            turn_slots(1, 1, 0)
            e = expert(0)
            gate(0, 0, e, 0)
            gate(0, 0, e, 1)

            def tile(t, u, before, more):
                if more > 1:
                    e = expert(t + 1)
                    gate(t + 1, 1 - u, e, 0)
                turn_acts(t, u)
                if more > 1:
                    gate(t + 1, 1 - u, e, 1)
                if more > 2:
                    turn_slots(t + 2, u, before + 1)
                down(t, expert(t))

            with pe.Fori(0, (CAP - 3) // 4) as it:
                for v in range(4):
                    tile(4 * it + v, v % 2, 2 * it + v // 2, 3)
            for t in range(CAP - 3, CAP):
                tile(t, t % 2, t // 2, CAP - t)


_INS = ["L0_attn_query", "L0_attn_Wqkv", "L0_attn_Wproj", "L0_attn_bproj", "L0_ffn_router_logits",
        "L0_ffn_gating_einsum", "L0_ffn_linear", "L0_ffn_per_expert_scale", "L0_ffn_router_scale", "L0_c", "L0_wmod"]
_OUTS = [((B, SQ, H), "float32")]


def kernel(**inputs):
    import numpy as _np
    import concourse.bacc as _bacc
    from concourse import mybir as _mybir
    from concourse.bass_utils import run_bass_kernel_spmd as _run

    nc = _bacc.Bacc("TRN2", target_bir_lowering=False, num_devices=1)
    arrays, args = {}, []
    for name in _INS:
        a = _np.ascontiguousarray(inputs[name])
        arrays[f"in_{name}_dram"] = a
        args.append(nc.dram_tensor(f"in_{name}_dram", a.shape, _mybir.dt.from_np(a.dtype), kind="ExternalInput").ap())
    for i, (shape, dtype) in enumerate(_OUTS):
        dt = _mybir.dt.from_np(_np.dtype(dtype))
        args.append(nc.dram_tensor(f"out_{i}_dram", shape, dt, kind="ExternalOutput").ap())
    adaln_block(nc, *args)
    r = _run(nc, [arrays], core_ids=[0])
    got = tuple(r.results[0][f"out_{i}_dram"] for i in range(len(_OUTS)))
    return got[0]
```
